# Optimizing a Trainium2 kernel written in Bass

```python
import numpy as np
import jax
import jax.numpy as jnp

def _softmax(x, axis=-1):
    return jax.nn.softmax(x, axis=axis)

def _gelu(x):
    return jax.nn.gelu(x, approximate=True)

def _silu(x):
    return jax.nn.silu(x)

def _sigmoid(x):
    return jax.nn.sigmoid(x)

def _layernorm(x, axis=-1, eps=1e-05):
    m = jnp.mean(x, axis=axis, keepdims=True)
    v = jnp.var(x, axis=axis, keepdims=True)
    return (x - m) / jnp.sqrt(v + eps)

def _scatter_add(tgt, idx, src, axis=0):
    return tgt.at[idx].add(src)

def _segment_sum(src, seg, n):
    return jax.ops.segment_sum(src, seg, n)
kernel_name = 'mk_gps_d1_gnn_r32_6e814c'

def setup_inputs(seed: int=0):
    np.random.seed(seed)
    _w = jnp.asarray

    def _rec_inputs():
        import jax
        import jax.numpy as jnp
        _gk = jax.random.key(seed)
        x = -0.0003713 + 1 * jax.random.normal(jax.random.fold_in(_gk, 1), (3125, 256), jnp.float32)
        src = jax.random.randint(jax.random.fold_in(_gk, 2), (50000,), 0, 3125, jnp.int32)
        dst = jnp.minimum((3125 * jax.random.uniform(jax.random.fold_in(_gk, 3), (50000,)) ** 2.0).astype(jnp.int32), 99999)
        _o = jnp.argsort(dst, stable=True)
        src = src[_o]
        dst = dst[_o]
        return (x, src, dst)
    x, src, dst = _rec_inputs()

    def _L0_gnn_setup():
        import jax, jax.numpy as jnp
        import numpy as np
        N_NODES, IN_DIM, HID, OUT_DIM, H, E = (50000, 256, 256, 256, 8, 12500)
        NEG_SLOPE = 0.2
        LN_EPS = 1e-05
        key = jax.random.key(seed)
        ks = jax.random.split(key, 8)
        s = 1.0 / np.sqrt(IN_DIM)
        return {'x': jax.random.normal(ks[0], (N_NODES, IN_DIM), jnp.float32), 'edge_index': jax.random.randint(ks[1], (2, E), 0, N_NODES, jnp.int64), 'W': jax.random.normal(ks[2], (H, IN_DIM, HID), jnp.float32) * s, 'att_src': jax.random.normal(ks[3], (H, HID), jnp.float32) * s, 'att_dst': jax.random.normal(ks[4], (H, HID), jnp.float32) * s, 'bias_gat': jnp.zeros((H, HID), jnp.float32), 'gate_weights': jnp.ones((H,), jnp.float32) / H, 'ln_gamma': jnp.ones((HID,), jnp.float32), 'ln_beta': jnp.zeros((HID,), jnp.float32), 'Wo': jax.random.normal(ks[5], (OUT_DIM, HID), jnp.float32) * (1.0 / np.sqrt(HID)), 'bo': jnp.zeros((OUT_DIM,), jnp.float32)}
    _L0_gnn_all = _L0_gnn_setup()
    _L0_gnn_in = {k: v for k, v in _L0_gnn_all.items() if k in ('W', 'att_src', 'att_dst', 'bias_gat', 'gate_weights', 'ln_gamma', 'ln_beta', 'Wo', 'bo')}
    del _L0_gnn_all

    def _L0_mix_setup():
        import jax, jax.numpy as jnp
        import numpy as np
        EPS_NORM = 1e-06
        EPS_ATTN = 1e-06
        HEADS = 8

        def rmsnorm(x, w):
            ms = jnp.mean(x * x, axis=-1, keepdims=True)
            return w * (x * jax.lax.rsqrt(ms + EPS_NORM))

        def linear_attention(x, w_qkv, w_out, b_out):
            B, N, D = x.shape
            hd = D // HEADS
            qkv = (x @ w_qkv).reshape(B, N, 3, HEADS, hd)
            q, k, v = (qkv[:, :, 0], qkv[:, :, 1], qkv[:, :, 2])
            q = jax.nn.elu(q) + 1.0
            k = jax.nn.elu(k) + 1.0
            kv = jnp.einsum('bnhd,bnhm->bhdm', k, v)
            z = 1.0 / (jnp.einsum('bnhd,bhd->bnh', q, k.sum(axis=1)) + EPS_ATTN)
            out = jnp.einsum('bnhd,bhdm,bnh->bnhm', q, kv, z)
            out = out.reshape(B, N, D)
            return out @ w_out + b_out
        key = jax.random.key(seed)
        ks = jax.random.split(key, 4)
        B, N, D = (16, 256, 256)
        x = jax.random.normal(ks[0], (B, N, D), dtype=jnp.float32)
        w_norm1 = jnp.ones((D,), dtype=jnp.float32)
        w_qkv = jax.random.normal(ks[1], (D, 3 * D), dtype=jnp.float32) * 0.02
        w_out = jax.random.normal(ks[2], (D, D), dtype=jnp.float32) * 0.02
        b_out = jnp.zeros((D,), dtype=jnp.float32)
        w_norm2 = jnp.ones((D,), dtype=jnp.float32)
        return {'x': x, 'w_norm1': w_norm1, 'w_qkv': w_qkv, 'w_out': w_out, 'b_out': b_out, 'w_norm2': w_norm2}
    _L0_mix_all = _L0_mix_setup()
    _L0_mix_in = {k: v for k, v in _L0_mix_all.items() if k in ('w_norm1', 'w_qkv', 'w_out', 'b_out', 'w_norm2')}
    del _L0_mix_all

    def _L0_ffn_setup():
        import jax, jax.numpy as jnp
        import numpy as np
        B, S, H, F, E, K = (8, 128, 256, 512, 16, 2)
        EPS = 1e-05
        key = jax.random.key(seed)
        ks = jax.random.split(key, 9)
        sc = 0.02
        return {'x': jax.random.normal(ks[0], (B, S, H), dtype=jnp.float32), 'gate_w': jax.random.normal(ks[1], (H, E), dtype=jnp.float32) * sc, 'gate_b': jnp.zeros((E,), dtype=jnp.float32), 'w1': jax.random.normal(ks[2], (E, H, F), dtype=jnp.float32) * sc, 'b1': jnp.zeros((E, F), dtype=jnp.float32), 'w2': jax.random.normal(ks[3], (E, F, H), dtype=jnp.float32) * sc, 'b2': jnp.zeros((E, H), dtype=jnp.float32), 'gamma': jnp.ones((H,), dtype=jnp.float32), 'beta': jnp.zeros((H,), dtype=jnp.float32)}
    _L0_ffn_all = _L0_ffn_setup()
    _L0_ffn_in = {k: v for k, v in _L0_ffn_all.items() if k in ('gate_w', 'gate_b', 'w1', 'b1', 'w2', 'b2', 'gamma', 'beta')}
    del _L0_ffn_all
    return {'x': x, 'src': src, 'dst': dst, 'L0_gnn_W': _L0_gnn_in['W'], 'L0_gnn_att_src': _L0_gnn_in['att_src'], 'L0_gnn_att_dst': _L0_gnn_in['att_dst'], 'L0_gnn_bias_gat': _L0_gnn_in['bias_gat'], 'L0_gnn_gate_weights': _L0_gnn_in['gate_weights'], 'L0_gnn_ln_gamma': _L0_gnn_in['ln_gamma'], 'L0_gnn_ln_beta': _L0_gnn_in['ln_beta'], 'L0_gnn_Wo': _L0_gnn_in['Wo'], 'L0_gnn_bo': _L0_gnn_in['bo'], 'L0_mix_w_norm1': _L0_mix_in['w_norm1'], 'L0_mix_w_qkv': _L0_mix_in['w_qkv'], 'L0_mix_w_out': _L0_mix_in['w_out'], 'L0_mix_b_out': _L0_mix_in['b_out'], 'L0_mix_w_norm2': _L0_mix_in['w_norm2'], 'L0_ffn_gate_w': _L0_ffn_in['gate_w'], 'L0_ffn_gate_b': _L0_ffn_in['gate_b'], 'L0_ffn_w1': _L0_ffn_in['w1'], 'L0_ffn_b1': _L0_ffn_in['b1'], 'L0_ffn_w2': _L0_ffn_in['w2'], 'L0_ffn_b2': _L0_ffn_in['b2'], 'L0_ffn_gamma': _L0_ffn_in['gamma'], 'L0_ffn_beta': _L0_ffn_in['beta']}

def reference(x, src, dst, L0_gnn_W, L0_gnn_att_src, L0_gnn_att_dst, L0_gnn_bias_gat, L0_gnn_gate_weights, L0_gnn_ln_gamma, L0_gnn_ln_beta, L0_gnn_Wo, L0_gnn_bo, L0_mix_w_norm1, L0_mix_w_qkv, L0_mix_w_out, L0_mix_b_out, L0_mix_w_norm2, L0_ffn_gate_w, L0_ffn_gate_b, L0_ffn_w1, L0_ffn_b1, L0_ffn_w2, L0_ffn_b2, L0_ffn_gamma, L0_ffn_beta):
    import jax
    import jax.numpy as jnp

    def _L0_gnn_ref(x, edge_index, W, att_src, att_dst, bias_gat, gate_weights, ln_gamma, ln_beta, Wo, bo):
        import jax, jax.numpy as jnp
        import numpy as np
        N_NODES, IN_DIM, HID, OUT_DIM, H, E = (50000, 256, 256, 256, 8, 12500)
        NEG_SLOPE = 0.2
        LN_EPS = 1e-05
        N = x.shape[0]
        D = W.shape[2]
        loops = jnp.arange(N, dtype=edge_index.dtype)
        src = jnp.concatenate([edge_index[0], loops])
        dst = jnp.concatenate([edge_index[1], loops])
        h = jnp.einsum('nf,hfd->hnd', x, W)
        a_s = jnp.einsum('hnd,hd->hn', h, att_src)
        a_d = jnp.einsum('hnd,hd->hn', h, att_dst)
        e = jax.nn.leaky_relu(a_s[:, src] + a_d[:, dst], NEG_SLOPE)
        gw = jax.nn.softmax(gate_weights)

        def head_step(acc, xs):
            h_h, e_h, g_h = xs
            m = jax.ops.segment_max(e_h, dst, num_segments=N)
            ex = jnp.exp(e_h - m[dst])
            den = jax.ops.segment_sum(ex, dst, num_segments=N)
            alpha = ex / den[dst]
            out = jax.ops.segment_sum(h_h[src] * alpha[:, None], dst, num_segments=N)
            return (acc + g_h * out, None)
        agg, _ = jax.lax.scan(head_step, jnp.zeros((N, D), x.dtype), (h, e, gw))
        agg = agg + gw @ bias_gat
        res = agg + x[:, :D]
        mu = jnp.mean(res, axis=-1, keepdims=True)
        var = jnp.var(res, axis=-1, keepdims=True)
        ln = ln_gamma * (res - mu) * jax.lax.rsqrt(var + LN_EPS) + ln_beta
        return ln @ Wo.T + bo

    def _L0_mix_ref(x, w_norm1, w_qkv, w_out, b_out, w_norm2):
        import jax, jax.numpy as jnp
        import numpy as np
        EPS_NORM = 1e-06
        EPS_ATTN = 1e-06
        HEADS = 8

        def rmsnorm(x, w):
            ms = jnp.mean(x * x, axis=-1, keepdims=True)
            return w * (x * jax.lax.rsqrt(ms + EPS_NORM))

        def linear_attention(x, w_qkv, w_out, b_out):
            B, N, D = x.shape
            hd = D // HEADS
            qkv = (x @ w_qkv).reshape(B, N, 3, HEADS, hd)
            q, k, v = (qkv[:, :, 0], qkv[:, :, 1], qkv[:, :, 2])
            q = jax.nn.elu(q) + 1.0
            k = jax.nn.elu(k) + 1.0
            kv = jnp.einsum('bnhd,bnhm->bhdm', k, v)
            z = 1.0 / (jnp.einsum('bnhd,bhd->bnh', q, k.sum(axis=1)) + EPS_ATTN)
            out = jnp.einsum('bnhd,bhdm,bnh->bnhm', q, kv, z)
            out = out.reshape(B, N, D)
            return out @ w_out + b_out
        h = x + linear_attention(rmsnorm(x, w_norm1), w_qkv, w_out, b_out)
        return h + rmsnorm(h, w_norm2)

    def _L0_ffn_ref(x, gate_w, gate_b, w1, b1, w2, b2, gamma, beta):
        import jax, jax.numpy as jnp
        import numpy as np
        B, S, H, F, E, K = (8, 128, 256, 512, 16, 2)
        EPS = 1e-05
        gate_logits = x @ gate_w + gate_b
        topk_vals, topk_idx = jax.lax.top_k(gate_logits, K)
        topk_w = jax.nn.softmax(topk_vals, axis=-1)
        h = jax.nn.relu(jnp.einsum('bsh,ehf->bsef', x, w1) + b1)
        expert_out = jnp.einsum('bsef,efh->bseh', h, w2) + b2
        sel = jnp.take_along_axis(expert_out, topk_idx[:, :, :, None], axis=2)
        moe = jnp.sum(topk_w[..., None] * sel, axis=2)
        y = x + moe
        mu = jnp.mean(y, axis=-1, keepdims=True)
        var = jnp.var(y, axis=-1, keepdims=True)
        return (y - mu) / jnp.sqrt(var + EPS) * gamma + beta
    edge_index = jnp.stack([src, dst])
    xn = _layernorm(x, axis=-1)
    x = x + _L0_gnn_ref(xn, edge_index, L0_gnn_W, L0_gnn_att_src, L0_gnn_att_dst, L0_gnn_bias_gat, L0_gnn_gate_weights, L0_gnn_ln_gamma, L0_gnn_ln_beta, L0_gnn_Wo, L0_gnn_bo) + _L0_mix_ref(xn[None], L0_mix_w_norm1, L0_mix_w_qkv, L0_mix_w_out, L0_mix_b_out, L0_mix_w_norm2)[0]
    x = x + _L0_ffn_ref(_layernorm(x, axis=-1)[None], L0_ffn_gate_w, L0_ffn_gate_b, L0_ffn_w1, L0_ffn_b1, L0_ffn_w2, L0_ffn_b2, L0_ffn_gamma, L0_ffn_beta)[0]
    return x

_drawn_inputs = setup_inputs


def setup_inputs(seed=0):
    import zlib

    import numpy as np

    out = dict(_drawn_inputs(seed))
    spreads = {'L0_gnn_bias_gat': (0.0, 0.698),
     'L0_gnn_gate_weights': (0.125, 0.6),
     'L0_gnn_ln_gamma': (1.0, 0.2),
     'L0_gnn_ln_beta': (0.0, 0.1),
     'L0_gnn_bo': (0.0, 0.1),
     'L0_mix_w_norm1': (1.0, 0.6),
     'L0_mix_b_out': (0.0, 0.1),
     'L0_mix_w_norm2': (1.0, 0.2),
     'L0_ffn_gate_b': (0.0, 0.481),
     'L0_ffn_b1': (0.0, 0.8),
     'L0_ffn_b2': (0.0, 0.454),
     'L0_ffn_gamma': (1.0, 0.2),
     'L0_ffn_beta': (0.0, 0.338)}
    factors = {'L0_gnn_att_dst': 7.148,
     'L0_mix_w_qkv': 8.0,
     'L0_mix_w_out': 8.0,
     'L0_ffn_w1': 3.815,
     'L0_ffn_w2': 3.042}
    for name, (base, spread) in spreads.items():
        noise = np.random.default_rng([zlib.crc32(name.encode()), seed]).standard_normal(out[name].shape)
        drawn = base * np.exp(spread * noise) if base else spread * noise
        out[name] = jnp.asarray(drawn.astype(out[name].dtype))
    for name, factor in factors.items():
        out[name] = (out[name] * factor).astype(out[name].dtype)
    return out
```

```python
from contextlib import ExitStack

import concourse.bass as bass
from concourse import mybir

P = 128
N, D, H = 3125, 256, 8
KD = D // P
NT = -(-N // P)
NP = NT * P
LAST = N - (NT - 1) * P
NE = 50000
CHUNKS = -(-NE // P)
DW = P // H
WINDOWS = -(-N // DW)
STEPS = CHUNKS + WINDOWS - 1
G = 8
GROUPS = -(-STEPS // G)
SJ = -(-(GROUPS * G) // P)
SP_ = SJ * P
ONE, AS = D, D + 1
RW = 272
DST_PAD = 4080
BIG = 1e30
QH = 8
HD = D // QH
E, F, FK = 16, 512, 512 // P
TILES = 2 * NP // P + E
SLOTS = TILES * P
LN_EPS, RMS_EPS, ATT_EPS = 1e-5, 1e-6, 1e-6

F32, BF16 = mybir.dt.float32, mybir.dt.bfloat16
I32, U32 = mybir.dt.int32, mybir.dt.uint32
ALU = mybir.AluOpType
ACT = mybir.ActivationFunctionType
AX = mybir.AxisListType
ds = bass.ds


class Count:

    def __init__(self, sem, n=1):
        self.sem, self.n = sem, n

    def at(self, t, k=None):
        return t * self.n + (self.n if k is None else k)


def wait(eng, count, t, k=None):
    v = count.at(t, k)
    if not isinstance(v, int) or v > 0:
        eng.wait_ge(count.sem, v)


def pipeline(eng, n, stages, U=2, extra=2):
    L = max(lag for lag, _ in stages)
    start = L + extra
    turns = (n - start) // U
    for tau in range(start):
        for lag, stage in stages:
            if 0 <= tau - lag < n:
                t = tau - lag
                stage(t, t % U, t // U)
    with eng.Fori(0, turns) as i:
        for u in range(U):
            for lag, stage in stages:
                t = start + u - lag
                stage(i * U + t, t % U, i + t // U)
    for tau in range(start + turns * U, n + L):
        for lag, stage in stages:
            if 0 <= tau - lag < n:
                t = tau - lag
                stage(t, t % U, t // U)


def tile(T, t, lo, hi):
    return T[:, t, lo:hi] if isinstance(t, int) else T[:, ds(t, 1), lo:hi].rearrange("p t f -> p (t f)")


def col(T, t, n=1):
    return T[:, t * n:t * n + n] if isinstance(t, int) else T[:, ds(t * n, n)]


def row(T, t):
    return T[t * P:(t + 1) * P, :] if isinstance(t, int) else T[ds(t * P, P), :]


def at_row(ap):
    return bass.IndirectOffsetOnAxis(ap=ap, axis=0)


class Line:

    def __init__(self, eng, sem):
        self.eng, self.sem, self.n = eng, sem, 0

    def do(self, ins):
        ins.then_inc(self.sem, 1)
        self.n += 1
        self.eng.wait_ge(self.sem, self.n)


def build(nc, a, out, dbg):
    with ExitStack() as top:
        def dram(name, shape, dt=F32):
            return nc.dram_tensor(name, shape, dt, kind="ExternalOutput" if dbg else "Internal").ap()

        def sb(name, shape, dt=F32, ctx=top):
            return ctx.enter_context(nc.sbuf_tensor(name, shape, dt))

        def ps(ctx, name, shape=(P, 512)):
            return ctx.enter_context(nc.psum_tensor(name, list(shape), F32))

        def sem(name):
            return top.enter_context(nc.semaphore(name))

        node_rows = dram("node_rows", (NP, RW))
        ad_rows = dram("ad_rows", (NP, H))
        xs_rows, ys_rows = dram("xs_rows", (SLOTS, D)), dram("ys_rows", (SLOTS, D))
        agg_rows = dram("agg_rows", (GROUPS * G, P, D))
        cst = sb("cst", [P, 3 * P + 16 + SJ + NT + 1 + 64])
        ident, tri, ones = cst[:, 0:P], cst[:, P:2 * P], cst[:, 2 * P:3 * P]
        o = 3 * P
        iota16, step_no = cst[:, o:o + 16], cst[:, o + 16:o + 16 + SJ]
        o += 16 + SJ
        win_no, dst_no = cst[:, o:o + NT], cst[:, o + NT:o + NT + 1]
        same_step = cst[:, o + NT + 1:o + NT + 65].rearrange("p (s h) -> p s h", h=H)
        xna = sb("xna", [P, NT, RW])
        ad = sb("ad", [P, NT, H])
        W = sb("W", [P, KD, H, D])
        qT = sb("qT", [P, KD, NP])
        kvd = sb("kvd", [P, KD, P + 4])
        gw = sb("gw", [P, H])
        eps = sb("eps", [P, 3])
        s_cst = sem("s_cst")
        s_gate = sem("s_gate")

        with ExitStack() as ctx:
            A = sb("att", [P, 2, H, D], ctx=ctx)
            tmpW = sb("tmpW", [P, H, D], ctx=ctx)
            V = sb("V", [P, KD, 2 * H], ctx=ctx)
            wq = sb("wq", [P, KD, 3 * D], ctx=ctx)
            wn1 = sb("wn1", [P, KD], ctx=ctx)
            gmx = sb("gmx", [P, 2], ctx=ctx)
            st6 = sb("st6", [P, NT, 6], ctx=ctx)
            mean = sb("mean", [P, NT], ctx=ctx)
            var = sb("var", [P, NT], ctx=ctx)
            rs = sb("rs", [P, NT], ctx=ctx)
            rr = sb("rr", [P, NT], ctx=ctx)
            xs = sb("xs", [P, 2, D], ctx=ctx)
            xT = sb("xT", [P, 2, KD, P], ctx=ctx)
            ez = sb("ez", [P, 2, 2 * D], ctx=ctx)
            mz = sb("mz", [P, 2, 2 * D], ctx=ctx)
            qk = sb("qk", [P, 2, 2 * D], ctx=ctx)
            vv = sb("vv", [P, 2, KD, P + 1], ctx=ctx)
            pT = [ps(ctx, f"pT{c}") for c in range(2)]
            pQ = [ps(ctx, f"pQ{c}") for c in range(2)]
            pV = [ps(ctx, f"pV{c}") for c in range(2)]
            pq = ps(ctx, "pq")
            pK = ps(ctx, "pK")[:, 0:KD * (P + 1)].rearrange("p (g n) -> p g n", g=KD)
            s_W, s_att, s_wq, s_gw = sem("s_W"), sem("s_att"), sem("s_wq"), sem("s_gw")
            s_x = [sem(f"s_x{j}") for j in range(5)]
            ones_in, v_line, v_W, v_gw, v_stat = sem("ones_in"), sem("v_line"), sem("v_W"), sem("v_gw"), sem("v_stat")
            a_gw, a_rs = sem("a_gw"), sem("a_rs")
            normed, copied, xT_ps, xT_sb = (Count(sem(n)) for n in ("normed", "copied", "xT_ps", "xT_sb"))
            qkv_ps, elu_e, v_sb = Count(sem("qkv_ps")), Count(sem("elu_e")), Count(sem("v_sb"), 2)
            qk_sb, a_sb, kv_done = Count(sem("qk_sb"), 2), Count(sem("a_sb"), 2), Count(sem("kv_done"))
            qT_ps, qT_sb = Count(sem("qT_ps")), Count(sem("qT_sb"))
            kv_sb, s_st = sem("kv_sb"), sem("s_st")
            with nc.Block() as block:
                @block.sync
                def _(sp):
                    sp.dma_start(cst[:, :], a["cst"][:, :]).then_inc(s_cst, 16)
                    for j in range(5):
                        sp.dma_start(xna[:, 5 * j:5 * j + 5, 0:D],
                                     a["x"][5 * j * P:(5 * j + 5) * P, :].rearrange("(t p) f -> p t f", p=P)).then_inc(s_x[j], 16)
                    for k in range(KD):
                        sp.dma_start(W[:, k, :, :], a["W"][:, k * P:(k + 1) * P, :].rearrange("h p d -> p h d")).then_inc(s_W, 16)
                    wait(sp, a_sb, NT - 1)
                    wait(sp, copied, NT - 1)
                    sp.wait_ge(ones_in, 1)
                    sp.dma_start(node_rows.rearrange("(t p) f -> p t f", p=P), xna[:, :, :]).then_inc(s_st, 16)
                    sp.dma_start(ad_rows.rearrange("(t p) h -> p t h", p=P), ad[:, :, :]).then_inc(s_st, 16)
                    sp.wait_ge(s_st, 32)

                @block.gpsimd
                def _(pool):
                    pool.memset(xna[:, :, AS + H:RW], 0.0)
                    pool.memset(xna[:, :, ONE:ONE + 1], 1.0).then_inc(ones_in, 1)

                @block.scalar
                def _(act):
                    act.dma_start(A[:, 0, :, :], a["att_src"].partition_broadcast(P)).then_inc(s_att, 16)
                    act.dma_start(A[:, 1, :, :], a["att_dst"].partition_broadcast(P)).then_inc(s_att, 16)
                    act.dma_start(wq[:, :, :], a["mix_w_qkv"].rearrange("(k p) n -> p k n", p=P)).then_inc(s_wq, 16)
                    act.dma_start(wn1[:, :], a["mix_w_norm1"][:, :]).then_inc(s_wq, 16)
                    act.dma_start(gw[:, :], a["gate_weights"].partition_broadcast(P)).then_inc(s_gw, 16)
                    act.wait_ge(v_gw, 1)
                    act.activation(gw[:, :], gw[:, :], ACT.Exp, bias=gmx[:, 0:1], accum_out=gmx[:, 1:2]).then_inc(a_gw, 1)
                    act.wait_ge(v_stat, NT + 1)
                    act.activation(rs[:, :], var[:, :], ACT.Sqrt, bias=eps[:, 0:1]).then_inc(a_rs, 1)
                    act.wait_ge(v_stat, NT + 2)
                    act.activation(rr[:, :], rr[:, :], ACT.Sqrt, bias=eps[:, 1:2]).then_inc(a_rs, 1)

                    def copies(t, c, r):
                        wait(act, normed, t)
                        act.sem_inc(s_gate, 1)
                        act.activation(tile(xna, t, 0, D), xs[:, c, :], ACT.Copy).then_inc(copied.sem, 1)
                        wait(act, xT_ps, t)
                        wait(act, qkv_ps, t - 2)
                        act.activation(xT[:, c, :, :], pT[c][:, 0:D].rearrange("p (k f) -> p k f", k=KD), ACT.Copy).then_inc(xT_sb.sem, 1)

                    def exps(t, c, r):
                        wait(act, qkv_ps, t)
                        wait(act, qk_sb, t - 2)
                        act.sem_inc(s_gate, 1)
                        act.activation(ez[:, c, :], pQ[c][:, :], ACT.Exp, scale=col(rr, t)).then_inc(elu_e.sem, 1)

                    def vs(t, c, r):
                        wait(act, kv_done, t - 2)
                        act.sem_inc(s_gate, 1)
                        for g in range(KD):
                            act.activation(vv[:, c, g, 0:P], pV[c][:, g * P:(g + 1) * P], ACT.Copy, scale=col(rr, t)).then_inc(v_sb.sem, 1)

                    act.wait_ge(v_stat, NT + 3)
                    pipeline(act, NT, [(0, copies), (1, exps), (1, vs)])

                @block.tensor
                def _(pe):
                    pe.wait_ge(s_cst, 16)
                    pe.wait_ge(v_W, KD)

                    def xTs(t, c, r):
                        wait(pe, normed, t)
                        wait(pe, xT_sb, t - 2)
                        for k in range(KD):
                            mm = pe.transpose(pT[c][:, k * P:(k + 1) * P], xs[:, c, k * P:(k + 1) * P], ident)
                        mm.then_inc(xT_ps.sem, 1)

                    def qkv(t, c, r):
                        wait(pe, xT_sb, t)
                        wait(pe, elu_e, t - 2)
                        wait(pe, v_sb, t - 2)
                        wait(pe, qk_sb, t - 2)
                        wait(pe, a_sb, t - 2)
                        for k in range(KD):
                            pe.matmul(pQ[c][:, :], xT[:, c, k, :], wq[:, k, 0:2 * D], start=(k == 0), stop=(k == KD - 1))
                        for k in range(KD):
                            pe.matmul(pV[c][:, 0:D], xT[:, c, k, :], wq[:, k, 2 * D:3 * D], start=(k == 0), stop=(k == KD - 1))
                        for k in range(KD):
                            mm = pe.matmul(pV[c][:, D:D + 2 * H], xT[:, c, k, :], V[:, k, :], start=(k == 0), stop=(k == KD - 1))
                        mm.then_inc(qkv_ps.sem, 1)

                    def kv(t, c, r):
                        wait(pe, qk_sb, t)
                        wait(pe, v_sb, t)
                        first, last = isinstance(t, int) and t == 0, isinstance(t, int) and t == NT - 1
                        m = LAST if last else P
                        for g in range(KD):
                            mm = pe.matmul(pK[:, g, :], qk[0:m, c, D + g * P:D + (g + 1) * P], vv[0:m, c, g, :],
                                           start=first and g == 0, stop=last, skip_group_check=True)
                        mm.then_inc(kv_done.sem, 1)
                        wait(pe, qT_sb, t - 1)
                        for k in range(KD):
                            mm = pe.transpose(pq[:, k * P:(k + 1) * P], qk[:, c, k * P:(k + 1) * P], ident)
                        mm.then_inc(qT_ps.sem, 1)

                    pipeline(pe, NT, [(0, xTs), (0, qkv), (1, kv)])

                @block.vector
                def _(dve):
                    line = Line(dve, v_line)
                    dve.memset(eps[:, 0:1], LN_EPS)
                    dve.memset(eps[:, 1:2], RMS_EPS)
                    dve.memset(eps[:, 2:3], 0.0)
                    line.do(dve.memset(vv[:, :, :, P:P + 1], 1.0))
                    dve.wait_ge(s_gw, 16)
                    line.do(dve.tensor_reduce(gmx[:, 0:1], gw[:, :], AX.X, ALU.max))
                    dve.tensor_scalar(gmx[:, 0:1], gmx[:, 0:1], -1.0, None, ALU.mult).then_inc(v_gw, 1)
                    dve.wait_ge(a_gw, 1)
                    line.do(dve.reciprocal(gmx[:, 1:2], gmx[:, 1:2]))
                    line.do(dve.tensor_scalar(gw[:, :], gw[:, :], gmx[:, 1:2], None, ALU.mult))
                    for j in range(5):
                        dve.wait_ge(s_x[j], 16)
                    with dve.Fori(0, NT) as t:
                        dve.bn_stats(tile(st6, t, 0, 6), tile(xna, t, 0, D)).then_inc(v_stat, 1)
                    dve.wait_ge(v_stat, NT)
                    line.do(dve.tensor_tensor(mean[:, :], st6[:, :, 1], st6[:, :, 4], ALU.subtract))
                    line.do(dve.tensor_scalar(mean[:, :], mean[:, :], 0.5, None, ALU.mult))
                    line.do(dve.tensor_tensor(mean[:, :], mean[:, :], mean[:, :], ALU.mult))
                    line.do(dve.tensor_tensor(var[:, :], st6[:, :, 2], st6[:, :, 5], ALU.add))
                    line.do(dve.scalar_tensor_tensor(out=var[:, :], in0=var[:, :], scalar=1.0 / D, in1=mean[:, :], op0=ALU.mult, op1=ALU.add))
                    line.do(dve.tensor_tensor(mean[:, :], st6[:, :, 1], st6[:, :, 4], ALU.add))
                    line.do(dve.tensor_scalar(mean[:, :], mean[:, :], 0.5, None, ALU.mult))
                    dve.sem_inc(v_stat, 1)
                    dve.wait_ge(a_rs, 1)
                    line.do(dve.reciprocal(rs[:, :], rs[:, :]))
                    line.do(dve.tensor_tensor(rr[:, :], rs[:, :], rs[:, :], ALU.mult))
                    dve.tensor_tensor(rr[:, :], rr[:, :], var[:, :], ALU.mult).then_inc(v_stat, 1)
                    dve.wait_ge(a_rs, 2)
                    dve.reciprocal(rr[:, :], rr[:, :]).then_inc(v_stat, 1)
                    dve.wait_ge(v_stat, NT + 3)
                    dve.wait_ge(s_W, 32)
                    dve.wait_ge(s_att, 32)
                    for k in range(KD):
                        for i in range(2):
                            line.do(dve.tensor_tensor(tmpW[:, :, :], W[:, k, :, :], A[:, i, :, :], ALU.mult))
                            line.do(dve.tensor_reduce(V[:, k, i * H:(i + 1) * H], tmpW[:, :, :], AX.X, ALU.add))
                    dve.wait_ge(s_wq, 32)
                    for k in range(KD):
                        dve.tensor_scalar(wq[:, k, :], wq[:, k, :], wn1[:, k:k + 1], None, ALU.mult).then_inc(v_W, 1)

                    def norm(t, c, r):
                        wait(dve, xT_ps, t - 2)
                        wait(dve, copied, t - 2)
                        dve.tensor_scalar(xs[:, c, :], tile(xna, t, 0, D), col(mean, t), col(rs, t), ALU.subtract, ALU.mult).then_inc(normed.sem, 1)

                    def elu(t, c, r):
                        wait(dve, elu_e, t)
                        dve.tensor_scalar(mz[:, c, :], pQ[c][:, :], col(rr, t), 0.0, ALU.mult, ALU.max).then_inc(qk_sb.sem, 1)
                        wait(dve, qk_sb, t, 1)
                        wait(dve, kv_done, t - 2)
                        wait(dve, qT_ps, t - 2)
                        dve.scalar_tensor_tensor(out=qk[:, c, :], in0=ez[:, c, :], scalar=1.0, in1=mz[:, c, :], op0=ALU.min, op1=ALU.add).then_inc(qk_sb.sem, 1)
                        wait(dve, v_sb, t)
                        dve.tensor_scalar(tile(xna, t, AS, AS + H), pV[c][:, D:D + H], 0.0, None, ALU.add).then_inc(a_sb.sem, 1)
                        dve.tensor_scalar(tile(ad, t, 0, H), pV[c][:, D + H:D + 2 * H], 0.0, None, ALU.add).then_inc(a_sb.sem, 1)

                    def qTs(t, c, r):
                        wait(dve, qT_ps, t)
                        for k in range(KD):
                            ins = dve.tensor_scalar(qT[:, k, t * P:(t + 1) * P] if isinstance(t, int) else qT[:, k, ds(t * P, P)],
                                                    pq[:, k * P:(k + 1) * P], 0.0, None, ALU.add)
                        ins.then_inc(qT_sb.sem, 1)

                    pipeline(dve, NT, [(0, norm), (1, elu), (2, qTs)])
                    wait(dve, kv_done, NT - 1)
                    dve.memset(kvd[:, :, :], 0.0).then_inc(kv_sb, 1)
                    dve.wait_ge(kv_sb, 1)
                    for g in range(KD):
                        for b in range(P // HD):
                            s = slice(b * HD, (b + 1) * HD)
                            dve.tensor_copy(kvd[s, g, b * HD:(b + 1) * HD], pK[s, g, b * HD:(b + 1) * HD]).then_inc(kv_sb, 1)
                            dve.tensor_copy(kvd[s, g, P + b:P + b + 1], pK[s, g, P:P + 1]).then_inc(kv_sb, 1)
                    dve.wait_ge(kv_sb, 1 + 2 * KD * (P // HD))


        md_rows = dram("md_rows", (SP_ * DW, 2 * H))
        last_row = sb("last_row", [P, NT], U32)
        edge_ctx = ExitStack()
        srcT = sb("srcT", [P, SP_], U32, edge_ctx)
        dlocT = sb("dlocT", [P, SP_], ctx=edge_ctx)
        resetT = sb("resetT", [P, SP_], ctx=edge_ctx)
        adsd = sb("adsd", [P, SP_ // G, H], ctx=edge_ctx)
        with ExitStack() as ctx:
            C1 = CHUNKS - 1
            end_i = sb("end_i", [1, C1], I32, ctx)
            ends = sb("ends", [1, 3, C1], ctx=ctx)
            junk = sb("junk", [P, C1], ctx=ctx)
            cs = sb("cs", [P, 6, SJ], ctx=ctx)
            rowc = sb("rowc", [P, 2, SJ], U32, ctx)
            cnt = sb("cnt", [P, NT], ctx=ctx)
            gsrc = sb("gsrc", [P, SJ, P], I32, ctx)
            gdst = sb("gdst", [P, SJ, P], I32, ctx)
            gad = sb("gad", [P, SJ, P], ctx=ctx)
            tab = sb("tab", [P, SJ, 3, P], ctx=ctx)
            pE = ps(ctx, "pE")
            pW = ps(ctx, "pW")
            pj = [ps(ctx, f"pj{j}") for j in range(SJ)]
            ad_step = dram("ad_step", (SP_, P))
            s_end, end_ready, ends_ps, v_sch, rows_ready = sem("s_end"), sem("end_ready"), sem("ends_ps"), sem("v_sch"), sem("rows_ready")
            s_gsd, s_gad, tabs, tabs_ps, s_ads = sem("s_gsd"), sem("s_gad"), sem("tabs"), sem("tabs_ps"), sem("s_ads")
            with nc.Block() as block:
                @block.sync
                def _(sp):
                    sp.dma_start(end_i[:, :], a["chunk_end"][:, :]).then_inc(s_end, 16)
                    sp.dma_start(ends[:, 2, :], a["chunk_no"][:, :]).then_inc(s_end, 16)
                    sp.wait_ge(s_gad, 16 * SJ)
                    sp.dma_start(ad_step.rearrange("(j p) n -> p j n", p=P), gad[:, :, :]).then_inc(s_ads, 16)
                    sp.wait_ge(s_ads, 16)
                    sp.dma_start(adsd[:, :, :], ad_step.rearrange("(g s) (d h) -> (s d) g h", s=G, h=H)).then_inc(s_ads, 16)
                    sp.wait_ge(s_ads, 32)

                @block.vector
                def _(dve):
                    line = Line(dve, v_sch)
                    dve.wait_ge(s_end, 32)
                    line.do(dve.tensor_scalar(end_i[:, :], end_i[:, :], 4, None, ALU.arith_shift_right))
                    line.do(dve.tensor_copy(ends[:, 0, :], end_i[:, :]))
                    dve.tensor_tensor(ends[:, 1, :], ends[:, 0, :], ends[:, 2, :], ALU.add).then_inc(end_ready, 1)
                    line.do(dve.tensor_scalar(cs[:, 5, :], step_no, -1.0, None, ALU.add))
                    dve.wait_ge(ends_ps, 2)
                    for j in range(SJ):
                        line.do(dve.tensor_scalar(junk[:, :], pE[:, 0:C1], step_no[:, j:j + 1], None, ALU.is_lt, ALU.add, accum_out=cs[:, 0, j:j + 1]))
                        line.do(dve.tensor_scalar(junk[:, :], pE[:, 0:C1], cs[:, 5, j:j + 1], None, ALU.is_lt, ALU.add, accum_out=cs[:, 1, j:j + 1]))
                    line.do(dve.tensor_copy(rowc[:, 0, :], cs[:, 0, :]))
                    line.do(dve.tensor_tensor(cs[:, 2, :], step_no, cs[:, 0, :], ALU.subtract))
                    line.do(dve.tensor_scalar(cs[:, 3, :], cs[:, 2, :], float(DW), None, ALU.mult))
                    line.do(dve.tensor_scalar(rowc[:, 1, :], cs[:, 2, :], float(WINDOWS - 1), None, ALU.min))
                    dve.sem_inc(rows_ready, 1)
                    line.do(dve.tensor_tensor(cs[:, 4, :], cs[:, 0, :], cs[:, 1, :], ALU.subtract))
                    line.do(dve.tensor_scalar(cs[:, 4, :], cs[:, 4, :], -1.0, BIG, ALU.add, ALU.mult))
                    for t in range(NT):
                        line.do(dve.tensor_scalar(junk[:, :], pW[:, 0:C1], win_no[:, t:t + 1], None, ALU.is_le, ALU.add, accum_out=cnt[:, t:t + 1]))
                    line.do(dve.tensor_tensor(cnt[:, :], cnt[:, :], win_no, ALU.add))
                    line.do(dve.tensor_scalar(last_row[:, :], cnt[:, :], float(DW), dst_no, ALU.mult, ALU.add))
                    dve.wait_ge(s_gsd, 32 * SJ)
                    for j in range(SJ):
                        dve.tensor_copy(tab[:, j, 0, :], gsrc[:, j, :])
                        dve.tensor_scalar(tab[:, j, 1, :], gdst[:, j, :], cs[:, 3, j:j + 1], None, ALU.subtract)
                        dve.tensor_scalar(tab[:, j, 2, :], ones, cs[:, 4, j:j + 1], None, ALU.mult).then_inc(tabs, 1)
                    for j in range(SJ):
                        dve.wait_ge(tabs_ps, j + 1)
                        s = slice(j * P, (j + 1) * P)
                        dve.tensor_copy(srcT[:, s], pj[j][:, 0:P])
                        dve.tensor_copy(dlocT[:, s], pj[j][:, P:2 * P])
                        dve.tensor_copy(resetT[:, s], pj[j][:, 2 * P:3 * P])

                @block.tensor
                def _(pe):
                    pe.wait_ge(end_ready, 1)
                    pe.matmul(pE[:, 0:C1], ones[0:1, :], ends[:, 1, :], start=True, stop=True).then_inc(ends_ps, 1)
                    pe.matmul(pW[:, 0:C1], ones[0:1, :], ends[:, 0, :], start=True, stop=True).then_inc(ends_ps, 1)
                    for j in range(SJ):
                        pe.wait_ge(tabs, j + 1)
                        for i in range(3):
                            mm = pe.transpose(pj[j][:, i * P:(i + 1) * P], tab[:, j, i, :], ident)
                        mm.then_inc(tabs_ps, 1)

                @block.gpsimd
                def _(pool):
                    pool.wait_ge(rows_ready, 1)
                    for j in range(SJ):
                        pool.indirect_dma_start(gad[:, j, :], None, ad_rows.rearrange("(w d) h -> w (d h)", d=DW), at_row(rowc[:, 1, j:j + 1])).then_inc(s_gad, 16)
                    for j in range(SJ):
                        pool.indirect_dma_start(gsrc[:, j, :], None, a["src"][:, :], at_row(rowc[:, 0, j:j + 1])).then_inc(s_gsd, 16)
                        pool.indirect_dma_start(gdst[:, j, :], None, a["dst"][:, :], at_row(rowc[:, 0, j:j + 1])).then_inc(s_gsd, 16)

        with ExitStack() as ctx:
            U, V2 = 6, 2
            idx = sb("idx", [P, U, G], U32, ctx)
            rows = sb("rows", [P, U, G, RW], ctx=ctx)
            eq = sb("eq", [P, V2, G, DW], ctx=ctx)
            pen = sb("pen", [P, V2, G, DW], ctx=ctx)
            adb = sb("adb", [P, V2, G, H], ctx=ctx)
            eqT = sb("eqT", [P, V2, P], ctx=ctx)
            zs = sb("zs", [P, V2, 2, G, H], ctx=ctx)
            zm = sb("zm", [P, V2, G, DW, H], ctx=ctx)
            mst = sb("mst", [P, V2, 3, G], ctx=ctx)
            rsc = sb("rsc", [P, V2, G], ctx=ctx)
            pexp = sb("pexp", [P, V2, G, P], ctx=ctx)
            pw = sb("pw", [P, V2, G, P], ctx=ctx)
            acc = sb("acc", [P, V2, G, D + 2], ctx=ctx)
            mall = sb("mall", [P, SP_ + 8], ctx=ctx)
            dall = sb("dall", [P, SP_], ctx=ctx)
            mdT = sb("mdT", [P, 2, DW, 2, H], ctx=ctx)
            pA = ps(ctx, "pA", (P, 1024))
            pP = ps(ctx, "pP", (P, 1024))
            pO = [ps(ctx, f"pO{i}") for i in range(3)]
            pM = ps(ctx, "pM")
            zero = sb("zero", [P, D], ctx=ctx)
            zero_in, s_zero = sem("zero_in"), sem("s_zero")
            first_set, s_md = sem("first_set"), [sem("s_md0"), sem("s_md1")]
            s_rows = [sem(f"s_rows{c}") for c in range(U)]
            s_agg = [sem(f"s_agg{c}") for c in range(V2)]
            idx_in, masks, eqT_ps, eqT_sb = Count(sem("idx_in")), Count(sem("masks"), 3), Count(sem("eqT_ps")), Count(sem("eqT_sb"))
            adE_ps, scored, zT_ps, maxed = Count(sem("adE_ps")), Count(sem("scored"), 3), Count(sem("zT_ps")), Count(sem("maxed"), 5)
            exped, pT_ps, pw_in, prod, acced = Count(sem("exped"), 2), Count(sem("pT_ps")), Count(sem("pw_in")), Count(sem("prod"), G), Count(sem("acced"), G + 1)
            md_ps, md_sb = Count(sem("md_ps")), Count(sem("md_sb"))

            def half(g, c, r):
                return r * (U // V2) + c // V2

            with nc.Block() as block:
                @block.gpsimd
                def _(pool):
                    pool.memset(zero[:, :], 0.0).then_inc(zero_in, 1)

                    def gather(g, c, r):
                        wait(pool, prod, g - U)
                        pool.sem_inc(s_gate, 1)
                        pool.tensor_copy(idx[:, c, :], col(srcT, g, G)).then_inc(idx_in.sem, 1)
                        wait(pool, idx_in, g)
                        pool.sem_inc(s_gate, 1)
                        for s in range(G):
                            pool.indirect_dma_start(rows[:, c, s, :], None, node_rows[:, :], at_row(idx[:, c, s:s + 1])).then_inc(s_rows[c], 16)
                    pipeline(pool, GROUPS, [(0, gather)], U, U)

                @block.vector
                def _(dve):
                    dve.memset(acc[:, V2 - 1, G - 1, :], 0.0)
                    dve.memset(dall[:, :], 0.0)
                    dve.memset(mall[:, :], 0.0).then_inc(first_set, 1)
                    dve.wait_ge(first_set, 1)

                    m_at = lambda g, one: mall[:, one + g * G:one + g * G + G] if isinstance(g, int) else mall[:, ds(g * G + one, G)]

                    def mask_eq(g, c, r):
                        wait(dve, eqT_ps, g - V2)
                        wait(dve, masks, g - V2)
                        dve.tensor_tensor(eq[:, c % V2, :, :], col(dlocT, g, G).unsqueeze(2).to_broadcast([P, G, DW]),
                                          iota16.unsqueeze(1).to_broadcast([P, G, DW]), ALU.is_equal).then_inc(masks.sem, 1)

                    def mask_ad(g, c, r):
                        wait(dve, adE_ps, g - V2)
                        dve.tensor_tensor(adb[:, c % V2, :, :], same_step, tile(adsd, g, 0, H).unsqueeze(1).to_broadcast([P, G, H]),
                                          ALU.mult).then_inc(masks.sem, 1)

                    def mask_pen(g, c, r):
                        wait(dve, masks, g, 1)
                        wait(dve, scored, g - V2)
                        dve.tensor_scalar(pen[:, c % V2, :, :], eq[:, c % V2, :, :], -1.0, BIG, ALU.add, ALU.mult).then_inc(masks.sem, 1)

                    def score_sum(g, c, r):
                        dve.wait_ge(s_rows[c], (r + 1) * (16 * G))
                        wait(dve, adE_ps, g)
                        dve.tensor_tensor(zs[:, c % V2, 0, :, :], rows[:, c, :, AS:AS + H], pM[:, P:P + G * H].rearrange("p (s h) -> p s h", h=H),
                                          ALU.add).then_inc(scored.sem, 1)

                    def score_relu(g, c, r):
                        wait(dve, scored, g, 1)
                        dve.scalar_tensor_tensor(out=zs[:, c % V2, 1, :, :], in0=zs[:, c % V2, 0, :, :], scalar=0.2, in1=zs[:, c % V2, 0, :, :],
                                                 op0=ALU.mult, op1=ALU.max).then_inc(scored.sem, 1)

                    def score_mask(g, c, r):
                        wait(dve, scored, g, 2)
                        wait(dve, masks, g)
                        wait(dve, zT_ps, g - V2)
                        dve.tensor_tensor(zm[:, c % V2, :, :, :], zs[:, c % V2, 1, :, :].unsqueeze(2).to_broadcast([P, G, DW, H]),
                                          pen[:, c % V2, :, :].unsqueeze(3).to_broadcast([P, G, DW, H]), ALU.add).then_inc(scored.sem, 1)

                    def max_step(g, c, r):
                        wait(dve, zT_ps, g)
                        wait(dve, maxed, g - 1)
                        wait(dve, exped, g - V2)
                        dve.tensor_reduce(mst[:, c % V2, 0, :], pA[:, :].rearrange("p (s e) -> p s e", s=G), AX.X, ALU.max).then_inc(maxed.sem, 1)

                    def max_scan(g, c, r):
                        wait(dve, maxed, g, 1)
                        dve.tensor_tensor_scan(m_at(g, 1), col(resetT, g, G), mst[:, c % V2, 0, :], mall[:, g * G:g * G + 1] if isinstance(g, int) else mall[:, ds(g * G, 1)],
                                               ALU.add, ALU.max).then_inc(maxed.sem, 1)

                    def max_neg(g, c, r):
                        wait(dve, maxed, g, 2)
                        dve.tensor_scalar(mst[:, c % V2, 1, :], m_at(g, 1), -1.0, None, ALU.mult).then_inc(maxed.sem, 1)

                    def max_old(g, c, r):
                        dve.tensor_tensor(mst[:, c % V2, 2, :], col(mall, g, G), col(resetT, g, G), ALU.add).then_inc(maxed.sem, 1)

                    def max_change(g, c, r):
                        wait(dve, maxed, g, 4)
                        dve.tensor_tensor(mst[:, c % V2, 2, :], mst[:, c % V2, 2, :], mst[:, c % V2, 1, :], ALU.add).then_inc(maxed.sem, 1)

                    def accumulate(s):
                        def stage(g, c, r):
                            if s == 0:
                                wait(dve, exped, g)
                                if not isinstance(g, int) or g >= V2:
                                    dve.wait_ge(s_agg[c % V2], half(g, c, r) * 16)
                            wait(dve, prod, g, s + 1)
                            before = acc[:, c % V2, s - 1, 0:D + 1] if s else acc[:, (c - 1) % V2, G - 1, 0:D + 1]
                            if s or not (isinstance(g, int) and g == 0):
                                wait(dve, acced, g if s else g - 1, s if s else None)
                            dve.scalar_tensor_tensor(out=acc[:, c % V2, s, 0:D + 1], in0=before, scalar=rsc[:, c % V2, s:s + 1],
                                                     in1=pO[(c * G + s) % 3][:, 0:D + 1], op0=ALU.mult, op1=ALU.add).then_inc(acced.sem, 1)
                        return stage

                    def keep_den(g, c, r):
                        wait(dve, acced, g, G)
                        dve.tensor_scalar(col(dall, g, G), acc[:, c % V2, :, D], 0.0, None, ALU.add).then_inc(acced.sem, 1)

                    add = [(4, accumulate(s)) for s in range(G)]
                    pipeline(dve, GROUPS, [(2, score_sum), (0, mask_eq), (2, score_relu), (0, mask_ad), (2, score_mask), (3, max_step),
                                           add[0], (3, max_scan), add[1], (3, max_neg), add[2], (3, max_old), add[3], (3, max_change),
                                           add[4], (0, mask_pen), add[5], add[6], add[7], (4, keep_den)], U, U)
                    for j in range(SJ):
                        for i in range(2):
                            wait(dve, md_ps, 2 * j + i)
                            if j >= 2 and i == 0:
                                dve.wait_ge(s_md[j % 2], 16 * (j // 2))
                            dve.tensor_copy(mdT[:, j % 2, :, i, :], (pM, pA)[i][:, 0:P].rearrange("p (d h) -> p d h", h=H)).then_inc(md_sb.sem, 1)

                @block.scalar
                def _(act):
                    def copy_eq(g, c, r):
                        wait(act, eqT_ps, g)
                        wait(act, adE_ps, g - V2)
                        act.activation(eqT[:, c % V2, :], pM[:, 0:P], ACT.Copy).then_inc(eqT_sb.sem, 1)

                    def exps(g, c, r):
                        wait(act, maxed, g)
                        wait(act, pT_ps, g - V2)
                        wait(act, acced, g - V2)
                        for s in range(G):
                            ins = act.activation(pexp[:, c % V2, s, :], pA[:, s * P:(s + 1) * P], ACT.Exp, bias=mst[:, c % V2, 1, s:s + 1])
                        ins.then_inc(exped.sem, 1)
                        act.activation(rsc[:, c % V2, :], mst[:, c % V2, 2, :], ACT.Exp).then_inc(exped.sem, 1)

                    def copy_p(g, c, r):
                        wait(act, pT_ps, g)
                        wait(act, prod, g - V2)
                        act.activation(pw[:, c % V2, :, :], pP[:, :].rearrange("p (s e) -> p s e", s=G), ACT.Copy).then_inc(pw_in.sem, 1)

                    pipeline(act, GROUPS, [(4, copy_p), (1, copy_eq), (3, exps)], U, U)

                @block.tensor
                def _(pe):
                    def eq_turn(g, c, r):
                        wait(pe, masks, g, 1)
                        wait(pe, scored, g - 1, 1)
                        pe.transpose(pM[:, 0:P], eq[:, c % V2, :, :].rearrange("p s d -> p (s d)"), ident).then_inc(eqT_ps.sem, 1)

                    def ad_edges(g, c, r):
                        wait(pe, eqT_sb, g)
                        wait(pe, masks, g, 2)
                        pe.matmul(pM[:, P:P + G * H], eqT[:, c % V2, :], adb[:, c % V2, :, :].rearrange("p s h -> p (s h)"), start=True, stop=True).then_inc(adE_ps.sem, 1)

                    def z_turn(g, c, r):
                        wait(pe, scored, g)
                        wait(pe, exped, g - 1, 1)
                        for s in range(G):
                            mm = pe.transpose(pA[:, s * P:(s + 1) * P], zm[:, c % V2, s, :, :].rearrange("p d h -> p (d h)"), ident)
                        mm.then_inc(zT_ps.sem, 1)

                    def p_turn(g, c, r):
                        wait(pe, exped, g, 1)
                        wait(pe, pw_in, g - 1)
                        for s in range(G):
                            mm = pe.transpose(pP[:, s * P:(s + 1) * P], pexp[:, c % V2, s, :], ident)
                        mm.then_inc(pT_ps.sem, 1)

                    def product(lo, hi):
                        def stage(g, c, r):
                            if lo == 0:
                                wait(pe, pw_in, g)
                            for s in range(lo, hi):
                                if s >= 3:
                                    wait(pe, acced, g, s - 2)
                                elif not isinstance(g, int) or g > 0:
                                    wait(pe, acced, g - 1, G - 2 + s)
                                pe.matmul(pO[(c * G + s) % 3][:, 0:D + 1], pw[:, c % V2, s, :], rows[:, c, s, 0:D + 1], start=True, stop=True).then_inc(prod.sem, 1)
                        return stage

                    pipeline(pe, GROUPS, [(4, p_turn), (3, z_turn), (1, eq_turn), (4, product(0, 4)), (1, ad_edges), (4, product(4, G))], U, U)
                    wait(pe, acced, GROUPS - 1)
                    for j in range(SJ):
                        for i in range(2):
                            if j:
                                wait(pe, md_sb, 2 * (j - 1) + i)
                            pe.transpose((pM, pA)[i][:, 0:P], (mall[:, 1 + j * P:1 + (j + 1) * P], dall[:, j * P:(j + 1) * P])[i], ident).then_inc(md_ps.sem, 1)

                @block.sync
                def _(sp):
                    def store(g, c, r):
                        wait(sp, acced, g)
                        o8 = agg_rows[g * G:(g + 1) * G, :, :] if isinstance(g, int) else agg_rows[ds(g * G, G), :, :]
                        sp.dma_start(o8.rearrange("s p f -> p s f"), acc[:, c % V2, :, 0:D]).then_inc(s_agg[c % V2], 16)
                    sp.wait_ge(zero_in, 1)
                    sp.dma_start(xs_rows.rearrange("(j p) f -> p j f", p=P), zero[:, :].unsqueeze(1).to_broadcast([P, TILES, D])).then_inc(s_zero, 16)
                    pipeline(sp, GROUPS, [(0, store)], U, U)
                    sp.wait_ge(s_zero, 16)
                    for c in range(V2):
                        sp.wait_ge(s_agg[c], 16 * len(range(c, GROUPS, V2)))
                    for j in range(SJ):
                        wait(sp, md_sb, 2 * j + 1)
                        sp.dma_start(md_rows.rearrange("(j p d) m -> j p d m", p=P, d=DW)[j], mdT[:, j % 2, :, :, :].rearrange("p d i h -> p d (i h)")).then_inc(s_md[j % 2], 16)
                    sp.wait_ge(s_md[0], 16 * 3)
                    sp.wait_ge(s_md[1], 16 * 2)
        edge_ctx.close()

        y_all = sb("y_all", [P, NT, D])
        x2 = sb("x2", [P, NT, D])
        al = sb("al", [P, 2, NT, H])
        lg = sb("lg", [P, NT, E])
        kept = ExitStack()
        with ExitStack() as ctx:
            U = 4
            qs = sb("qs", [P, U, KD, P], ctx=ctx)
            xt = sb("xt", [P, U, D], ctx=ctx)
            wo = sb("wo", [P, KD, D], ctx=ctx)
            bo_, wn2 = sb("mix_bo", [P, D], ctx=ctx), sb("wn2", [P, D], ctx=ctx)
            rz = sb("rz", [P, 2, 2 * QH], ctx=ctx)
            on = sb("on", [P, 2, D], ctx=ctx)
            onT = sb("onT", [P, 2, KD, P], ctx=ctx)
            hh = sb("hh", [P, 2, D], ctx=ctx)
            sq = sb("sq", [P, D], ctx=ctx)
            hw = sb("hw", [P, 2, D], ctx=ctx)
            ms = sb("ms", [P, 2, 2], ctx=ctx)
            mdg = sb("mdg", [P, NT, 2, H], ctx=ctx)
            es = sb("es", [P, 4, NT, H], ctx=ctx)
            pN = [ps(ctx, f"pN{c}") for c in range(2)]
            pT = [ps(ctx, f"pnT{c}") for c in range(2)]
            pH = [ps(ctx, f"pH{c}") for c in range(2)]
            s_wm = sem("s_wm")
            s_q, s_xt = [sem(f"s_q{c}") for c in range(U)], [sem(f"s_xt{c}") for c in range(U)]
            num_ps, on_sb, onT_ps, onT_sb, h_ps = Count(sem("num_ps")), Count(sem("on_sb"), 3), Count(sem("onT_ps")), Count(sem("onT_sb")), Count(sem("h_ps"))
            h_sb, rms, hw_in, mixed = Count(sem("h_sb"), 2), Count(sem("rms"), 2), Count(sem("hw_in")), Count(sem("mixed"), 3)
            s_mdg, v_al, a_al = sem("s_mdg"), sem("v_al"), sem("a_al")
            al_in, al_ex = sem("al_in"), sem("al_ex")
            with nc.Block() as block:
                @block.sync
                def _(sp):
                    sp.dma_start(wo[:, :, :], a["mix_w_out"].rearrange("(k p) n -> p k n", p=P)).then_inc(s_wm, 16)
                    sp.dma_start(bo_[:, :], a["mix_b_out"].partition_broadcast(P)).then_inc(s_wm, 16)
                    sp.dma_start(wn2[:, :], a["mix_w_norm2"].partition_broadcast(P)).then_inc(s_wm, 16)

                    def load(t, c, r):
                        wait(sp, num_ps, t - U)
                        sp.dma_start(qs[:, c, :, :], qT[:, :, t * P:(t + 1) * P] if isinstance(t, int) else qT[:, :, ds(t * P, P)]).then_inc(s_q[c], 16)
                        wait(sp, mixed, t - U)
                        sp.dma_start(xt[:, c, :], row(a["x"], t)).then_inc(s_xt[c], 16)
                    pipeline(sp, NT, [(0, load)], U, U)

                @block.gpsimd
                def _(pool):
                    for t in range(NT):
                        pool.indirect_dma_start(mdg[:, t, :, :].rearrange("p i h -> p (i h)"), None, md_rows[:, :], at_row(last_row[:, t:t + 1])).then_inc(s_mdg, 16)
                    pool.wait_ge(s_wm, 48)

                    def scaled(t, c, r):
                        wait(pool, h_sb, t)
                        wait(pool, mixed, t - 2)
                        pool.tensor_tensor(hw[:, c % 2, :], hh[:, c % 2, :], wn2[:, :], ALU.mult).then_inc(hw_in.sem, 1)
                    pipeline(pool, NT, [(0, scaled)], U, U)

                @block.tensor
                def _(pe):
                    pe.wait_ge(s_wm, 48)

                    def num(t, c, r):
                        pe.wait_ge(s_q[c], (r + 1) * 16)
                        wait(pe, on_sb, t - 2)
                        for g in range(KD):
                            mm = pe.matmul(pN[c % 2][:, g * (P + 4):(g + 1) * (P + 4)], qs[:, c, g, :], kvd[:, g, :], start=True, stop=True)
                        mm.then_inc(num_ps.sem, 1)

                    def turn(t, c, r):
                        wait(pe, on_sb, t)
                        wait(pe, onT_sb, t - 2)
                        for k in range(KD):
                            mm = pe.transpose(pT[c % 2][:, k * P:(k + 1) * P], on[:, c % 2, k * P:(k + 1) * P], ident)
                        mm.then_inc(onT_ps.sem, 1)

                    def out_proj(t, c, r):
                        wait(pe, onT_sb, t)
                        wait(pe, h_sb, t - 2)
                        for k in range(KD):
                            mm = pe.matmul(pH[c % 2][:, 0:D], onT[:, c % 2, k, :], wo[:, k, :], start=(k == 0), stop=(k == KD - 1))
                        mm.then_inc(h_ps.sem, 1)
                    pipeline(pe, NT, [(0, num), (2, out_proj), (1, turn)], U, U)

                @block.scalar
                def _(act):
                    def copy_t(t, c, r):
                        wait(act, onT_ps, t)
                        wait(act, h_ps, t - 2)
                        act.activation(onT[:, c % 2, :, :], pT[c % 2][:, 0:D].rearrange("p (k f) -> p k f", k=KD), ACT.Copy).then_inc(onT_sb.sem, 1)

                    def rms_of(t, c, r):
                        wait(act, h_sb, t)
                        wait(act, mixed, t - 2)
                        wait(act, rms, t - 1)
                        act.activation(sq[:, :], hh[:, c % 2, :], ACT.Square, accum_out=ms[:, c % 2, 0:1]).then_inc(rms.sem, 1)
                        wait(act, rms, t, 1)
                        act.activation(ms[:, c % 2, 1:2], ms[:, c % 2, 0:1], ACT.Sqrt, scale=1.0 / D, bias=eps[:, 1:2]).then_inc(rms.sem, 1)
                    pipeline(act, NT, [(1, rms_of), (0, copy_t)], U, U)
                    act.wait_ge(al_in, 1)
                    act.activation(es[:, 2:4, :, :], es[:, 2:4, :, :], ACT.Exp).then_inc(al_ex, 1)

                @block.vector
                def _(dve):
                    dve.wait_ge(s_wm, 48)

                    def divide(t, c, r):
                        wait(dve, num_ps, t)
                        wait(dve, onT_ps, t - 2)
                        both = pN[c % 2][:, 0:KD * (P + 4)].rearrange("p (g n) -> p g n", g=KD)
                        z = rz[:, c % 2, 0:QH].rearrange("p (g b) -> p g b", g=KD)
                        dve.tensor_scalar(z, both[:, :, P:P + 4], ATT_EPS, None, ALU.add).then_inc(on_sb.sem, 1)
                        wait(dve, on_sb, t, 1)
                        dve.reciprocal(rz[:, c % 2, QH:2 * QH], rz[:, c % 2, 0:QH]).then_inc(on_sb.sem, 1)
                        wait(dve, on_sb, t, 2)
                        for g in range(KD):
                            ins = dve.tensor_tensor(on[:, c % 2, g * P:(g + 1) * P].rearrange("p (b m) -> p b m", m=HD), both[:, g, 0:P].rearrange("p (b m) -> p b m", m=HD),
                                                    rz[:, c % 2, QH + g * 4:QH + g * 4 + 4].unsqueeze(2).to_broadcast([P, 4, HD]), ALU.mult)
                        ins.then_inc(on_sb.sem, 1)

                    def residual(t, c, r):
                        wait(dve, h_ps, t)
                        wait(dve, mixed, t - 2)
                        wait(dve, hw_in, t - 2)
                        wait(dve, rms, t - 2)
                        dve.tensor_tensor(hh[:, c % 2, :], pH[c % 2][:, 0:D], tile(xna, t, 0, D), ALU.add).then_inc(h_sb.sem, 1)
                        wait(dve, h_sb, t, 1)
                        dve.tensor_tensor(hh[:, c % 2, :], hh[:, c % 2, :], bo_[:, :], ALU.add).then_inc(h_sb.sem, 1)

                    def mixed_of(t, c, r):
                        wait(dve, rms, t)
                        dve.reciprocal(ms[:, c % 2, 1:2], ms[:, c % 2, 1:2]).then_inc(mixed.sem, 1)
                        wait(dve, mixed, t, 1)
                        wait(dve, hw_in, t)
                        dve.scalar_tensor_tensor(out=hw[:, c % 2, :], in0=hw[:, c % 2, :], scalar=ms[:, c % 2, 1:2], in1=hh[:, c % 2, :], op0=ALU.mult, op1=ALU.add).then_inc(mixed.sem, 1)
                        wait(dve, mixed, t, 2)
                        dve.wait_ge(s_xt[c], (r + 1) * 16)
                        dve.tensor_tensor(tile(x2, t, 0, D), hw[:, c % 2, :], xt[:, c, :], ALU.add).then_inc(mixed.sem, 1)
                    pipeline(dve, NT, [(3, mixed_of), (2, residual), (0, divide)], U, U)

                    line = Line(dve, v_al)
                    dve.wait_ge(s_mdg, 16 * NT)
                    line.do(dve.tensor_tensor(es[:, 0, :, :], xna[:, :, AS:AS + H], ad[:, :, :], ALU.add))
                    line.do(dve.scalar_tensor_tensor(out=es[:, 0, :, :], in0=es[:, 0, :, :], scalar=0.2, in1=es[:, 0, :, :], op0=ALU.mult, op1=ALU.max))
                    line.do(dve.tensor_tensor(es[:, 1, :, :], es[:, 0, :, :], mdg[:, :, 0, :], ALU.max))
                    dve.tensor_tensor(es[:, 2, :, :], mdg[:, :, 0, :], es[:, 1, :, :], ALU.subtract)
                    dve.tensor_tensor(es[:, 3, :, :], es[:, 0, :, :], es[:, 1, :, :], ALU.subtract).then_inc(al_in, 1)
                    dve.wait_ge(al_ex, 1)
                    line.do(dve.tensor_tensor(es[:, 0, :, :], es[:, 2, :, :], mdg[:, :, 1, :], ALU.mult))
                    line.do(dve.tensor_tensor(es[:, 0, :, :], es[:, 0, :, :], es[:, 3, :, :], ALU.add))
                    line.do(dve.reciprocal(es[:, 1, :, :], es[:, 0, :, :]))
                    line.do(dve.tensor_tensor(es[:, 1, :, :], es[:, 1, :, :], gw[:, :].unsqueeze(1).to_broadcast([P, NT, H]), ALU.mult))
                    for i in range(2):
                        line.do(dve.tensor_tensor(al[:, i, :, :], es[:, 1, :, :], es[:, 2 + i, :, :], ALU.mult))

        with ExitStack() as ctx:
            lr = sb("lr", [P, 2], U32, ctx)
            AG = sb("AG", [P, 2, H, D], ctx=ctx)
            own = sb("own", [P, 2, H, D], ctx=ctx)
            aT = sb("aT", [P, 2, H * KD, P], ctx=ctx)
            bg = sb("bg", [P, H, D], ctx=ctx)
            gwb = sb("gwb", [P, D], ctx=ctx)
            WoT = sb("WoT", [P, KD, D], ctx=ctx)
            gam = sb("gam", [P, 2, KD], ctx=ctx)
            betaR = sb("betaR", [P, KD, P], ctx=ctx)
            bob = sb("bob", [P, D], ctx=ctx)
            gtw = sb("gtw", [P, KD, E], ctx=ctx)
            gtb = sb("gtb", [P, E], ctx=ctx)
            res = sb("res", [P, 2, D], ctx=ctx)
            st = sb("st", [P, 2, 2, 8], ctx=ctx)
            nT = sb("nT", [P, 2, KD, P], ctx=ctx)
            yt = sb("yt", [P, 2, D], ctx=ctx)
            yT = sb("yT", [P, 2, KD, P], ctx=ctx)
            pA = [ps(ctx, f"pa{i}") for i in range(4)]
            pW, pG, pX, pY = ps(ctx, "pW_"), ps(ctx, "pG_"), ps(ctx, "pX_"), ps(ctx, "pY_")
            s_cw, v_cl, v_cw, cw_ps = sem("s_cw"), sem("v_cl"), sem("v_cw"), sem("cw_ps")
            s_AG = [sem(f"s_AG{c}") for c in range(2)]
            lr_in, own_in, agg_in, aT_ps = Count(sem("lr_in")), Count(sem("own_in")), Count(sem("agg_in")), Count(sem("aT_ps"), 4)
            aT_a, aT_v, w_ps = Count(sem("aT_a"), 2), Count(sem("aT_v"), 2), Count(sem("w_ps"))
            res_in, res_sd, nT_ps, nT_sb, g_ps = Count(sem("res_in"), 6), Count(sem("res_sd")), Count(sem("nT_ps")), Count(sem("nT_sb")), Count(sem("g_ps"))
            y_in, y_sd, yT_ps, yT_sb, lg_ps, lg_in = Count(sem("y_in"), 7), Count(sem("y_sd")), Count(sem("yT_ps")), Count(sem("yT_sb")), Count(sem("lg_ps")), Count(sem("lg_in"))
            with nc.Block() as block:
                @block.sync
                def _(sp):
                    sp.dma_start(bg[:, :, :], a["bias_gat"].partition_broadcast(P)).then_inc(s_cw, 16)
                    sp.dma_start(WoT[:, :, :], a["WoT"].rearrange("(k p) n -> p k n", p=P)).then_inc(s_cw, 16)
                    sp.dma_start(gam[:, 0, :], a["ln_gamma"][:, :]).then_inc(s_cw, 16)
                    sp.dma_start(gam[:, 1, :], a["ln_beta"][:, :]).then_inc(s_cw, 16)
                    sp.dma_start(bob[:, :], a["bo"].partition_broadcast(P)).then_inc(s_cw, 16)
                    sp.dma_start(gtw[:, :, :], a["ffn_gate_w"].rearrange("(k p) n -> p k n", p=P)).then_inc(s_cw, 16)
                    sp.dma_start(gtb[:, :], a["ffn_gate_b"].partition_broadcast(P)).then_inc(s_cw, 16)

                @block.gpsimd
                def _(pool):
                    def gather(t, c, r):
                        wait(pool, agg_in, t - 2)
                        pool.sem_inc(s_gate, 1)
                        pool.tensor_copy(lr[:, c:c + 1], col(last_row, t)).then_inc(lr_in.sem, 1)
                        wait(pool, lr_in, t)
                        pool.sem_inc(s_gate, 1)
                        pool.indirect_dma_start(AG[:, c, :, :].rearrange("p h f -> p (h f)"), None,
                                                agg_rows.rearrange("s (d h) f -> (s d) (h f)", h=H), at_row(lr[:, c:c + 1])).then_inc(s_AG[c], 16)
                    pipeline(pool, NT, [(0, gather)])

                @block.scalar
                def _(act):
                    def own_rows(t, c, r):
                        wait(act, agg_in, t - 2)
                        wait(act, aT_ps, t - 2)
                        act.sem_inc(s_gate, 1)
                        for h in range(H):
                            ins = act.activation(own[:, c, h, :], tile(xna, t, 0, D), ACT.Copy, scale=al[:, 1, t, h:h + 1] if isinstance(t, int) else al[:, 1, ds(t, 1), h:h + 1].rearrange("p t h -> p (t h)"))
                        ins.then_inc(own_in.sem, 1)

                    def copy_a(t, c, r):
                        for i in range(2):
                            wait(act, aT_ps, t, 2 * i + 1)
                            wait(act, w_ps, t - 2)
                            act.activation(aT[:, c, 8 * i:8 * i + 4, :], pA[2 * i][:, :].rearrange("p (k f) -> p k f", k=4), ACT.Copy).then_inc(aT_a.sem, 1)

                    def res_std(t, c, r):
                        wait(act, res_in, t, 4)
                        act.activation(st[:, c, 0, 7:8], st[:, c, 0, 7:8], ACT.Sqrt, bias=eps[:, 0:1]).then_inc(res_sd.sem, 1)

                    def copy_n(t, c, r):
                        wait(act, nT_ps, t)
                        wait(act, g_ps, t - 2)
                        act.activation(nT[:, c, :, :], pX[:, 0:D].rearrange("p (k f) -> p k f", k=KD), ACT.Copy).then_inc(nT_sb.sem, 1)

                    def y_std(t, c, r):
                        wait(act, y_in, t, 4)
                        act.activation(st[:, c, 1, 7:8], st[:, c, 1, 7:8], ACT.Sqrt, bias=eps[:, 0:1]).then_inc(y_sd.sem, 1)

                    def copy_y(t, c, r):
                        wait(act, yT_ps, t)
                        wait(act, lg_ps, t - 2)
                        act.activation(yT[:, c, :, :], pY[:, 0:D].rearrange("p (k f) -> p k f", k=KD), ACT.Copy).then_inc(yT_sb.sem, 1)
                    pipeline(act, NT, [(5, y_std), (2, copy_a), (4, copy_n), (0, own_rows), (3, res_std), (5, copy_y)])

                @block.tensor
                def _(pe):
                    pe.wait_ge(v_cw, 1)
                    for k in range(KD):
                        mm = pe.matmul(pG[:, 0:D], betaR[:, k, :], WoT[:, k, :], start=(k == 0), stop=(k == KD - 1))
                    mm.then_inc(cw_ps, 1)
                    pe.wait_ge(v_cw, 2)

                    def turn_a(t, c, r):
                        wait(pe, agg_in, t)
                        for i in range(4):
                            wait(pe, (aT_a, aT_v)[i % 2], t - 1, i // 2 + 1)
                            for k in range(4):
                                n = 4 * i + k
                                mm = pe.transpose(pA[i][:, k * P:(k + 1) * P], own[:, c, n // KD, (n % KD) * P:(n % KD + 1) * P], ident)
                            mm.then_inc(aT_ps.sem, 1)

                    def weigh(t, c, r):
                        wait(pe, res_in, t - 1, 1)
                        for i in range(4):
                            wait(pe, (aT_a, aT_v)[i % 2], t, i // 2 + 1)
                            for k in range(4):
                                n = 4 * i + k
                                mm = pe.matmul(pW[:, 0:D], aT[:, c, n, :], W[:, n % KD, n // KD, :], start=(n == 0), stop=(n == H * KD - 1))
                        mm.then_inc(w_ps.sem, 1)

                    def turn_n(t, c, r):
                        wait(pe, res_in, t)
                        wait(pe, nT_sb, t - 1)
                        for k in range(KD):
                            mm = pe.transpose(pX[:, k * P:(k + 1) * P], res[:, c, k * P:(k + 1) * P], ident)
                        mm.then_inc(nT_ps.sem, 1)

                    def project(t, c, r):
                        wait(pe, nT_sb, t)
                        wait(pe, y_in, t - 1, 1)
                        for k in range(KD):
                            mm = pe.matmul(pG[:, 0:D], nT[:, c, k, :], WoT[:, k, :], start=(k == 0), stop=(k == KD - 1))
                        mm.then_inc(g_ps.sem, 1)

                    def turn_y(t, c, r):
                        wait(pe, y_in, t)
                        wait(pe, lg_in, t - 1)
                        for k in range(KD):
                            mm = pe.transpose(pY[:, k * P:(k + 1) * P], yt[:, c, k * P:(k + 1) * P], ident)
                        mm.then_inc(yT_ps.sem, 1)

                    def gate(t, c, r):
                        wait(pe, yT_sb, t)
                        for k in range(KD):
                            mm = pe.matmul(pY[:, D:D + E], yT[:, c, k, :], gtw[:, k, :], start=(k == 0), stop=(k == KD - 1))
                        mm.then_inc(lg_ps.sem, 1)
                    pipeline(pe, NT, [(2, turn_a), (4, turn_n), (6, gate), (3, weigh), (4, project), (5, turn_y)])

                @block.vector
                def _(dve):
                    line = Line(dve, v_cl)
                    dve.wait_ge(s_cw, 16 * 7)
                    line.do(dve.tensor_scalar(gwb[:, :], bg[:, 0, :], gw[:, 0:1], None, ALU.mult))
                    for h in range(1, H):
                        line.do(dve.scalar_tensor_tensor(out=gwb[:, :], in0=bg[:, h, :], scalar=gw[:, h:h + 1], in1=gwb[:, :], op0=ALU.mult, op1=ALU.add))
                    for k in range(KD):
                        ins = dve.tensor_scalar(betaR[:, k, :], ones, gam[:, 1, k:k + 1], None, ALU.mult)
                    ins.then_inc(v_cw, 1)
                    dve.wait_ge(cw_ps, 1)
                    line.do(dve.tensor_tensor(bob[:, :], bob[:, :], pG[:, 0:D], ALU.add))
                    for k in range(KD):
                        ins = dve.tensor_scalar(WoT[:, k, :], WoT[:, k, :], gam[:, 0, k:k + 1], None, ALU.mult)
                    ins.then_inc(v_cw, 1)

                    def neighbours(t, c, r):
                        dve.wait_ge(s_AG[c], (r + 1) * 16)
                        wait(dve, own_in, t)
                        for h in range(H):
                            ins = dve.scalar_tensor_tensor(out=own[:, c, h, :], in0=AG[:, c, h, :], scalar=al[:, 0, t, h:h + 1] if isinstance(t, int) else al[:, 0, ds(t, 1), h:h + 1].rearrange("p t h -> p (t h)"),
                                                           in1=own[:, c, h, :], op0=ALU.mult, op1=ALU.add)
                        ins.then_inc(agg_in.sem, 1)

                    def copy_a(t, c, r):
                        for i in range(2):
                            wait(dve, aT_ps, t, 2 * i + 2)
                            wait(dve, w_ps, t - 2)
                            dve.tensor_copy(aT[:, c, 8 * i + 4:8 * i + 8, :], pA[2 * i + 1][:, :].rearrange("p (k f) -> p k f", k=4)).then_inc(aT_v.sem, 1)

                    def layer_norm(buf, c, i, count, t, k, sd):
                        s_ = st[:, c, i, :]
                        dve.bn_stats(s_[:, 0:6], buf).then_inc(count.sem, 1)
                        wait(dve, count, t, k + 1)
                        dve.sem_inc(s_gate, 1)
                        dve.bn_aggr(s_[:, 6:8], s_[:, 0:6]).then_inc(count.sem, 1)
                        wait(dve, sd, t)
                        dve.reciprocal(s_[:, 7:8], s_[:, 7:8]).then_inc(count.sem, 1)
                        wait(dve, count, t, k + 3)
                        dve.tensor_scalar(buf, buf, s_[:, 6:7], s_[:, 7:8], ALU.subtract, ALU.mult).then_inc(count.sem, 1)

                    def residual(t, c, r):
                        wait(dve, w_ps, t)
                        wait(dve, nT_ps, t - 2)
                        dve.tensor_tensor(res[:, c, :], pW[:, 0:D], tile(xna, t, 0, D), ALU.add).then_inc(res_in.sem, 1)
                        wait(dve, res_in, t, 1)
                        dve.tensor_tensor(res[:, c, :], res[:, c, :], gwb[:, :], ALU.add).then_inc(res_in.sem, 1)
                        wait(dve, res_in, t, 2)
                        layer_norm(res[:, c, :], c, 0, res_in, t, 2, res_sd)

                    def node_out(t, c, r):
                        wait(dve, g_ps, t)
                        dve.tensor_tensor(tile(x2, t, 0, D), pG[:, 0:D], tile(x2, t, 0, D), ALU.add).then_inc(y_in.sem, 1)
                        wait(dve, y_in, t, 1)
                        wait(dve, yT_ps, t - 2)
                        dve.tensor_tensor(tile(x2, t, 0, D), tile(x2, t, 0, D), bob[:, :], ALU.add).then_inc(y_in.sem, 1)
                        wait(dve, y_in, t, 2)
                        s_ = st[:, c, 1, :]
                        dve.sem_inc(s_gate, 1)
                        dve.bn_stats(s_[:, 0:6], tile(x2, t, 0, D)).then_inc(y_in.sem, 1)
                        wait(dve, y_in, t, 3)
                        dve.sem_inc(s_gate, 1)
                        dve.bn_aggr(s_[:, 6:8], s_[:, 0:6]).then_inc(y_in.sem, 1)
                        wait(dve, y_sd, t)
                        dve.reciprocal(s_[:, 7:8], s_[:, 7:8]).then_inc(y_in.sem, 1)
                        wait(dve, y_in, t, 5)
                        dve.tensor_scalar(tile(y_all, t, 0, D), tile(x2, t, 0, D), s_[:, 6:7], s_[:, 7:8], ALU.subtract, ALU.mult).then_inc(y_in.sem, 1)
                        wait(dve, y_in, t, 6)
                        dve.tensor_scalar(yt[:, c, :], tile(y_all, t, 0, D), 0.0, None, ALU.add).then_inc(y_in.sem, 1)

                    def logits(t, c, r):
                        wait(dve, lg_ps, t)
                        dve.tensor_tensor(tile(lg, t, 0, E), pY[:, D:D + E], gtb[:, :], ALU.add).then_inc(lg_in.sem, 1)
                    pipeline(dve, NT, [(5, node_out), (2, copy_a), (6, logits), (1, neighbours), (3, residual)])

        slot = sb("slot", [P, 2, NT], U32)
        wts = sb("wts", [P, 2, NT])
        expert_of = sb("expert_of", [1, TILES], I32)
        with ExitStack() as ctx:
            iota = iota16.unsqueeze(1).to_broadcast([P, NT, E])
            O = sb("O", [P, 3, NT, E], ctx=ctx)
            T = sb("T", [P, 2, NT, E], ctx=ctx)
            m = sb("m", [P, 6, NT], ctx=ctx)
            cn = sb("cn", [P, 2, NT, E], ctx=ctx)
            te = sb("te", [P, 4, E], ctx=ctx)
            ti = sb("ti", [P, E], I32, ctx)
            tj = sb("tj", [1, TILES, E + 1], ctx=ctx)
            jn = sb("jn", [1, TILES], ctx=ctx)
            pR, pC = ps(ctx, "pR"), ps(ctx, "pC")
            s_jn, v_rt, a_rt, rt_ps, slots_in, s_sc = sem("s_jn"), sem("v_rt"), sem("a_rt"), sem("rt_ps"), sem("slots_in"), sem("s_sc")
            m_in, o_in = sem("m_in"), sem("o_in")
            with nc.Block() as block:
                @block.sync
                def _(sp):
                    sp.dma_start(jn[:, :], a["tile_no"][:, :]).then_inc(s_jn, 16)

                @block.vector
                def _(dve):
                    line = Line(dve, v_rt)
                    left = lg
                    for k in range(2):
                        line.do(dve.tensor_reduce(m[:, k, :], left[:, :, :], AX.X, ALU.max))
                        line.do(dve.tensor_tensor(T[:, 0, :, :], left[:, :, :], m[:, k, :].unsqueeze(2).to_broadcast([P, NT, E]), ALU.not_equal))
                        line.do(dve.scalar_tensor_tensor(out=T[:, 0, :, :], in0=T[:, 0, :, :], scalar=float(E), in1=iota, op0=ALU.mult, op1=ALU.add))
                        line.do(dve.tensor_reduce(m[:, 2, :], T[:, 0, :, :], AX.X, ALU.min))
                        line.do(dve.tensor_tensor(O[:, k, :, :], iota, m[:, 2, :].unsqueeze(2).to_broadcast([P, NT, E]), ALU.is_equal))
                        if k == 0:
                            line.do(dve.scalar_tensor_tensor(out=T[:, 1, :, :], in0=O[:, 0, :, :], scalar=-3e38, in1=lg[:, :, :], op0=ALU.mult, op1=ALU.add))
                            left = T[:, 1, :, :]
                    dve.tensor_tensor(m[:, 3, :], m[:, 1, :], m[:, 0, :], ALU.subtract).then_inc(m_in, 1)
                    dve.tensor_tensor(O[:, 2, :, :], O[:, 0, :, :], O[:, 1, :, :], ALU.add).then_inc(o_in, 1)
                    dve.wait_ge(a_rt, 1)
                    line.do(dve.tensor_scalar(m[:, 4, :], m[:, 3, :], 1.0, None, ALU.add))
                    line.do(dve.reciprocal(wts[:, 0, :], m[:, 4, :]))
                    line.do(dve.tensor_tensor(wts[:, 1, :], wts[:, 0, :], m[:, 3, :], ALU.mult))
                    dve.wait_ge(rt_ps, 2)
                    line.do(dve.tensor_copy(cn[:, 0, :, :], pC[:, 0:NT * E].rearrange("p (t e) -> p t e", e=E)))
                    a_, b_, d_ = 0, 1, 1
                    while d_ < NT:
                        dve.tensor_copy(cn[:, b_, 0:d_, :], cn[:, a_, 0:d_, :])
                        line.do(dve.tensor_tensor(cn[:, b_, d_:, :], cn[:, a_, d_:, :], cn[:, a_, 0:NT - d_, :], ALU.add))
                        a_, b_, d_ = b_, a_, 2 * d_
                    line.do(dve.tensor_scalar(ti[:, :], cn[:, a_, NT - 1, :], float(P - 1), None, ALU.add))
                    line.do(dve.tensor_scalar(ti[:, :], ti[:, :], 7, None, ALU.arith_shift_right))
                    line.do(dve.tensor_copy(te[:, 0, :], ti[:, :]))
                    line.do(dve.tensor_tensor_scan(te[:, 1, :], ones[:, 0:E], te[:, 0, :], 0.0, ALU.mult, ALU.add))
                    line.do(dve.tensor_tensor(te[:, 2, :], te[:, 1, :], te[:, 0, :], ALU.subtract))
                    line.do(dve.tensor_scalar(te[:, 2, :], te[:, 2, :], float(P), None, ALU.mult))
                    line.do(dve.tensor_tensor(T[:, 0, 1:, :], cn[:, a_, 0:NT - 1, :], pR[:, E:NT * E].rearrange("p (t e) -> p t e", e=E), ALU.add))
                    line.do(dve.tensor_copy(T[:, 0, 0:1, :], pR[:, 0:E].rearrange("p (t e) -> p t e", e=E)))
                    line.do(dve.tensor_tensor(T[:, 0, :, :], T[:, 0, :, :], te[:, 2, :].unsqueeze(1).to_broadcast([P, NT, E]), ALU.add))
                    for k in range(2):
                        line.do(dve.tensor_tensor(T[:, 1, :, :], T[:, 0, :, :], O[:, k, :, :], ALU.mult))
                        line.do(dve.tensor_reduce(m[:, 5, :], T[:, 1, :, :], AX.X, ALU.add))
                        line.do(dve.tensor_copy(slot[:, k, :], m[:, 5, :]))
                    dve.sem_inc(slots_in, 1)
                    dve.wait_ge(s_jn, 16)
                    line.do(dve.tensor_tensor(tj[:, :, 0:E], te[0:1, 1, :].unsqueeze(1).to_broadcast([1, TILES, E]), jn[:, :].unsqueeze(2).to_broadcast([1, TILES, E]), ALU.is_le))
                    line.do(dve.tensor_reduce(tj[:, :, E], tj[:, :, 0:E], AX.X, ALU.add))
                    line.do(dve.tensor_scalar(expert_of[:, :], tj[:, :, E], float(E - 1), None, ALU.min))

                @block.scalar
                def _(act):
                    act.wait_ge(m_in, 1)
                    act.activation(m[:, 3, :], m[:, 3, :], ACT.Exp).then_inc(a_rt, 1)

                @block.tensor
                def _(pe):
                    pe.wait_ge(o_in, 1)
                    pe.matmul(pR[:, 0:NT * E], tri, O[:, 2, :, :].rearrange("p t e -> p (t e)"), start=True, stop=True).then_inc(rt_ps, 1)
                    pe.matmul(pC[:, 0:NT * E], ones, O[:, 2, :, :].rearrange("p t e -> p (t e)"), start=True, stop=True).then_inc(rt_ps, 1)

                @block.gpsimd
                def _(pool):
                    pool.wait_ge(slots_in, 1)
                    for t in range(NT):
                        for k in range(2):
                            pool.indirect_dma_start(xs_rows[:, :], at_row(slot[:, k, t:t + 1]), y_all[:, t, :], None).then_inc(s_sc, 16)
                    pool.wait_ge(s_sc, 2 * 16 * NT)

        with ExitStack() as ctx:
            U = 6
            S3 = 3
            xe = sb("xe", [P, S3, D], ctx=ctx)
            xeT = sb("xeT", [P, 2, KD, P], ctx=ctx)
            w1 = sb("w1", [P, S3, KD, F], ctx=ctx)
            w2 = sb("w2", [P, S3, FK, D], ctx=ctx)
            b1 = sb("b1", [P, S3, FK], ctx=ctx)
            b2 = sb("b2", [P, S3, D], ctx=ctx)
            hT = sb("hT", [P, 2, FK, P], ctx=ctx)
            ye = sb("ye", [P, 2, D], ctx=ctx)
            pX = [ps(ctx, f"pXe{c}") for c in range(2)]
            pH = [ps(ctx, f"pHe{c}") for c in range(2)]
            pY = [ps(ctx, f"pYe{c}") for c in range(2)]
            s_we = [sem(f"s_we{c}") for c in range(S3)]
            s_xe = [sem(f"s_xe{c}") for c in range(S3)]
            s_ye = [sem(f"s_ye{c}") for c in range(2)]
            xeT_ps, xeT_sb, he_ps, he_sb, ye_ps, ye_sb = (Count(sem(n)) for n in ("xeT_ps", "xeT_sb", "he_ps", "he_sb", "ye_ps", "ye_sb"))

            def nth(c, r, slots):
                return r * (U // slots) + c // slots

            with nc.Block() as block:
                @block.sync
                def _(sp):
                    def load(j, c, r):
                        e = sp.value_load(expert_of[0:1, j:j + 1] if isinstance(j, int) else expert_of[0:1, ds(j, 1)], min_val=0, max_val=E - 1)
                        wait(sp, ye_ps, j - S3)
                        sp.dma_start(xe[:, c % S3, :], row(xs_rows, j)).then_inc(s_xe[c % S3], 16)
                        sp.dma_start(w1[:, c % S3, :, :], a["ffn_w1"][ds(e, 1), :, :].rearrange("e (k p) f -> p (e k) f", p=P)).then_inc(s_we[c % S3], 16)
                        sp.dma_start(b1[:, c % S3, :], a["ffn_b1"][ds(e, 1), :, :].rearrange("e p f -> p (e f)")).then_inc(s_we[c % S3], 16)
                        sp.dma_start(w2[:, c % S3, :, :], a["ffn_w2"][ds(e, 1), :, :].rearrange("e (k p) f -> p (e k) f", p=P)).then_inc(s_we[c % S3], 16)
                        wait(sp, ye_sb, j - S3)
                        sp.dma_start(b2[:, c % S3, :], a["ffn_b2"][ds(e, 1), :].rearrange("e d -> (e d)").partition_broadcast(P)).then_inc(s_we[c % S3], 16)
                    pipeline(sp, TILES, [(0, load)], U, S3)

                @block.tensor
                def _(pe):
                    def turn(j, c, r):
                        pe.wait_ge(s_xe[c % S3], (nth(c, r, S3) + 1) * 16)
                        wait(pe, xeT_sb, j - 2)
                        for k in range(KD):
                            mm = pe.transpose(pX[c % 2][:, k * P:(k + 1) * P], xe[:, c % S3, k * P:(k + 1) * P], ident)
                        mm.then_inc(xeT_ps.sem, 1)

                    def hidden(j, c, r):
                        pe.wait_ge(s_we[c % S3], (nth(c, r, S3) + 1) * 64)
                        wait(pe, xeT_sb, j)
                        wait(pe, he_sb, j - 2)
                        for f in range(FK):
                            for k in range(KD):
                                mm = pe.matmul(pH[c % 2][:, f * P:(f + 1) * P], w1[:, c % S3, k, f * P:(f + 1) * P], xeT[:, c % 2, k, :], start=(k == 0), stop=(k == KD - 1))
                        mm.then_inc(he_ps.sem, 1)

                    def output(j, c, r):
                        wait(pe, he_sb, j)
                        wait(pe, ye_sb, j - 2)
                        for f in range(FK):
                            mm = pe.matmul(pY[c % 2][:, 0:D], hT[:, c % 2, f, :], w2[:, c % S3, f, :], start=(f == 0), stop=(f == FK - 1))
                        mm.then_inc(ye_ps.sem, 1)
                    pipeline(pe, TILES, [(0, turn), (1, output), (0, hidden)], U, S3)

                @block.scalar
                def _(act):
                    def relu(j, c, r):
                        wait(act, he_ps, j)
                        wait(act, ye_ps, j - 2)
                        for f in range(FK):
                            ins = act.activation(hT[:, c % 2, f, :], pH[c % 2][:, f * P:(f + 1) * P], ACT.Relu, bias=b1[:, c % S3, f:f + 1])
                        ins.then_inc(he_sb.sem, 1)
                    pipeline(act, TILES, [(0, relu)], U, S3)

                @block.vector
                def _(dve):
                    def copy_x(j, c, r):
                        wait(dve, xeT_ps, j)
                        wait(dve, he_ps, j - 2)
                        dve.tensor_copy(xeT[:, c % 2, :, :], pX[c % 2][:, 0:D].rearrange("p (k f) -> p k f", k=KD)).then_inc(xeT_sb.sem, 1)

                    def add_b2(j, c, r):
                        wait(dve, ye_ps, j)
                        if not isinstance(j, int) or j >= 2:
                            dve.wait_ge(s_ye[c % 2], nth(c, r, 2) * 16)
                        dve.tensor_tensor(ye[:, c % 2, :], pY[c % 2][:, 0:D], b2[:, c % S3, :], ALU.add).then_inc(ye_sb.sem, 1)
                    pipeline(dve, TILES, [(0, copy_x), (1, add_b2)], U, S3)

                @block.gpsimd
                def _(pool):
                    def store(j, c, r):
                        wait(pool, ye_sb, j)
                        pool.sem_inc(s_gate, 1)
                        pool.dma_start(row(ys_rows, j), ye[:, c % 2, :]).then_inc(s_ye[c % 2], 16)
                    pipeline(pool, TILES, [(0, store)], U, S3)
                    for c in range(2):
                        pool.wait_ge(s_ye[c], 16 * (TILES // 2))

        with ExitStack() as ctx:
            sl = sb("sl", [P, 2, 2], U32, ctx)
            g = sb("g", [P, 2, 2, D], ctx=ctx)
            v = sb("v", [P, 2, D], ctx=ctx)
            o = sb("o", [P, 2, D], ctx=ctx)
            sf = sb("sf", [P, 2, 8], ctx=ctx)
            gb = sb("gb", [P, 2, D], ctx=ctx)
            s_gb, s_g, s_out = sem("s_gb"), [sem(f"s_g{c}") for c in range(2)], [sem(f"s_out{c}") for c in range(2)]
            sl_in, v_in, v_sd, o_in = Count(sem("sl_in")), Count(sem("v_in"), 6), Count(sem("v_sd")), Count(sem("o_fin"), 2)
            with nc.Block() as block:
                @block.gpsimd
                def _(pool):
                    def gather(t, c, r):
                        wait(pool, v_in, t - 2)
                        pool.sem_inc(s_gate, 1)
                        pool.tensor_copy(sl[:, c, :], slot[:, :, t] if isinstance(t, int) else slot[:, :, ds(t, 1)].rearrange("p k t -> p (k t)")).then_inc(sl_in.sem, 1)
                        wait(pool, sl_in, t)
                        pool.sem_inc(s_gate, 1)
                        for k in range(2):
                            pool.indirect_dma_start(g[:, c, k, :], None, ys_rows[:, :], at_row(sl[:, c, k:k + 1])).then_inc(s_g[c], 16)
                    pipeline(pool, NT, [(0, gather)])

                @block.scalar
                def _(act):
                    def std(t, c, r):
                        wait(act, v_in, t, 4)
                        act.activation(sf[:, c, 7:8], sf[:, c, 7:8], ACT.Sqrt, bias=eps[:, 0:1]).then_inc(v_sd.sem, 1)
                    pipeline(act, NT, [(0, std)])

                @block.vector
                def _(dve):
                    dve.wait_ge(s_gb, 32)

                    def weighted(t, c, r):
                        dve.wait_ge(s_g[c], (r + 1) * 32)
                        wait(dve, o_in, t - 2)
                        for k in range(2):
                            w = wts[:, k, t:t + 1] if isinstance(t, int) else wts[:, k, ds(t, 1)]
                            dve.scalar_tensor_tensor(out=v[:, c, :], in0=g[:, c, k, :], scalar=w, in1=v[:, c, :] if k else tile(y_all, t, 0, D), op0=ALU.mult, op1=ALU.add).then_inc(v_in.sem, 1)
                            wait(dve, v_in, t, k + 1)
                        dve.bn_stats(sf[:, c, 0:6], v[:, c, :]).then_inc(v_in.sem, 1)
                        wait(dve, v_in, t, 3)
                        dve.sem_inc(s_gate, 1)
                        dve.bn_aggr(sf[:, c, 6:8], sf[:, c, 0:6]).then_inc(v_in.sem, 1)

                    def finish(t, c, r):
                        wait(dve, v_sd, t)
                        dve.reciprocal(sf[:, c, 7:8], sf[:, c, 7:8]).then_inc(v_in.sem, 1)
                        wait(dve, v_in, t, 5)
                        dve.tensor_scalar(v[:, c, :], v[:, c, :], sf[:, c, 6:7], sf[:, c, 7:8], ALU.subtract, ALU.mult).then_inc(v_in.sem, 1)
                        wait(dve, v_in, t)
                        if not isinstance(r, int) or r > 0:
                            dve.wait_ge(s_out[c], r * 16)
                        dve.tensor_tensor(o[:, c, :], v[:, c, :], gb[:, 0, :], ALU.mult).then_inc(o_in.sem, 1)
                        wait(dve, o_in, t, 1)
                        dve.tensor_tensor(o[:, c, :], o[:, c, :], tile(x2, t, 0, D), ALU.add).then_inc(o_in.sem, 1)
                    dve.tensor_tensor(x2[:, :, :], x2[:, :, :], gb[:, 1, :].unsqueeze(1).to_broadcast([P, NT, D]), ALU.add).then_inc(s_gate, 1)
                    dve.drain()
                    pipeline(dve, NT, [(0, weighted), (0, finish)])

                @block.sync
                def _(sp):
                    sp.dma_start(gb[:, 0, :], a["ffn_gamma"].partition_broadcast(P)).then_inc(s_gb, 16)
                    sp.dma_start(gb[:, 1, :], a["ffn_beta"].partition_broadcast(P)).then_inc(s_gb, 16)

                    def store(t, c, r):
                        wait(sp, o_in, t)
                        sp.dma_start(row(out, t), o[:, c, :]).then_inc(s_out[c], 16)
                    pipeline(sp, NT, [(0, store)])
                    sp.wait_ge(s_out[0], 16 * 13)
                    sp.wait_ge(s_out[1], 16 * 12)


_PAD_ROWS = ("x",)


def constants():
    import numpy as np
    p = np.arange(P)
    same = (p[:, None] // DW == np.arange(G)[None, :]).repeat(H, axis=1)
    parts = [np.eye(P), p[:, None] < p[None, :], np.ones((P, P)), np.tile(np.arange(16), (P, 1)),
             p[:, None] + P * np.arange(SJ)[None, :], G * np.arange(NT)[None, :] + p[:, None] // DW,
             (p % DW)[:, None], same]
    return np.concatenate([np.asarray(x, np.float32) for x in parts], axis=1)


def lay_out(inputs):
    import numpy as np
    g = {k: np.asarray(v) for k, v in inputs.items()}
    x = np.zeros((NP, D), g["x"].dtype)
    x[:N] = g["x"]
    src = np.zeros((CHUNKS * P,), g["src"].dtype)
    dst = np.full((CHUNKS * P,), DST_PAD, g["dst"].dtype)
    src[:NE], dst[:NE] = g["src"], g["dst"]
    a = {"x": x, "src": src.reshape(CHUNKS, P), "dst": dst.reshape(CHUNKS, P), "cst": constants(),
         "chunk_end": dst[P - 1::P][:CHUNKS - 1].reshape(1, -1), "chunk_no": np.arange(CHUNKS - 1, dtype=np.float32).reshape(1, -1)}
    for k, v in g.items():
        if k.startswith("L0_"):
            a[k.split("_", 2)[2] if k.split("_")[1] == "gnn" else k[3:]] = v
    for k in ("mix_w_norm1", "ln_gamma", "ln_beta"):
        a[k] = a[k].reshape(KD, P).T
    a["ffn_b1"] = a["ffn_b1"].reshape(E, FK, P).transpose(0, 2, 1)
    a["tile_no"] = np.arange(TILES, dtype=np.float32).reshape(1, -1)
    a["WoT"] = a.pop("Wo").T
    return {k: np.ascontiguousarray(v) for k, v in a.items()}


def kernel(**inputs):
    import concourse.bacc as _bacc
    from concourse.bass_utils import run_bass_kernel_spmd as _run
    nc = _bacc.Bacc("TRN2", target_bir_lowering=False, num_devices=1)
    arrays = lay_out(inputs)
    args = {k: nc.dram_tensor("in_" + k, v.shape, mybir.dt.from_np(v.dtype), kind="ExternalInput").ap()
            for k, v in arrays.items()}
    out = nc.dram_tensor("out", (NP, D), F32, kind="ExternalOutput").ap()
    build(nc, args, out, DEBUG)
    r = _run(nc, [{"in_" + k: v for k, v in arrays.items()}], core_ids=[0])
    return r.results[0]["out"][:N]


DEBUG = False
```

```python
from contextlib import ExitStack

import concourse.bass as bass
from concourse import mybir

P = 128
N, D, H = 3125, 256, 8
KD = D // P
NT = -(-N // P)
NP = NT * P
LAST = N - (NT - 1) * P
NE = 50000
CHUNKS = -(-NE // P)
DW = P // H
WINDOWS = -(-N // DW)
STEPS = CHUNKS + WINDOWS - 1
G = 8
GROUPS = -(-STEPS // G)
SJ = -(-(GROUPS * G) // P)
SP_ = SJ * P
ONE, AS = D, D + 1
RW = 272
DST_PAD = 4080
BIG = 1e30
QH = 8
HD = D // QH
E, F, FK = 16, 512, 512 // P
TILES = 2 * NP // P + E
SLOTS = TILES * P
LN_EPS, RMS_EPS, ATT_EPS = 1e-5, 1e-6, 1e-6

F32, BF16 = mybir.dt.float32, mybir.dt.bfloat16
I32, U32 = mybir.dt.int32, mybir.dt.uint32
ALU = mybir.AluOpType
ACT = mybir.ActivationFunctionType
AX = mybir.AxisListType
ds = bass.ds


class Count:

    def __init__(self, sem, n=1):
        self.sem, self.n = sem, n

    def at(self, t, k=None):
        return t * self.n + (self.n if k is None else k)


def wait(eng, count, t, k=None):
    v = count.at(t, k)
    if not isinstance(v, int) or v > 0:
        eng.wait_ge(count.sem, v)


def pipeline(eng, n, stages, U=2, extra=2, between=None):
    L = max(lag for lag, _ in stages)
    start = L + extra
    turns = (n - start) // U
    for tau in range(start):
        for lag, stage in stages:
            if 0 <= tau - lag < n:
                t = tau - lag
                stage(t, t % U, t // U)
    if between:
        between()
    with eng.Fori(0, turns) as i:
        for u in range(U):
            for lag, stage in stages:
                t = start + u - lag
                stage(i * U + t, t % U, i + t // U)
    for tau in range(start + turns * U, n + L):
        for lag, stage in stages:
            if 0 <= tau - lag < n:
                t = tau - lag
                stage(t, t % U, t // U)


def tile(T, t, lo, hi):
    return T[:, t, lo:hi] if isinstance(t, int) else T[:, ds(t, 1), lo:hi].rearrange("p t f -> p (t f)")


def col(T, t, n=1):
    return T[:, t * n:t * n + n] if isinstance(t, int) else T[:, ds(t * n, n)]


def row(T, t):
    return T[t * P:(t + 1) * P, :] if isinstance(t, int) else T[ds(t * P, P), :]


def at_row(ap):
    return bass.IndirectOffsetOnAxis(ap=ap, axis=0)


class Line:

    def __init__(self, sem):
        self.sem, self.n = sem, 0

    def on(self, eng):
        self.eng = eng
        return self

    def do(self, ins):
        ins.then_inc(self.sem, 1)
        self.n += 1
        self.eng.wait_ge(self.sem, self.n)


class Loads:

    def __init__(self, sem):
        self.sem, self.n = sem, 0

    def expect(self, n):
        self.n += n

    def wait(self, eng, but=0):
        eng.wait_ge(self.sem, 16 * (self.n - but))


def build(nc, a, out, dbg):
    with ExitStack() as top:
        def dram(name, shape, dt=F32):
            return nc.dram_tensor(name, shape, dt, kind="ExternalOutput" if dbg else "Internal").ap()

        def sb(name, shape, dt=F32, ctx=top):
            return ctx.enter_context(nc.sbuf_tensor(name, shape, dt))

        def ps(ctx, name, shape=(P, 512)):
            return ctx.enter_context(nc.psum_tensor(name, list(shape), F32))

        def sem(name):
            return top.enter_context(nc.semaphore(name))

        node_rows = dram("node_rows", (NP, RW))
        ad_rows = dram("ad_rows", (NP, H))
        x2_rows = dram("x2_rows", (NP, D))
        xs_rows, ys_rows = dram("xs_rows", (max(TILES, GROUPS) * P, D)), dram("ys_rows", (SLOTS, D))
        agg_rows = dram("agg_rows", (GROUPS * G, P, D))
        cst = sb("cst", [P, 4 * P + 16 + SJ + 2 * NT + 1 + G * H])
        ident, tri, ones, same_win = (cst[:, i * P:(i + 1) * P] for i in range(4))
        o = 4 * P
        iota16, step_no = cst[:, o:o + 16], cst[:, o + 16:o + 16 + SJ]
        o += 16 + SJ
        tile_win, dst_no = cst[:, o:o + 2 * NT].rearrange("p (j t) -> p j t", t=NT), cst[:, o + 2 * NT:o + 2 * NT + 1]
        o += 2 * NT + 1
        same_step = cst[:, o:o + G * H].rearrange("p (s h) -> p s h", h=H)
        eps = sb("eps", [P, 3])
        last_row = sb("last_row", [P, NT], U32)
        last_step = sb("last_step", [P, 2], U32)
        lg = sb("lg", [P, NT, E])
        both_y = sb("qT_y", [P, NT * D])
        qT = both_y.rearrange("p (k n) -> p k n", k=KD)
        y_all = both_y.rearrange("p (t f) -> p t f", f=D)
        node_ctx = ExitStack()
        xna = sb("xna", [P, NT, RW], ctx=node_ctx)
        ad = sb("ad", [P, NT, H], ctx=node_ctx)
        W = sb("W", [P, KD, H, D], ctx=node_ctx)
        kvd = sb("kvd", [P, KD, P + 4], ctx=node_ctx)
        gw = sb("gw", [P, H], ctx=node_ctx)
        WoT = sb("WoT", [P, KD, D], ctx=node_ctx)
        gwb = sb("gwb", [P, D], ctx=node_ctx)
        bob = sb("bob", [P, D], ctx=node_ctx)
        v_chain = Line(sem("v_chain"))
        consts = Loads(sem("consts_loaded"))
        moves = Loads(sem("sp_moved"))
        s_gate = sem("s_gate")

        edge_ctx = ExitStack()
        srcT = sb("srcT", [P, SP_], U32, edge_ctx)
        dlocT = sb("dlocT", [P, SP_], ctx=edge_ctx)
        resetT = sb("resetT", [P, SP_], ctx=edge_ctx)
        rowc = sb("rowc", [P, 2, SJ], U32, edge_ctx)
        with ExitStack() as ctx:
            C1 = CHUNKS - 1
            end_i = sb("end_i", [1, C1], I32, ctx)
            ends = sb("ends", [1, 3, C1], ctx=ctx)
            junk = sb("junk", [P, C1], ctx=ctx)
            cs = sb("cs", [P, 6, SJ], ctx=ctx)
            cnt = sb("cnt", [P, 2], ctx=ctx)
            by_tile = sb("by_tile", [P, 2, NT], ctx=ctx)
            gsd = sb("gsd", [P, SJ, 2, P], I32, ctx)
            tab = sb("tab", [P, SJ, 3, P], ctx=ctx)
            end_ready, ends_ps, rows_ready, steps_in, steps_ps = sem("end_ready"), sem("ends_ps"), sem("rows_ready"), sem("steps_in"), sem("steps_ps")
            s_gsd, tabs, tabs_ps = sem("s_gsd"), sem("tabs"), sem("tabs_ps")
            A = sb("att", [P, 2, H, D], ctx=ctx)
            tmpW = sb("tmpW", [P, 3, H, D], ctx=ctx)
            V = sb("V", [P, KD, 2 * H], ctx=ctx)
            wq = sb("wq", [P, KD, 3 * D], ctx=ctx)
            wn1 = sb("wn1", [P, KD], ctx=ctx)
            gmx = sb("gmx", [P, 2], ctx=ctx)
            st6 = sb("st6", [P, NT, 6], ctx=ctx)
            mean = sb("mean", [P, NT], ctx=ctx)
            var = sb("var", [P, NT], ctx=ctx)
            rs = sb("rs", [P, NT], ctx=ctx)
            rr = sb("rr", [P, NT], ctx=ctx)
            xs = sb("xs", [P, 2, D], ctx=ctx)
            xT = sb("xT", [P, 2, KD, P], ctx=ctx)
            ez = sb("ez", [P, 2, 2 * D], ctx=ctx)
            mz = sb("mz", [P, 2, 2 * D], ctx=ctx)
            qk = sb("qk", [P, 2, 2 * D], ctx=ctx)
            vv = sb("vv", [P, 2, KD, P + 1], ctx=ctx)
            pT = [ps(ctx, f"pT{c}") for c in range(2)]
            pQ = [ps(ctx, f"pQ{c}") for c in range(2)]
            pV = [ps(ctx, f"pV{c}") for c in range(2)]
            pq = ps(ctx, "pq")
            pK = ps(ctx, "pK")[:, 0:KD * (P + 1)].rearrange("p (g n) -> p g n", g=KD)
            s_W, s_att, s_wq = sem("s_W"), sem("s_att"), sem("s_wq")
            consts.expect(3)
            v_prod, a_wq = sem("v_prod"), sem("a_wq")
            s_x = [sem(f"s_x{j}") for j in range(5)]
            pE, pW = pT[0], pT[1]
            pj = [pT[0], pT[1], pQ[0], pQ[1], pV[0]]
            ones_in, v_W, v_gw, v_stat = sem("ones_in"), sem("v_W"), sem("v_gw"), sem("v_stat")
            a_gw, a_rs = sem("a_gw"), sem("a_rs")
            normed, copied, xT_ps, xT_sb = (Count(sem(n)) for n in ("normed", "copied", "xT_ps", "xT_sb"))
            qkv_ps, elu_e, v_sb = Count(sem("qkv_ps")), Count(sem("elu_e")), Count(sem("v_sb"), 2)
            qk_sb, a_sb, kv_done = Count(sem("qk_sb"), 2), Count(sem("a_sb"), 2), Count(sem("kv_done"))
            qT_ps, qT_sb = Count(sem("qT_ps")), Count(sem("qT_sb"))
            with nc.Block() as block:
                @block.sync
                def _(sp):
                    sp.dma_start(cst[:, :], a["cst"][:, :]).then_inc(consts.sem, 16)
                    sp.dma_start(end_i[:, :], a["chunk_end"][:, :]).then_inc(consts.sem, 16)
                    sp.dma_start(ends[:, 2, :], a["chunk_no"][:, :]).then_inc(consts.sem, 16)
                    for k in range(KD):
                        sp.dma_start(W[:, k, :, :], a["W"][:, k * P:(k + 1) * P, :].rearrange("h p d -> p h d")).then_inc(s_W, 16)
                    for j in range(5):
                        sp.dma_start(xna[:, 5 * j:5 * j + 5, 0:D],
                                     a["x"][5 * j * P:(5 * j + 5) * P, :].rearrange("(t p) f -> p t f", p=P)).then_inc(s_x[j], 16)
                    wait(sp, a_sb, NT - 1)
                    wait(sp, copied, NT - 1)
                    sp.wait_ge(ones_in, 1)
                    sp.dma_start(ad_rows.rearrange("(t p) h -> p t h", p=P), ad[:, :, :]).then_inc(moves.sem, 16)
                    sp.dma_start(node_rows.rearrange("(t p) f -> p t f", p=P), xna[:, :, :]).then_inc(moves.sem, 16)
                    moves.expect(2)
                    moves.wait(sp)

                @block.gpsimd
                def _(pool):
                    pool.memset(xna[:, :, AS + H:RW], 0.0)
                    pool.memset(xna[:, :, ONE:ONE + 1], 1.0).then_inc(ones_in, 1)
                    pool.wait_ge(rows_ready, 1)
                    for j in range(SJ):
                        pool.indirect_dma_start(gsd[:, j, :, :].rearrange("p i n -> p (i n)"), None, a["src_dst"][:, :], at_row(rowc[:, 0, j:j + 1])).then_inc(s_gsd, 16)
                    pool.wait_ge(s_W, 32)
                    pool.wait_ge(s_att, 32)
                    for i in range(2):
                        pool.tensor_tensor(tmpW[:, 1 + i, :, :], W[:, 1, :, :], A[:, i, :, :], ALU.mult).then_inc(v_prod, 1)

                @block.scalar
                def _(act):
                    act.dma_start(A[:, 0, :, :], a["att_src"].partition_broadcast(P)).then_inc(s_att, 16)
                    act.dma_start(A[:, 1, :, :], a["att_dst"].partition_broadcast(P)).then_inc(s_att, 16)
                    act.dma_start(wq[:, :, :], a["mix_w_qkv"].rearrange("(k p) n -> p k n", p=P)).then_inc(s_wq, 16)
                    act.dma_start(wn1[:, :], a["mix_w_norm1"][:, :]).then_inc(s_wq, 16)
                    act.dma_start(gw[:, :], a["gate_weights"].partition_broadcast(P)).then_inc(s_wq, 16)
                    act.wait_ge(s_wq, 48)
                    for k in range(KD):
                        act.activation(wq[:, k, :], wq[:, k, :], ACT.Copy, scale=wn1[:, k:k + 1]).then_inc(a_wq, 1)
                    act.wait_ge(v_stat, NT + 1)
                    act.activation(rs[:, :], var[:, :], ACT.Sqrt, bias=eps[:, 0:1]).then_inc(a_rs, 1)
                    act.wait_ge(v_stat, NT + 2)
                    act.activation(rr[:, :], rr[:, :], ACT.Sqrt, bias=eps[:, 1:2]).then_inc(a_rs, 1)

                    def copies(t, c, r):
                        wait(act, normed, t)
                        act.sem_inc(s_gate, 1)
                        act.activation(tile(xna, t, 0, D), xs[:, c, :], ACT.Copy).then_inc(copied.sem, 1)
                        wait(act, xT_ps, t)
                        wait(act, qkv_ps, t - 2)
                        act.activation(xT[:, c, :, :], pT[c][:, 0:D].rearrange("p (k f) -> p k f", k=KD), ACT.Copy).then_inc(xT_sb.sem, 1)

                    def exps(t, c, r):
                        wait(act, qkv_ps, t)
                        wait(act, qk_sb, t - 2)
                        act.sem_inc(s_gate, 1)
                        act.activation(ez[:, c, :], pQ[c][:, :], ACT.Exp, scale=col(rr, t)).then_inc(elu_e.sem, 1)

                    def vs(t, c, r):
                        wait(act, kv_done, t - 2)
                        act.sem_inc(s_gate, 1)
                        for g in range(KD):
                            act.activation(vv[:, c, g, 0:P], pV[c][:, g * P:(g + 1) * P], ACT.Copy, scale=col(rr, t)).then_inc(v_sb.sem, 1)

                    act.wait_ge(v_gw, 1)
                    act.activation(gw[:, :], gw[:, :], ACT.Exp, bias=gmx[:, 0:1], accum_out=gmx[:, 1:2]).then_inc(a_gw, 1)
                    act.wait_ge(v_stat, NT + 3)
                    pipeline(act, NT, [(0, copies), (1, exps), (1, vs)])

                @block.tensor
                def _(pe):
                    consts.wait(pe)
                    pe.wait_ge(end_ready, 1)
                    pe.matmul(pE[:, 0:C1], ones[0:1, :], ends[:, 1, :], start=True, stop=True).then_inc(ends_ps, 1)
                    pe.matmul(pW[:, 0:C1], ones[0:1, :], ends[:, 0, :], start=True, stop=True).then_inc(ends_ps, 1)
                    pe.wait_ge(steps_in, 1)
                    for j in range(2):
                        mm = pe.matmul(pE[:, 448:448 + NT], same_win, by_tile[:, j, :], start=(j == 0), stop=(j == 1))
                    mm.then_inc(steps_ps, 1)
                    pe.wait_ge(v_W, 2)
                    pe.wait_ge(a_wq, KD)

                    def xTs(t, c, r):
                        wait(pe, normed, t)
                        wait(pe, xT_sb, t - 2)
                        for k in range(KD):
                            mm = pe.transpose(pT[c][:, k * P:(k + 1) * P], xs[:, c, k * P:(k + 1) * P], ident)
                        mm.then_inc(xT_ps.sem, 1)

                    def qkv(t, c, r):
                        wait(pe, xT_sb, t)
                        wait(pe, elu_e, t - 2)
                        wait(pe, v_sb, t - 2)
                        wait(pe, qk_sb, t - 2)
                        wait(pe, a_sb, t - 2)
                        for k in range(KD):
                            pe.matmul(pQ[c][:, :], xT[:, c, k, :], wq[:, k, 0:2 * D], start=(k == 0), stop=(k == KD - 1))
                        for k in range(KD):
                            pe.matmul(pV[c][:, 0:D], xT[:, c, k, :], wq[:, k, 2 * D:3 * D], start=(k == 0), stop=(k == KD - 1))
                        for k in range(KD):
                            mm = pe.matmul(pV[c][:, D:D + 2 * H], xT[:, c, k, :], V[:, k, :], start=(k == 0), stop=(k == KD - 1))
                        mm.then_inc(qkv_ps.sem, 1)

                    def kv(t, c, r):
                        wait(pe, qk_sb, t)
                        wait(pe, v_sb, t)
                        first, last = isinstance(t, int) and t == 0, isinstance(t, int) and t == NT - 1
                        m = LAST if last else P
                        for g in range(KD):
                            mm = pe.matmul(pK[:, g, :], qk[0:m, c, D + g * P:D + (g + 1) * P], vv[0:m, c, g, :],
                                           start=first and g == 0, stop=last, skip_group_check=True)
                        mm.then_inc(kv_done.sem, 1)
                        wait(pe, qT_sb, t - 1)
                        for k in range(KD):
                            mm = pe.transpose(pq[:, k * P:(k + 1) * P], qk[:, c, k * P:(k + 1) * P], ident)
                        mm.then_inc(qT_ps.sem, 1)

                    pipeline(pe, NT, [(3, kv), (0, xTs), (1, qkv)])
                    for j in range(SJ):
                        pe.wait_ge(tabs, j + 1)
                        for i in range(3):
                            mm = pe.transpose(pj[j][:, i * P:(i + 1) * P], tab[:, j, i, :], ident)
                        mm.then_inc(tabs_ps, 1)

                @block.vector
                def _(dve):
                    line = v_chain.on(dve)
                    dve.memset(eps[:, 0:1], LN_EPS)
                    dve.memset(eps[:, 1:2], RMS_EPS)
                    dve.memset(eps[:, 2:3], 0.0)
                    line.do(dve.memset(vv[:, :, :, P:P + 1], 1.0))
                    consts.wait(dve)
                    line.do(dve.tensor_scalar(end_i[:, :], end_i[:, :], 4, None, ALU.arith_shift_right))
                    line.do(dve.tensor_copy(ends[:, 0, :], end_i[:, :]))
                    dve.tensor_tensor(ends[:, 1, :], ends[:, 0, :], ends[:, 2, :], ALU.add).then_inc(end_ready, 1)
                    line.do(dve.tensor_scalar(cs[:, 5, :], step_no, -1.0, None, ALU.add))
                    dve.wait_ge(ends_ps, 2)
                    for j in range(SJ):
                        line.do(dve.tensor_scalar(junk[:, :], pE[:, 0:C1], step_no[:, j:j + 1], None, ALU.is_lt, ALU.add, accum_out=cs[:, 0, j:j + 1]))
                        line.do(dve.tensor_scalar(junk[:, :], pE[:, 0:C1], cs[:, 5, j:j + 1], None, ALU.is_lt, ALU.add, accum_out=cs[:, 1, j:j + 1]))
                    line.do(dve.tensor_copy(rowc[:, 0, :], cs[:, 0, :]))
                    line.do(dve.tensor_tensor(cs[:, 2, :], step_no, cs[:, 0, :], ALU.subtract))
                    line.do(dve.tensor_scalar(cs[:, 3, :], cs[:, 2, :], float(DW), None, ALU.mult))
                    line.do(dve.tensor_scalar(rowc[:, 1, :], cs[:, 2, :], float(WINDOWS - 1), None, ALU.min))
                    dve.sem_inc(rows_ready, 1)
                    line.do(dve.tensor_tensor(cs[:, 4, :], cs[:, 0, :], cs[:, 1, :], ALU.subtract))
                    line.do(dve.tensor_scalar(cs[:, 4, :], cs[:, 4, :], -1.0, BIG, ALU.add, ALU.mult))
                    for j in range(2):
                        line.do(dve.tensor_scalar(junk[:, :], pW[:, 0:C1], step_no[:, j:j + 1], None, ALU.is_le, ALU.add, accum_out=cnt[:, j:j + 1]))
                    line.do(dve.tensor_tensor(cnt[:, :], cnt[:, :], step_no[:, 0:2], ALU.add))
                    line.do(dve.tensor_scalar(cnt[:, :], cnt[:, :], float(STEPS - 1), None, ALU.min))
                    line.do(dve.tensor_copy(last_step[:, :], cnt[:, :]))
                    for j in range(2):
                        line.do(dve.tensor_scalar(by_tile[:, j, :], tile_win[:, j, :], cnt[:, j:j + 1], None, ALU.mult))
                    dve.sem_inc(steps_in, 1)
                    dve.wait_ge(steps_ps, 1)
                    line.do(dve.tensor_scalar(last_row[:, :], pE[:, 448:448 + NT], float(DW), dst_no, ALU.mult, ALU.add))
                    dve.wait_ge(s_W, 32)
                    dve.wait_ge(s_att, 32)
                    for i in range(2):
                        line.do(dve.tensor_tensor(tmpW[:, 0, :, :], W[:, 0, :, :], A[:, i, :, :], ALU.mult))
                        line.do(dve.tensor_reduce(V[:, 0, i * H:(i + 1) * H], tmpW[:, 0, :, :], AX.X, ALU.add))
                    for j in range(5):
                        dve.wait_ge(s_x[j], 16)
                        for t in range(5 * j, 5 * j + 5):
                            dve.bn_stats(tile(st6, t, 0, 6), tile(xna, t, 0, D)).then_inc(v_stat, 1)
                    dve.wait_ge(v_stat, NT)
                    line.do(dve.tensor_tensor(mean[:, :], st6[:, :, 1], st6[:, :, 4], ALU.subtract))
                    line.do(dve.tensor_scalar(mean[:, :], mean[:, :], 0.5, None, ALU.mult))
                    line.do(dve.tensor_tensor(mean[:, :], mean[:, :], mean[:, :], ALU.mult))
                    line.do(dve.tensor_tensor(var[:, :], st6[:, :, 2], st6[:, :, 5], ALU.add))
                    line.do(dve.scalar_tensor_tensor(out=var[:, :], in0=var[:, :], scalar=1.0 / D, in1=mean[:, :], op0=ALU.mult, op1=ALU.add))
                    line.do(dve.tensor_tensor(mean[:, :], st6[:, :, 1], st6[:, :, 4], ALU.add))
                    line.do(dve.tensor_scalar(mean[:, :], mean[:, :], 0.5, None, ALU.mult))
                    dve.sem_inc(v_stat, 1)
                    dve.wait_ge(a_rs, 1)
                    line.do(dve.reciprocal(rs[:, :], rs[:, :]))
                    line.do(dve.tensor_tensor(rr[:, :], rs[:, :], rs[:, :], ALU.mult))
                    dve.tensor_tensor(rr[:, :], rr[:, :], var[:, :], ALU.mult).then_inc(v_stat, 1)
                    dve.wait_ge(a_rs, 2)
                    dve.reciprocal(rr[:, :], rr[:, :]).then_inc(v_stat, 1)
                    dve.wait_ge(v_stat, NT + 3)
                    dve.wait_ge(s_wq, 48)
                    line.do(dve.tensor_reduce(gmx[:, 0:1], gw[:, :], AX.X, ALU.max))
                    dve.tensor_scalar(gmx[:, 0:1], gmx[:, 0:1], -1.0, None, ALU.mult).then_inc(v_gw, 1)
                    for i in range(2):
                        dve.wait_ge(v_prod, i + 1)
                        dve.tensor_reduce(V[:, 1, i * H:(i + 1) * H], tmpW[:, 1 + i, :, :], AX.X, ALU.add).then_inc(v_W, 1)

                    def norm(t, c, r):
                        wait(dve, xT_ps, t - 2)
                        wait(dve, copied, t - 2)
                        dve.tensor_scalar(xs[:, c, :], tile(xna, t, 0, D), col(mean, t), col(rs, t), ALU.subtract, ALU.mult).then_inc(normed.sem, 1)

                    def elu(t, c, r):
                        wait(dve, elu_e, t)
                        dve.tensor_scalar(mz[:, c, :], pQ[c][:, :], col(rr, t), 0.0, ALU.mult, ALU.max).then_inc(qk_sb.sem, 1)
                        wait(dve, qk_sb, t, 1)
                        wait(dve, kv_done, t - 2)
                        wait(dve, qT_ps, t - 2)
                        dve.scalar_tensor_tensor(out=qk[:, c, :], in0=ez[:, c, :], scalar=1.0, in1=mz[:, c, :], op0=ALU.min, op1=ALU.add).then_inc(qk_sb.sem, 1)
                        wait(dve, v_sb, t)
                        dve.tensor_scalar(tile(xna, t, AS, AS + H), pV[c][:, D:D + H], 0.0, None, ALU.add).then_inc(a_sb.sem, 1)
                        dve.tensor_scalar(tile(ad, t, 0, H), pV[c][:, D + H:D + 2 * H], 0.0, None, ALU.add).then_inc(a_sb.sem, 1)

                    def qTs(t, c, r):
                        wait(dve, qT_ps, t)
                        for k in range(KD):
                            ins = dve.tensor_scalar(qT[:, k, t * P:(t + 1) * P] if isinstance(t, int) else qT[:, k, ds(t * P, P)],
                                                    pq[:, k * P:(k + 1) * P], 0.0, None, ALU.add)
                        ins.then_inc(qT_sb.sem, 1)

                    pipeline(dve, NT, [(0, norm), (2, elu), (3, qTs)])
                    dve.wait_ge(a_gw, 1)
                    line.do(dve.reciprocal(gmx[:, 1:2], gmx[:, 1:2]))
                    line.do(dve.tensor_scalar(gw[:, :], gw[:, :], gmx[:, 1:2], None, ALU.mult))
                    dve.wait_ge(s_gsd, 16 * SJ)
                    for j in range(SJ):
                        dve.tensor_copy(tab[:, j, 0, :], gsd[:, j, 0, :])
                        dve.tensor_scalar(tab[:, j, 1, :], gsd[:, j, 1, :], cs[:, 3, j:j + 1], None, ALU.subtract)
                        dve.tensor_scalar(tab[:, j, 2, :], ones, cs[:, 4, j:j + 1], None, ALU.mult).then_inc(tabs, 1)
                    wait(dve, kv_done, NT - 1)
                    line.do(dve.memset(kvd[:, :, :], 0.0))
                    for g in range(KD):
                        for b in range(P // HD):
                            s = slice(b * HD, (b + 1) * HD)
                            dve.tensor_copy(kvd[s, g, b * HD:(b + 1) * HD], pK[s, g, b * HD:(b + 1) * HD])
                            dve.tensor_copy(kvd[s, g, P + b:P + b + 1], pK[s, g, P:P + 1])
                    for j in range(SJ):
                        dve.wait_ge(tabs_ps, j + 1)
                        s = slice(j * P, (j + 1) * P)
                        dve.tensor_copy(srcT[:, s], pj[j][:, 0:P])
                        dve.tensor_copy(dlocT[:, s], pj[j][:, P:2 * P])
                        dve.tensor_copy(resetT[:, s], pj[j][:, 2 * P:3 * P])


        md_rows = dram("md_rows", (SP_ * DW, 2 * H))
        ad_step = dram("ad_step", (SP_, P))
        with ExitStack() as ctx:
            gad = sb("gad", [P, SJ, P], ctx=ctx)
            adsd = sb("adsd", [P, SP_ // G, H], ctx=ctx)
            s_gad = sem("s_gad")
            moves.expect(2)
            U, V2 = 6, 2
            idx = sb("idx", [P, U, G], U32, ctx)
            rows = sb("rows", [P, U, G, RW], ctx=ctx)
            eq = sb("eq", [P, V2, G, DW], ctx=ctx)
            pen = sb("pen", [P, V2, G, DW], ctx=ctx)
            adb = sb("adb", [P, V2, G, H], ctx=ctx)
            eqT = sb("eqT", [P, V2, P], ctx=ctx)
            zs = sb("zs", [P, V2, 2, G, H], ctx=ctx)
            zm = sb("zm", [P, V2, G, DW, H], ctx=ctx)
            mst = sb("mst", [P, V2, 3, G], ctx=ctx)
            rsc = sb("rsc", [P, V2, G], ctx=ctx)
            pexp = sb("pexp", [P, V2, G, P], ctx=ctx)
            pw = sb("pw", [P, V2, G, P], ctx=ctx)
            acc = sb("acc", [P, V2, G, D + 2], ctx=ctx)
            mall = sb("mall", [P, SP_ + 8], ctx=ctx)
            dall = sb("dall", [P, SP_], ctx=ctx)
            mdT = sb("mdT", [P, SJ, DW, 2, H], ctx=ctx)
            pA = ps(ctx, "pA", (P, 1024))
            pP = ps(ctx, "pP", (P, 1024))
            pO = [ps(ctx, f"pO{i}") for i in range(3)]
            pM = ps(ctx, "pM")
            zero = sb("zero", [P, D], ctx=ctx)
            zero_in, s_zero = sem("zero_in"), sem("s_zero")
            bg = sb("bg", [P, H, D], ctx=ctx)
            gam = sb("gam", [P, 2, KD], ctx=ctx)
            betaR = sb("betaR", [P, KD, P], ctx=ctx)
            v_cw, cw_ps = sem("v_cw"), sem("cw_ps")
            consts.expect(5)
            s_rows = [sem(f"s_rows{c}") for c in range(U)]
            s_agg = [sem(f"s_agg{c}") for c in range(V2)]
            idx_in, masks, eqT_ps, eqT_sb = Count(sem("idx_in")), Count(sem("masks"), 3), Count(sem("eqT_ps")), Count(sem("eqT_sb"))
            adE_ps, scored, zT_ps, maxed = Count(sem("adE_ps")), Count(sem("scored"), 3), Count(sem("zT_ps")), Count(sem("maxed"), 5)
            exped, pT_ps, pw_in, prod, acced = Count(sem("exped"), 2), Count(sem("pT_ps")), Count(sem("pw_in")), Count(sem("prod"), G), Count(sem("acced"), G + 1)
            md_ps, md_sb = Count(sem("md_ps")), Count(sem("md_sb"))

            def md_bank(i):
                return (pA, pP)[i][:, 0:SJ * P]

            def half(g, c, r):
                return r * (U // V2) + c // V2

            with nc.Block() as block:
                @block.gpsimd
                def _(pool):
                    pool.memset(zero[:, :], 0.0).then_inc(zero_in, 1)
                    for j in range(SJ):
                        pool.indirect_dma_start(gad[:, j, :], None, ad_rows.rearrange("(w d) h -> w (d h)", d=DW), at_row(rowc[:, 1, j:j + 1])).then_inc(s_gad, 16)

                    def gather(g, c, r):
                        wait(pool, prod, g - U)
                        wait(pool, idx_in, g)
                        pool.sem_inc(s_gate, 1)
                        for s in range(G):
                            pool.indirect_dma_start(rows[:, c, s, :], None, node_rows[:, :], at_row(idx[:, c, s:s + 1])).then_inc(s_rows[c], 16)
                    pipeline(pool, GROUPS, [(0, gather)], U, U)

                @block.vector
                def _(dve):
                    dve.memset(acc[:, V2 - 1, G - 1, :], 0.0)
                    dve.memset(dall[:, :], 0.0)
                    v_chain.on(dve).do(dve.memset(mall[:, :], 0.0))

                    def small_weights():
                        line = v_chain.on(dve)
                        consts.wait(dve)
                        for k in range(KD):
                            ins = dve.tensor_scalar(betaR[:, k, :], ones, gam[:, 1, k:k + 1], None, ALU.mult)
                        ins.then_inc(v_cw, 1)
                        line.do(dve.tensor_scalar(gwb[:, :], bg[:, 0, :], gw[:, 0:1], None, ALU.mult))
                        for h in range(1, H):
                            line.do(dve.scalar_tensor_tensor(out=gwb[:, :], in0=bg[:, h, :], scalar=gw[:, h:h + 1], in1=gwb[:, :], op0=ALU.mult, op1=ALU.add))
                        dve.wait_ge(cw_ps, 1)
                        dve.tensor_tensor(bob[:, :], bob[:, :], pM[:, D:2 * D], ALU.add).then_inc(v_cw, 1)
                        for k in range(KD):
                            dve.tensor_scalar(WoT[:, k, :], WoT[:, k, :], gam[:, 0, k:k + 1], None, ALU.mult)

                    m_at = lambda g, one: mall[:, one + g * G:one + g * G + G] if isinstance(g, int) else mall[:, ds(g * G + one, G)]

                    def sources(g, c, r):
                        dve.tensor_scalar(idx[:, c, :], col(srcT, g, G), 0.0, None, ALU.add).then_inc(idx_in.sem, 1)

                    def mask_eq(g, c, r):
                        wait(dve, eqT_ps, g - V2)
                        wait(dve, masks, g - V2)
                        dve.tensor_tensor(eq[:, c % V2, :, :], col(dlocT, g, G).unsqueeze(2).to_broadcast([P, G, DW]),
                                          iota16.unsqueeze(1).to_broadcast([P, G, DW]), ALU.is_equal).then_inc(masks.sem, 1)

                    def mask_ad(g, c, r):
                        if isinstance(g, int) and g == 0:
                            moves.wait(dve)
                        wait(dve, adE_ps, g - V2)
                        dve.tensor_tensor(adb[:, c % V2, :, :], same_step, tile(adsd, g, 0, H).unsqueeze(1).to_broadcast([P, G, H]),
                                          ALU.mult).then_inc(masks.sem, 1)

                    def mask_pen(g, c, r):
                        wait(dve, masks, g, 1)
                        wait(dve, scored, g - V2)
                        dve.tensor_scalar(pen[:, c % V2, :, :], eq[:, c % V2, :, :], -1.0, BIG, ALU.add, ALU.mult).then_inc(masks.sem, 1)

                    def score_sum(g, c, r):
                        dve.wait_ge(s_rows[c], (r + 1) * (16 * G))
                        wait(dve, adE_ps, g)
                        dve.tensor_tensor(zs[:, c % V2, 0, :, :], rows[:, c, :, AS:AS + H], pM[:, P:P + G * H].rearrange("p (s h) -> p s h", h=H),
                                          ALU.add).then_inc(scored.sem, 1)

                    def score_relu(g, c, r):
                        wait(dve, scored, g, 1)
                        dve.scalar_tensor_tensor(out=zs[:, c % V2, 1, :, :], in0=zs[:, c % V2, 0, :, :], scalar=0.2, in1=zs[:, c % V2, 0, :, :],
                                                 op0=ALU.mult, op1=ALU.max).then_inc(scored.sem, 1)

                    def score_mask(g, c, r):
                        wait(dve, scored, g, 2)
                        wait(dve, masks, g)
                        wait(dve, zT_ps, g - V2)
                        dve.tensor_tensor(zm[:, c % V2, :, :, :], zs[:, c % V2, 1, :, :].unsqueeze(2).to_broadcast([P, G, DW, H]),
                                          pen[:, c % V2, :, :].unsqueeze(3).to_broadcast([P, G, DW, H]), ALU.add).then_inc(scored.sem, 1)

                    def max_step(g, c, r):
                        wait(dve, zT_ps, g)
                        wait(dve, maxed, g - 1)
                        wait(dve, exped, g - V2)
                        dve.tensor_reduce(mst[:, c % V2, 0, :], pA[:, :].rearrange("p (s e) -> p s e", s=G), AX.X, ALU.max).then_inc(maxed.sem, 1)

                    def max_scan(g, c, r):
                        wait(dve, maxed, g, 1)
                        dve.tensor_tensor_scan(m_at(g, 1), col(resetT, g, G), mst[:, c % V2, 0, :], mall[:, g * G:g * G + 1] if isinstance(g, int) else mall[:, ds(g * G, 1)],
                                               ALU.add, ALU.max).then_inc(maxed.sem, 1)

                    def max_neg(g, c, r):
                        wait(dve, maxed, g, 2)
                        dve.tensor_scalar(mst[:, c % V2, 1, :], m_at(g, 1), -1.0, None, ALU.mult).then_inc(maxed.sem, 1)

                    def max_old(g, c, r):
                        dve.tensor_tensor(mst[:, c % V2, 2, :], col(mall, g, G), col(resetT, g, G), ALU.add).then_inc(maxed.sem, 1)

                    def max_change(g, c, r):
                        wait(dve, maxed, g, 4)
                        dve.tensor_tensor(mst[:, c % V2, 2, :], mst[:, c % V2, 2, :], mst[:, c % V2, 1, :], ALU.add).then_inc(maxed.sem, 1)

                    def accumulate(s):
                        def stage(g, c, r):
                            if s == 0:
                                wait(dve, exped, g)
                                if not isinstance(g, int) or g >= V2:
                                    dve.wait_ge(s_agg[c % V2], half(g, c, r) * 16)
                            wait(dve, prod, g, s + 1)
                            before = acc[:, c % V2, s - 1, 0:D + 1] if s else acc[:, (c - 1) % V2, G - 1, 0:D + 1]
                            if s or not (isinstance(g, int) and g == 0):
                                wait(dve, acced, g if s else g - 1, s if s else None)
                            dve.scalar_tensor_tensor(out=acc[:, c % V2, s, 0:D + 1], in0=before, scalar=rsc[:, c % V2, s:s + 1],
                                                     in1=pO[(c * G + s) % 3][:, 0:D + 1], op0=ALU.mult, op1=ALU.add).then_inc(acced.sem, 1)
                        return stage

                    def keep_den(g, c, r):
                        wait(dve, acced, g, G)
                        dve.tensor_scalar(col(dall, g, G), acc[:, c % V2, :, D], 0.0, None, ALU.add).then_inc(acced.sem, 1)

                    add = [(4, accumulate(s)) for s in range(G)]
                    pipeline(dve, GROUPS, [(0, sources), (2, score_sum), (1, mask_eq), (2, score_relu), (1, mask_ad), (2, score_mask), (3, max_step),
                                           add[0], (3, max_scan), add[1], (3, max_neg), add[2], (3, max_old), add[3], (3, max_change),
                                           add[4], (1, mask_pen), add[5], add[6], add[7], (4, keep_den)], U, U, small_weights)
                    for i in range(2):
                        wait(dve, md_ps, i)
                        dve.tensor_copy(mdT[:, :, :, i, :], md_bank(i).rearrange("p (j d h) -> p j d h", d=DW, h=H)).then_inc(md_sb.sem, 1)

                @block.scalar
                def _(act):
                    def copy_eq(g, c, r):
                        wait(act, eqT_ps, g)
                        wait(act, adE_ps, g - V2)
                        act.activation(eqT[:, c % V2, :], pM[:, 0:P], ACT.Copy).then_inc(eqT_sb.sem, 1)

                    def exps(g, c, r):
                        wait(act, maxed, g)
                        wait(act, pT_ps, g - V2)
                        wait(act, acced, g - V2)
                        for s in range(G):
                            ins = act.activation(pexp[:, c % V2, s, :], pA[:, s * P:(s + 1) * P], ACT.Exp, bias=mst[:, c % V2, 1, s:s + 1])
                        ins.then_inc(exped.sem, 1)
                        act.activation(rsc[:, c % V2, :], mst[:, c % V2, 2, :], ACT.Exp).then_inc(exped.sem, 1)

                    def copy_p(g, c, r):
                        wait(act, pT_ps, g)
                        wait(act, prod, g - V2)
                        act.activation(pw[:, c % V2, :, :], pP[:, :].rearrange("p (s e) -> p s e", s=G), ACT.Copy).then_inc(pw_in.sem, 1)

                    pipeline(act, GROUPS, [(4, copy_p), (1, copy_eq), (3, exps)], U, U)

                @block.tensor
                def _(pe):
                    def beta_out():
                        pe.wait_ge(v_cw, 1)
                        for k in range(KD):
                            mm = pe.matmul(pM[:, D:2 * D], betaR[:, k, :], WoT[:, k, :], start=(k == 0), stop=(k == KD - 1))
                        mm.then_inc(cw_ps, 1)
                        pe.wait_ge(v_cw, 2)

                    def eq_turn(g, c, r):
                        wait(pe, masks, g, 1)
                        wait(pe, scored, g - 1, 1)
                        pe.transpose(pM[:, 0:P], eq[:, c % V2, :, :].rearrange("p s d -> p (s d)"), ident).then_inc(eqT_ps.sem, 1)

                    def ad_edges(g, c, r):
                        wait(pe, eqT_sb, g)
                        wait(pe, masks, g, 2)
                        pe.matmul(pM[:, P:P + G * H], eqT[:, c % V2, :], adb[:, c % V2, :, :].rearrange("p s h -> p (s h)"), start=True, stop=True).then_inc(adE_ps.sem, 1)

                    def z_turn(g, c, r):
                        wait(pe, scored, g)
                        wait(pe, exped, g - 1, 1)
                        for s in range(G):
                            mm = pe.transpose(pA[:, s * P:(s + 1) * P], zm[:, c % V2, s, :, :].rearrange("p d h -> p (d h)"), ident)
                        mm.then_inc(zT_ps.sem, 1)

                    def p_turn(g, c, r):
                        wait(pe, exped, g, 1)
                        wait(pe, pw_in, g - 1)
                        for s in range(G):
                            mm = pe.transpose(pP[:, s * P:(s + 1) * P], pexp[:, c % V2, s, :], ident)
                        mm.then_inc(pT_ps.sem, 1)

                    def product(lo, hi):
                        def stage(g, c, r):
                            if lo == 0:
                                wait(pe, pw_in, g)
                            for s in range(lo, hi):
                                if s >= 3:
                                    wait(pe, acced, g, s - 2)
                                elif not isinstance(g, int) or g > 0:
                                    wait(pe, acced, g - 1, G - 2 + s)
                                pe.matmul(pO[(c * G + s) % 3][:, 0:D + 1], pw[:, c % V2, s, :], rows[:, c, s, 0:D + 1], start=True, stop=True).then_inc(prod.sem, 1)
                        return stage

                    pipeline(pe, GROUPS, [(4, p_turn), (3, z_turn), (1, eq_turn), (4, product(0, 4)), (1, ad_edges), (4, product(4, G))], U, U, beta_out)
                    wait(pe, acced, GROUPS - 1)
                    for i in range(2):
                        for j in range(SJ):
                            mm = pe.transpose(md_bank(i)[:, j * P:(j + 1) * P], (mall[:, 1 + j * P:1 + (j + 1) * P], dall[:, j * P:(j + 1) * P])[i], ident)
                        mm.then_inc(md_ps.sem, 1)

                @block.sync
                def _(sp):
                    sp.wait_ge(s_gad, 16 * SJ)
                    sp.dma_start(ad_step.rearrange("(j p) n -> p j n", p=P), gad[:, :, :]).then_inc(moves.sem, 16)
                    moves.wait(sp, 1)
                    sp.dma_start(adsd[:, :, :], ad_step.rearrange("(g s) (d h) -> (s d) g h", s=G, h=H)).then_inc(moves.sem, 16)

                    def store(g, c, r):
                        wait(sp, acced, g)
                        o8 = agg_rows[g * G:(g + 1) * G, :, :] if isinstance(g, int) else agg_rows[ds(g * G, G), :, :]
                        sp.dma_start(o8.rearrange("s p f -> p s f"), acc[:, c % V2, :, 0:D]).then_inc(s_agg[c % V2], 16)
                    sp.dma_start(WoT[:, :, :], a["WoT"].rearrange("(k p) n -> p k n", p=P)).then_inc(consts.sem, 16)
                    sp.dma_start(gam[:, 0, :], a["ln_gamma"][:, :]).then_inc(consts.sem, 16)
                    sp.dma_start(gam[:, 1, :], a["ln_beta"][:, :]).then_inc(consts.sem, 16)
                    sp.dma_start(bob[:, :], a["bo"].partition_broadcast(P)).then_inc(consts.sem, 16)
                    sp.dma_start(bg[:, :, :], a["bias_gat"].partition_broadcast(P)).then_inc(consts.sem, 16)
                    sp.wait_ge(zero_in, 1)

                    def clear(g, c, r):
                        sp.dma_start(row(xs_rows, g), zero[:, :]).then_inc(s_zero, 16)
                    pipeline(sp, GROUPS, [(0, store), (0, clear)], U, U)
                    sp.wait_ge(s_zero, 16 * GROUPS)
                    for c in range(V2):
                        sp.wait_ge(s_agg[c], 16 * len(range(c, GROUPS, V2)))
                    wait(sp, md_sb, 1)
                    moves.expect(1)
                    sp.dma_start(md_rows.rearrange("(j p d) m -> p j (d m)", p=P, d=DW), mdT[:, :, :, :, :].rearrange("p j d i h -> p j (d i h)")).then_inc(moves.sem, 16)
                    moves.wait(sp)
        edge_ctx.close()

        x2 = sb("x2", [P, NT, D], ctx=node_ctx)
        al = sb("al", [P, 2, NT, H], ctx=node_ctx)
        with ExitStack() as ctx:
            U = 4
            qs = sb("qs", [P, U, KD, P], ctx=ctx)
            xt = sb("xt", [P, U, D], ctx=ctx)
            wo = sb("wo", [P, KD, D], ctx=ctx)
            bo_, wn2 = sb("mix_bo", [P, D], ctx=ctx), sb("wn2", [P, D], ctx=ctx)
            rz = sb("rz", [P, 2, 2 * QH], ctx=ctx)
            on = sb("on", [P, 2, D], ctx=ctx)
            onT = sb("onT", [P, 2, KD, P], ctx=ctx)
            nb = sb("nb", [P, 2, D], ctx=ctx)
            hh = sb("hh", [P, 2, D], ctx=ctx)
            sq = sb("sq", [P, D], ctx=ctx)
            hw = sb("hw", [P, 2, D], ctx=ctx)
            ms = sb("ms", [P, 2, 2], ctx=ctx)
            mdw = sb("mdw", [P, 2, DW * 2 * H], ctx=ctx)
            mdg = sb("mdg", [P, NT, 2, H], ctx=ctx)
            es = sb("es", [P, 4, NT, H], ctx=ctx)
            md_win = dram("md_win", (2 * P * DW, 2 * H))
            pN = [ps(ctx, f"pN{c}") for c in range(2)]
            pT = [ps(ctx, f"pnT{c}") for c in range(2)]
            pH = [ps(ctx, f"pH{c}") for c in range(2)]
            consts.expect(3)
            s_q, s_xt = [sem(f"s_q{c}") for c in range(U)], [sem(f"s_xt{c}") for c in range(U)]
            num_ps, on_sb, onT_ps, onT_sb, h_ps = Count(sem("num_ps")), Count(sem("on_sb"), 3), Count(sem("onT_ps")), Count(sem("onT_sb")), Count(sem("h_ps"))
            h_sb, rms, hw_in, mixed = Count(sem("h_sb")), Count(sem("rms"), 2), Count(sem("hw_in")), Count(sem("mixed"), 3)
            nb_in, xt_in = Count(sem("nb_in")), Count(sem("xt_in"))
            s_mdw, al_in, al_ex = sem("s_mdw"), sem("al_in"), sem("al_ex")
            with nc.Block() as block:
                @block.sync
                def _(sp):
                    sp.dma_start(wo[:, :, :], a["mix_w_out"].rearrange("(k p) n -> p k n", p=P)).then_inc(consts.sem, 16)
                    sp.dma_start(bo_[:, :], a["mix_b_out"].partition_broadcast(P)).then_inc(consts.sem, 16)
                    sp.dma_start(wn2[:, :], a["mix_w_norm2"].partition_broadcast(P)).then_inc(consts.sem, 16)

                    def load_q(t, c, r):
                        wait(sp, num_ps, t - U)
                        sp.dma_start(qs[:, c, :, :], qT[:, :, t * P:(t + 1) * P] if isinstance(t, int) else qT[:, :, ds(t * P, P)]).then_inc(s_q[c], 16)

                    def load_x(t, c, r):
                        wait(sp, mixed, t - U)
                        sp.dma_start(xt[:, c, :], row(a["x"], t)).then_inc(s_xt[c], 16)

                    def by_node():
                        sp.wait_ge(s_mdw, 32)
                        sp.dma_start(md_win.rearrange("(j p d) m -> p j (d m)", p=P, d=DW), mdw[:, :, :]).then_inc(moves.sem, 16)
                        moves.expect(1)
                        moves.wait(sp)
                        sp.dma_start(mdg[:, :, :, :], md_win[0:NP, :].rearrange("(t p) (i h) -> p t i h", p=P, h=H)).then_inc(moves.sem, 16)
                        moves.expect(1)
                    pipeline(sp, NT, [(0, load_q), (2, load_x)], U, U, by_node)

                @block.gpsimd
                def _(pool):
                    for j in range(2):
                        pool.indirect_dma_start(mdw[:, j, :], None, md_rows.rearrange("(s d) m -> s (d m)", d=DW), at_row(last_step[:, j:j + 1])).then_inc(s_mdw, 16)
                    consts.wait(pool)

                    def biased(t, c, r):
                        wait(pool, h_sb, t - 2)
                        pool.tensor_tensor(nb[:, c % 2, :], tile(xna, t, 0, D), bo_[:, :], ALU.add).then_inc(nb_in.sem, 1)

                    def with_bias(t, c, r):
                        pool.wait_ge(s_xt[c], (r + 1) * 16)
                        pool.tensor_tensor(xt[:, c, :], xt[:, c, :], bob[:, :], ALU.add).then_inc(xt_in.sem, 1)

                    def scaled(t, c, r):
                        wait(pool, h_sb, t)
                        wait(pool, mixed, t - 2)
                        pool.tensor_tensor(hw[:, c % 2, :], hh[:, c % 2, :], wn2[:, :], ALU.mult).then_inc(hw_in.sem, 1)
                    pipeline(pool, NT, [(1, biased), (2, scaled), (2, with_bias)], U, U)

                @block.tensor
                def _(pe):
                    consts.wait(pe)

                    def num(t, c, r):
                        pe.wait_ge(s_q[c], (r + 1) * 16)
                        wait(pe, on_sb, t - 2)
                        for g in range(KD):
                            mm = pe.matmul(pN[c % 2][:, g * (P + 4):(g + 1) * (P + 4)], qs[:, c, g, :], kvd[:, g, :], start=True, stop=True)
                        mm.then_inc(num_ps.sem, 1)

                    def turn(t, c, r):
                        wait(pe, on_sb, t)
                        wait(pe, onT_sb, t - 2)
                        for k in range(KD):
                            mm = pe.transpose(pT[c % 2][:, k * P:(k + 1) * P], on[:, c % 2, k * P:(k + 1) * P], ident)
                        mm.then_inc(onT_ps.sem, 1)

                    def out_proj(t, c, r):
                        wait(pe, onT_sb, t)
                        wait(pe, h_sb, t - 2)
                        for k in range(KD):
                            mm = pe.matmul(pH[c % 2][:, 0:D], onT[:, c % 2, k, :], wo[:, k, :], start=(k == 0), stop=(k == KD - 1))
                        mm.then_inc(h_ps.sem, 1)
                    pipeline(pe, NT, [(0, num), (2, out_proj), (1, turn)], U, U)

                @block.scalar
                def _(act):
                    def copy_t(t, c, r):
                        wait(act, onT_ps, t)
                        wait(act, h_ps, t - 2)
                        act.activation(onT[:, c % 2, :, :], pT[c % 2][:, 0:D].rearrange("p (k f) -> p k f", k=KD), ACT.Copy).then_inc(onT_sb.sem, 1)

                    def rms_of(t, c, r):
                        wait(act, h_sb, t)
                        wait(act, mixed, t - 2)
                        wait(act, rms, t - 1)
                        act.activation(sq[:, :], hh[:, c % 2, :], ACT.Square, accum_out=ms[:, c % 2, 0:1]).then_inc(rms.sem, 1)
                        wait(act, rms, t, 1)
                        act.activation(ms[:, c % 2, 1:2], ms[:, c % 2, 0:1], ACT.Sqrt, scale=1.0 / D, bias=eps[:, 1:2]).then_inc(rms.sem, 1)

                    def weigh_loops():
                        act.wait_ge(al_in, 1)
                        act.activation(es[:, 2:4, :, :], es[:, 2:4, :, :], ACT.Exp).then_inc(al_ex, 1)
                    pipeline(act, NT, [(2, rms_of), (1, copy_t)], U, U + 1, weigh_loops)

                @block.vector
                def _(dve):
                    z_of = lambda c: pN[c % 2][:, 0:KD * (P + 4)].rearrange("p (g n) -> p g n", g=KD)

                    def z_sum(t, c, r):
                        wait(dve, num_ps, t)
                        wait(dve, onT_ps, t - 2)
                        dve.tensor_scalar(rz[:, c % 2, 0:QH].rearrange("p (g b) -> p g b", g=KD), z_of(c)[:, :, P:P + 4], ATT_EPS, None, ALU.add).then_inc(on_sb.sem, 1)

                    def z_inverse(t, c, r):
                        wait(dve, on_sb, t, 1)
                        dve.reciprocal(rz[:, c % 2, QH:2 * QH], rz[:, c % 2, 0:QH]).then_inc(on_sb.sem, 1)

                    def divide(t, c, r):
                        wait(dve, on_sb, t, 2)
                        for g in range(KD):
                            ins = dve.tensor_tensor(on[:, c % 2, g * P:(g + 1) * P].rearrange("p (b m) -> p b m", m=HD), z_of(c)[:, g, 0:P].rearrange("p (b m) -> p b m", m=HD),
                                                    rz[:, c % 2, QH + g * 4:QH + g * 4 + 4].unsqueeze(2).to_broadcast([P, 4, HD]), ALU.mult)
                        ins.then_inc(on_sb.sem, 1)

                    def residual(t, c, r):
                        wait(dve, h_ps, t)
                        wait(dve, nb_in, t)
                        wait(dve, hw_in, t - 2)
                        wait(dve, rms, t - 2)
                        dve.tensor_tensor(hh[:, c % 2, :], pH[c % 2][:, 0:D], nb[:, c % 2, :], ALU.add).then_inc(h_sb.sem, 1)

                    def rms_inverse(t, c, r):
                        wait(dve, rms, t)
                        dve.reciprocal(ms[:, c % 2, 1:2], ms[:, c % 2, 1:2]).then_inc(mixed.sem, 1)

                    def normed_sum(t, c, r):
                        wait(dve, mixed, t, 1)
                        wait(dve, hw_in, t)
                        dve.scalar_tensor_tensor(out=hw[:, c % 2, :], in0=hw[:, c % 2, :], scalar=ms[:, c % 2, 1:2], in1=hh[:, c % 2, :], op0=ALU.mult, op1=ALU.add).then_inc(mixed.sem, 1)

                    def with_x(t, c, r):
                        wait(dve, mixed, t, 2)
                        wait(dve, xt_in, t)
                        dve.tensor_tensor(tile(x2, t, 0, D), hw[:, c % 2, :], xt[:, c, :], ALU.add).then_inc(mixed.sem, 1)

                    def loops():
                        line = v_chain.on(dve)
                        moves.wait(dve)
                        line.do(dve.tensor_tensor(es[:, 0, :, :], xna[:, :, AS:AS + H], ad[:, :, :], ALU.add))
                        line.do(dve.scalar_tensor_tensor(out=es[:, 0, :, :], in0=es[:, 0, :, :], scalar=0.2, in1=es[:, 0, :, :], op0=ALU.mult, op1=ALU.max))
                        line.do(dve.tensor_tensor(es[:, 1, :, :], es[:, 0, :, :], mdg[:, :, 0, :], ALU.max))
                        dve.tensor_tensor(es[:, 2, :, :], mdg[:, :, 0, :], es[:, 1, :, :], ALU.subtract)
                        dve.tensor_tensor(es[:, 3, :, :], es[:, 0, :, :], es[:, 1, :, :], ALU.subtract).then_inc(al_in, 1)
                        dve.wait_ge(al_ex, 1)
                        line.do(dve.tensor_tensor(es[:, 0, :, :], es[:, 2, :, :], mdg[:, :, 1, :], ALU.mult))
                        line.do(dve.tensor_tensor(es[:, 0, :, :], es[:, 0, :, :], es[:, 3, :, :], ALU.add))
                        line.do(dve.reciprocal(es[:, 1, :, :], es[:, 0, :, :]))
                        line.do(dve.tensor_tensor(es[:, 1, :, :], es[:, 1, :, :], gw[:, :].unsqueeze(1).to_broadcast([P, NT, H]), ALU.mult))
                        for i in range(2):
                            line.do(dve.tensor_tensor(al[:, i, :, :], es[:, 1, :, :], es[:, 2 + i, :, :], ALU.mult))
                    pipeline(dve, NT, [(0, z_sum), (4, rms_inverse), (0, z_inverse), (4, normed_sum), (0, divide), (4, with_x), (2, residual)], U, U, loops)

        with ExitStack() as ctx:
            lr = sb("lr", [P, 2], U32, ctx)
            AG = sb("AG", [P, 2, H, D], ctx=ctx)
            own = sb("own", [P, 2, H, D], ctx=ctx)
            aT = sb("aT", [P, 2, H * KD, P], ctx=ctx)
            betb = sb("betb", [P, D], ctx=ctx)
            gtw = sb("gtw", [P, KD, E], ctx=ctx)
            gtb = sb("gtb", [P, E], ctx=ctx)
            xg = sb("xg", [P, 2, D], ctx=ctx)
            xo = sb("xo", [P, 2, D], ctx=ctx)
            res = sb("res", [P, 2, D], ctx=ctx)
            st = sb("st", [P, 2, 2, 8], ctx=ctx)
            nT = sb("nT", [P, 2, KD, P], ctx=ctx)
            yt = sb("yt", [P, 2, D], ctx=ctx)
            yT = sb("yT", [P, 2, KD, P], ctx=ctx)
            pA = [ps(ctx, f"pa{i}") for i in range(4)]
            pW, pG, pX, pY = ps(ctx, "pW_"), ps(ctx, "pG_"), ps(ctx, "pX_"), ps(ctx, "pY_")
            consts.expect(3)
            s_AG, s_xo = [sem(f"s_AG{c}") for c in range(2)], [sem(f"s_xo{c}") for c in range(2)]
            lr_in, own_in, agg_in, aT_ps = Count(sem("lr_in")), Count(sem("own_in")), Count(sem("agg_in")), Count(sem("aT_ps"), 4)
            aT_a, aT_v, w_ps = Count(sem("aT_a"), 2), Count(sem("aT_v"), 2), Count(sem("w_ps"))
            nT_ps, nT_sb, g_ps, yT_ps, yT_sb = (Count(sem(n)) for n in ("nT_ps", "nT_sb", "g_ps", "yT_ps", "yT_sb"))
            lg_ps, lg_in, xg_in, xo_in, y_kept = (Count(sem(n)) for n in ("lg_ps", "lg_in", "xg_in", "xo_in", "y_kept"))

            def norm_counts(name):
                return [Count(sem(name + "_sum")), Count(sem(name + "_mom"), 2), Count(sem(name + "_std")), Count(sem(name + "_inv")), Count(sem(name + "_out"))]
            r_sum, r_mom, r_std, r_inv, r_out = r_norm = norm_counts("res")
            y_sum, y_mom, y_std, y_inv, y_out = y_norm = norm_counts("y")
            with nc.Block() as block:
                @block.sync
                def _(sp):
                    sp.dma_start(betb[:, :], a["ffn_beta"].partition_broadcast(P)).then_inc(consts.sem, 16)
                    sp.dma_start(gtw[:, :, :], a["ffn_gate_w"].rearrange("(k p) n -> p k n", p=P)).then_inc(consts.sem, 16)
                    sp.dma_start(gtb[:, :], a["ffn_gate_b"].partition_broadcast(P)).then_inc(consts.sem, 16)

                    def store(t, c, r):
                        wait(sp, xo_in, t)
                        sp.dma_start(row(x2_rows, t), xo[:, c, :]).then_inc(s_xo[c], 16)
                    pipeline(sp, NT, [(0, store)])
                    for c in range(2):
                        sp.wait_ge(s_xo[c], 16 * len(range(c, NT, 2)))

                @block.gpsimd
                def _(pool):
                    def gather(t, c, r):
                        wait(pool, agg_in, t - 2)
                        pool.sem_inc(s_gate, 1)
                        pool.tensor_copy(lr[:, c:c + 1], col(last_row, t)).then_inc(lr_in.sem, 1)
                        wait(pool, lr_in, t)
                        pool.sem_inc(s_gate, 1)
                        pool.indirect_dma_start(AG[:, c, :, :].rearrange("p h f -> p (h f)"), None,
                                                agg_rows.rearrange("s (d h) f -> (s d) (h f)", h=H), at_row(lr[:, c:c + 1])).then_inc(s_AG[c], 16)

                    def with_bias(t, c, r):
                        wait(pool, r_sum, t - 2)
                        pool.tensor_tensor(xg[:, c, :], tile(xna, t, 0, D), gwb[:, :], ALU.add).then_inc(xg_in.sem, 1)

                    def with_beta(t, c, r):
                        if isinstance(t, int) and t == 0:
                            consts.wait(pool)
                        wait(pool, y_sum, t)
                        if not isinstance(r, int) or r > 0:
                            pool.wait_ge(s_xo[c], r * 16)
                        pool.tensor_tensor(xo[:, c, :], tile(x2, t, 0, D), betb[:, :], ALU.add).then_inc(xo_in.sem, 1)
                    pipeline(pool, NT, [(0, gather), (3, with_bias), (6, with_beta)])

                @block.scalar
                def _(act):
                    def own_rows(t, c, r):
                        wait(act, agg_in, t - 2)
                        wait(act, aT_ps, t - 2)
                        act.sem_inc(s_gate, 1)
                        for h in range(H):
                            ins = act.activation(own[:, c, h, :], tile(xna, t, 0, D), ACT.Copy, scale=al[:, 1, t, h:h + 1] if isinstance(t, int) else al[:, 1, ds(t, 1), h:h + 1].rearrange("p t h -> p (t h)"))
                        ins.then_inc(own_in.sem, 1)

                    def copy_a(t, c, r):
                        for i in range(2):
                            wait(act, aT_ps, t, 2 * i + 1)
                            wait(act, w_ps, t - 2)
                            act.activation(aT[:, c, 8 * i:8 * i + 4, :], pA[2 * i][:, :].rearrange("p (k f) -> p k f", k=4), ACT.Copy).then_inc(aT_a.sem, 1)

                    def root(i, counts):
                        def stage(t, c, r):
                            wait(act, counts[1], t)
                            act.activation(st[:, c, i, 7:8], st[:, c, i, 7:8], ACT.Sqrt, bias=eps[:, 0:1]).then_inc(counts[2].sem, 1)
                        return stage

                    def copy_n(t, c, r):
                        wait(act, nT_ps, t)
                        wait(act, g_ps, t - 2)
                        act.activation(nT[:, c, :, :], pX[:, 0:D].rearrange("p (k f) -> p k f", k=KD), ACT.Copy).then_inc(nT_sb.sem, 1)

                    def copy_y(t, c, r):
                        wait(act, yT_ps, t)
                        wait(act, lg_ps, t - 2)
                        act.activation(yT[:, c, :, :], pY[:, 0:D].rearrange("p (k f) -> p k f", k=KD), ACT.Copy).then_inc(yT_sb.sem, 1)

                    def keep_y(t, c, r):
                        wait(act, y_out, t)
                        act.sem_inc(s_gate, 1)
                        act.activation(tile(y_all, t, 0, D), yt[:, c, :], ACT.Copy).then_inc(y_kept.sem, 1)
                    pipeline(act, NT, [(4, root(0, r_norm)), (5, root(1, y_norm)), (2, copy_a), (4, copy_n), (5, keep_y), (5, copy_y), (0, own_rows)])

                @block.tensor
                def _(pe):
                    consts.wait(pe)

                    def turn_a(t, c, r):
                        wait(pe, agg_in, t)
                        for i in range(4):
                            wait(pe, (aT_a, aT_v)[i % 2], t - 1, i // 2 + 1)
                            for k in range(4):
                                n = 4 * i + k
                                mm = pe.transpose(pA[i][:, k * P:(k + 1) * P], own[:, c, n // KD, (n % KD) * P:(n % KD + 1) * P], ident)
                            mm.then_inc(aT_ps.sem, 1)

                    def weigh(lo, hi):
                        def stage(t, c, r):
                            if lo == 0:
                                wait(pe, r_sum, t - 1)
                            for i in range(lo, hi):
                                wait(pe, (aT_a, aT_v)[i % 2], t, i // 2 + 1)
                                for k in range(4):
                                    n = 4 * i + k
                                    mm = pe.matmul(pW[:, 0:D], aT[:, c, n, :], W[:, n % KD, n // KD, :], start=(n == 0), stop=(n == H * KD - 1))
                            if hi == 4:
                                mm.then_inc(w_ps.sem, 1)
                        return stage

                    def turn_n(t, c, r):
                        wait(pe, r_out, t)
                        wait(pe, nT_sb, t - 1)
                        for k in range(KD):
                            mm = pe.transpose(pX[:, k * P:(k + 1) * P], res[:, c, k * P:(k + 1) * P], ident)
                        mm.then_inc(nT_ps.sem, 1)

                    def project(t, c, r):
                        wait(pe, nT_sb, t)
                        wait(pe, y_sum, t - 1)
                        for k in range(KD):
                            mm = pe.matmul(pG[:, 0:D], nT[:, c, k, :], WoT[:, k, :], start=(k == 0), stop=(k == KD - 1))
                        mm.then_inc(g_ps.sem, 1)

                    def turn_y(t, c, r):
                        wait(pe, y_out, t)
                        wait(pe, lg_in, t - 1)
                        for k in range(KD):
                            mm = pe.transpose(pY[:, k * P:(k + 1) * P], yt[:, c, k * P:(k + 1) * P], ident)
                        mm.then_inc(yT_ps.sem, 1)

                    def gate(t, c, r):
                        wait(pe, yT_sb, t)
                        for k in range(KD):
                            mm = pe.matmul(pY[:, D:D + E], yT[:, c, k, :], gtw[:, k, :], start=(k == 0), stop=(k == KD - 1))
                        mm.then_inc(lg_ps.sem, 1)
                    pipeline(pe, NT, [(2, turn_a), (6, gate), (3, weigh(0, 2)), (4, turn_n), (5, turn_y), (3, weigh(2, 4)), (4, project)])

                @block.vector
                def _(dve):
                    def neighbours(lo, hi):
                        def stage(t, c, r):
                            if lo == 0:
                                dve.wait_ge(s_AG[c], (r + 1) * 16)
                                wait(dve, own_in, t)
                            for h in range(lo, hi):
                                ins = dve.scalar_tensor_tensor(out=own[:, c, h, :], in0=AG[:, c, h, :], scalar=al[:, 0, t, h:h + 1] if isinstance(t, int) else al[:, 0, ds(t, 1), h:h + 1].rearrange("p t h -> p (t h)"),
                                                               in1=own[:, c, h, :], op0=ALU.mult, op1=ALU.add)
                            if hi == H:
                                ins.then_inc(agg_in.sem, 1)
                        return stage

                    def copy_a(t, c, r):
                        for i in range(2):
                            wait(dve, aT_ps, t, 2 * i + 2)
                            wait(dve, w_ps, t - 2)
                            dve.tensor_copy(aT[:, c, 8 * i + 4:8 * i + 8, :], pA[2 * i + 1][:, :].rearrange("p (k f) -> p k f", k=4)).then_inc(aT_v.sem, 1)

                    def residual(t, c, r):
                        wait(dve, w_ps, t)
                        wait(dve, xg_in, t)
                        wait(dve, nT_ps, t - 2)
                        dve.tensor_tensor(res[:, c, :], pW[:, 0:D], xg[:, c, :], ALU.add).then_inc(r_sum.sem, 1)

                    def node_out(t, c, r):
                        wait(dve, g_ps, t)
                        dve.tensor_tensor(tile(x2, t, 0, D), pG[:, 0:D], tile(x2, t, 0, D), ALU.add).then_inc(y_sum.sem, 1)

                    source = lambda i, t, c: tile(x2, t, 0, D) if i else res[:, c, :]

                    def stats(i, counts):
                        def stage(t, c, r):
                            wait(dve, counts[0], t)
                            dve.sem_inc(s_gate, 1)
                            dve.bn_stats(st[:, c, i, 0:6], source(i, t, c)).then_inc(counts[1].sem, 1)
                        return stage

                    def moments(i, counts):
                        def stage(t, c, r):
                            wait(dve, counts[1], t, 1)
                            dve.sem_inc(s_gate, 1)
                            dve.bn_aggr(st[:, c, i, 6:8], st[:, c, i, 0:6]).then_inc(counts[1].sem, 1)
                        return stage

                    def inverse(i, counts):
                        def stage(t, c, r):
                            wait(dve, counts[2], t)
                            dve.reciprocal(st[:, c, i, 7:8], st[:, c, i, 7:8]).then_inc(counts[3].sem, 1)
                        return stage

                    def normalise(i, counts):
                        def stage(t, c, r):
                            wait(dve, counts[3], t)
                            if i:
                                wait(dve, yT_ps, t - 2)
                                wait(dve, y_kept, t - 2)
                            dve.tensor_scalar(yt[:, c, :] if i else res[:, c, :], source(i, t, c), st[:, c, i, 6:7], st[:, c, i, 7:8],
                                              ALU.subtract, ALU.mult).then_inc(counts[4].sem, 1)
                        return stage

                    def logits(t, c, r):
                        wait(dve, lg_ps, t)
                        dve.tensor_tensor(tile(lg, t, 0, E), pY[:, D:D + E], gtb[:, :], ALU.add).then_inc(lg_in.sem, 1)
                    pipeline(dve, NT, [(4, residual), (5, node_out), (4, stats(0, r_norm)), (5, stats(1, y_norm)), (4, moments(0, r_norm)), (5, moments(1, y_norm)),
                                       (1, neighbours(0, 3)), (4, inverse(0, r_norm)), (5, inverse(1, y_norm)), (4, normalise(0, r_norm)), (5, normalise(1, y_norm)),
                                       (6, logits), (2, copy_a), (1, neighbours(3, H))])

        node_ctx.close()
        slot = sb("slot", [P, 2, NT], U32)
        wts = sb("wts", [P, 2, NT])
        expert_of = sb("expert_of", [1, TILES], I32)
        experts_ctx = ExitStack()
        w1 = sb("w1", [P, E, KD, F], ctx=experts_ctx)
        w2 = sb("w2", [P, E, FK, D], ctx=experts_ctx)
        b1 = sb("b1", [P, E, FK], ctx=experts_ctx)
        b2 = sb("b2", [P, E, D], ctx=experts_ctx)
        s_we = sem("s_we")
        with ExitStack() as ctx:
            iota = iota16.unsqueeze(1).to_broadcast([P, NT, E])
            O = sb("O", [P, 3, NT, E], ctx=ctx)
            T = sb("T", [P, 2, NT, E], ctx=ctx)
            m = sb("m", [P, 6, NT], ctx=ctx)
            cn = sb("cn", [P, E, NT], ctx=ctx)
            keep = sb("keep", [P, E, NT], ctx=ctx)
            pairs = sb("pairs", [P, E, NT], ctx=ctx)
            te = sb("te", [P, 4, E], ctx=ctx)
            ti = sb("ti", [P, E], I32, ctx)
            tj = sb("tj", [1, TILES, E + 1], ctx=ctx)
            jn = sb("jn", [1, TILES], ctx=ctx)
            pR, pC = ps(ctx, "pR"), ps(ctx, "pC")
            a_rt, rt_ps, slots_in, s_sc = sem("a_rt"), sem("rt_ps"), sem("slots_in"), sem("s_sc")
            m_in, o_in = sem("m_in"), sem("o_in")
            consts.expect(1)
            with nc.Block() as block:
                @block.sync
                def _(sp):
                    sp.dma_start(jn[:, :], a["tile_no"][:, :]).then_inc(consts.sem, 16)
                    sp.dma_start(b1[:, :, :], a["ffn_b1"][:, :, :]).then_inc(s_we, 16)
                    sp.dma_start(b2[:, :, :], a["ffn_b2"].partition_broadcast(P)).then_inc(s_we, 16)
                    for e in range(E):
                        sp.dma_start(w1[:, e, :, :], a["ffn_w1"][e, :, :].rearrange("(k p) f -> p k f", p=P)).then_inc(s_we, 16)
                        sp.dma_start(w2[:, e, :, :], a["ffn_w2"][e, :, :].rearrange("(k p) f -> p k f", p=P)).then_inc(s_we, 16)

                @block.vector
                def _(dve):
                    line = v_chain.on(dve)
                    line.do(dve.memset(keep[:, :, :], 1.0))
                    dve.memset(keep[:, :, 0:1], 0.0)
                    left = lg
                    for k in range(2):
                        line.do(dve.tensor_reduce(m[:, k, :], left[:, :, :], AX.X, ALU.max))
                        line.do(dve.tensor_tensor(T[:, 0, :, :], left[:, :, :], m[:, k, :].unsqueeze(2).to_broadcast([P, NT, E]), ALU.not_equal))
                        line.do(dve.scalar_tensor_tensor(out=T[:, 0, :, :], in0=T[:, 0, :, :], scalar=float(E), in1=iota, op0=ALU.mult, op1=ALU.add))
                        line.do(dve.tensor_reduce(m[:, 2, :], T[:, 0, :, :], AX.X, ALU.min))
                        line.do(dve.tensor_tensor(O[:, k, :, :], iota, m[:, 2, :].unsqueeze(2).to_broadcast([P, NT, E]), ALU.is_equal))
                        if k == 0:
                            line.do(dve.scalar_tensor_tensor(out=T[:, 1, :, :], in0=O[:, 0, :, :], scalar=-3e38, in1=lg[:, :, :], op0=ALU.mult, op1=ALU.add))
                            left = T[:, 1, :, :]
                    dve.tensor_tensor(m[:, 3, :], m[:, 1, :], m[:, 0, :], ALU.subtract).then_inc(m_in, 1)
                    dve.tensor_tensor(O[:, 2, :, :], O[:, 0, :, :], O[:, 1, :, :], ALU.add).then_inc(o_in, 1)
                    dve.wait_ge(a_rt, 1)
                    line.do(dve.tensor_scalar(m[:, 4, :], m[:, 3, :], 1.0, None, ALU.add))
                    line.do(dve.reciprocal(wts[:, 0, :], m[:, 4, :]))
                    line.do(dve.tensor_tensor(wts[:, 1, :], wts[:, 0, :], m[:, 3, :], ALU.mult))
                    dve.wait_ge(rt_ps, 2)
                    line.do(dve.tensor_copy(pairs[:, :, :], pC[:, 0:NT * E].rearrange("p (t e) -> p e t", e=E)))
                    line.do(dve.tensor_tensor_scan(cn[:, :, :].rearrange("p e t -> p (e t)"), keep[:, :, :].rearrange("p e t -> p (e t)"), pairs[:, :, :].rearrange("p e t -> p (e t)"), 0.0, ALU.mult, ALU.add))
                    line.do(dve.tensor_scalar(ti[:, :], cn[:, :, NT - 1], float(P - 1), None, ALU.add))
                    line.do(dve.tensor_scalar(ti[:, :], ti[:, :], 7, None, ALU.arith_shift_right))
                    line.do(dve.tensor_copy(te[:, 0, :], ti[:, :]))
                    line.do(dve.tensor_tensor_scan(te[:, 1, :], ones[:, 0:E], te[:, 0, :], 0.0, ALU.mult, ALU.add))
                    line.do(dve.tensor_tensor(te[:, 2, :], te[:, 1, :], te[:, 0, :], ALU.subtract))
                    line.do(dve.tensor_scalar(te[:, 2, :], te[:, 2, :], float(P), None, ALU.mult))
                    line.do(dve.tensor_tensor(T[:, 0, 1:, :], cn[:, :, 0:NT - 1].rearrange("p e t -> p t e"), pR[:, E:NT * E].rearrange("p (t e) -> p t e", e=E), ALU.add))
                    line.do(dve.tensor_copy(T[:, 0, 0:1, :], pR[:, 0:E].rearrange("p (t e) -> p t e", e=E)))
                    line.do(dve.tensor_tensor(T[:, 0, :, :], T[:, 0, :, :], te[:, 2, :].unsqueeze(1).to_broadcast([P, NT, E]), ALU.add))
                    for k in range(2):
                        line.do(dve.tensor_tensor(T[:, 1, :, :], T[:, 0, :, :], O[:, k, :, :], ALU.mult))
                        line.do(dve.tensor_reduce(m[:, 5, :], T[:, 1, :, :], AX.X, ALU.add))
                        dve.tensor_copy(slot[:, k, :], m[:, 5, :]).then_inc(slots_in, 1)
                    consts.wait(dve)
                    line.do(dve.tensor_tensor(tj[:, :, 0:E], te[0:1, 1, :].unsqueeze(1).to_broadcast([1, TILES, E]), jn[:, :].unsqueeze(2).to_broadcast([1, TILES, E]), ALU.is_le))
                    line.do(dve.tensor_reduce(tj[:, :, E], tj[:, :, 0:E], AX.X, ALU.add))
                    line.do(dve.tensor_scalar(expert_of[:, :], tj[:, :, E], float(E - 1), None, ALU.min))

                @block.scalar
                def _(act):
                    act.wait_ge(m_in, 1)
                    act.activation(m[:, 3, :], m[:, 3, :], ACT.Exp).then_inc(a_rt, 1)

                @block.tensor
                def _(pe):
                    pe.wait_ge(o_in, 1)
                    pe.matmul(pR[:, 0:NT * E], tri, O[:, 2, :, :].rearrange("p t e -> p (t e)"), start=True, stop=True).then_inc(rt_ps, 1)
                    pe.matmul(pC[:, 0:NT * E], ones, O[:, 2, :, :].rearrange("p t e -> p (t e)"), start=True, stop=True).then_inc(rt_ps, 1)

                @block.gpsimd
                def _(pool):
                    for k in range(2):
                        pool.wait_ge(slots_in, k + 1)
                        for t in range(NT):
                            pool.indirect_dma_start(xs_rows[:, :], at_row(slot[:, k, t:t + 1]), y_all[:, t, :], None).then_inc(s_sc, 16)
                    pool.wait_ge(s_sc, 2 * 16 * NT)

        with ExitStack() as ctx:
            U = 6
            S3 = 3
            xe = sb("xe", [P, S3, D], ctx=ctx)
            xeT = sb("xeT", [P, 2, KD, P], ctx=ctx)
            w1e = sb("w1e", [P, 2, KD, F], ctx=ctx)
            hT = sb("hT", [P, 2, FK, P], ctx=ctx)
            ye = sb("ye", [P, 2, D], ctx=ctx)
            pX = [ps(ctx, f"pXe{c}") for c in range(2)]
            pH = [ps(ctx, f"pHe{c}") for c in range(2)]
            pY = [ps(ctx, f"pYe{c}") for c in range(2)]
            s_xe = [sem(f"s_xe{c}") for c in range(S3)]
            s_ye = [sem(f"s_ye{c}") for c in range(2)]
            xeT_ps, xeT_sb, w1_in, he_ps = (Count(sem(n)) for n in ("xeT_ps", "xeT_sb", "w1_in", "he_ps"))
            he_sb, ye_ps, ye_sb = (Count(sem(n)) for n in ("he_sb", "ye_ps", "ye_sb"))

            def nth(c, r, slots):
                return r * (U // slots) + c // slots

            def expert(eng, j):
                return eng.value_load(expert_of[0:1, j:j + 1] if isinstance(j, int) else expert_of[0:1, ds(j, 1)], min_val=0, max_val=E - 1)

            def of_expert(T, e, k):
                return T[:, ds(e, 1), k, :].rearrange("p e n -> p (e n)")

            with nc.Block() as block:
                @block.sync
                def _(sp):
                    def load(j, c, r):
                        wait(sp, xeT_ps, j - S3)
                        sp.dma_start(xe[:, c % S3, :], row(xs_rows, j)).then_inc(s_xe[c % S3], 16)
                    pipeline(sp, TILES, [(0, load)], U, S3)

                @block.tensor
                def _(pe):
                    pe.wait_ge(s_we, 16 * (2 * E + 2))

                    def turn(j, c, r):
                        pe.wait_ge(s_xe[c % S3], (nth(c, r, S3) + 1) * 16)
                        wait(pe, xeT_sb, j - 2)
                        for k in range(KD):
                            mm = pe.transpose(pX[c % 2][:, k * P:(k + 1) * P], xe[:, c % S3, k * P:(k + 1) * P], ident)
                        mm.then_inc(xeT_ps.sem, 1)

                    def hidden(j, c, r):
                        wait(pe, w1_in, j)
                        wait(pe, xeT_sb, j)
                        wait(pe, he_sb, j - 2)
                        for f in range(FK):
                            for k in range(KD):
                                mm = pe.matmul(pH[c % 2][:, f * P:(f + 1) * P], w1e[:, c % 2, k, f * P:(f + 1) * P], xeT[:, c % 2, k, :], start=(k == 0), stop=(k == KD - 1))
                        mm.then_inc(he_ps.sem, 1)

                    def output(j, c, r):
                        e = expert(pe, j)
                        wait(pe, he_sb, j)
                        wait(pe, ye_sb, j - 2)
                        pe.sem_inc(s_gate, 1)
                        for f in range(FK):
                            mm = pe.matmul(pY[c % 2][:, 0:D], hT[:, c % 2, f, :], of_expert(w2, e, f), start=(f == 0), stop=(f == FK - 1))
                        mm.then_inc(ye_ps.sem, 1)
                    pipeline(pe, TILES, [(1, hidden), (0, turn), (2, output)], U, S3)

                @block.scalar
                def _(act):
                    act.wait_ge(s_we, 16 * (2 * E + 2))

                    def relu(j, c, r):
                        e = expert(act, j)
                        wait(act, he_ps, j)
                        wait(act, ye_ps, j - 2)
                        act.sem_inc(s_gate, 1)
                        for f in range(FK):
                            ins = act.activation(hT[:, c % 2, f, :], pH[c % 2][:, f * P:(f + 1) * P], ACT.Relu,
                                                 bias=b1[:, ds(e, 1), f:f + 1].rearrange("p e f -> p (e f)"))
                        ins.then_inc(he_sb.sem, 1)
                    pipeline(act, TILES, [(0, relu)], U, S3)

                @block.vector
                def _(dve):
                    dve.wait_ge(s_we, 16 * (2 * E + 2))

                    def copy_x(j, c, r):
                        wait(dve, xeT_ps, j)
                        wait(dve, he_ps, j - 2)
                        dve.tensor_copy(xeT[:, c % 2, :, :], pX[c % 2][:, 0:D].rearrange("p (k f) -> p k f", k=KD)).then_inc(xeT_sb.sem, 1)

                    def take_w1(j, c, r):
                        e = expert(dve, j)
                        wait(dve, he_ps, j - 2)
                        dve.sem_inc(s_gate, 1)
                        dve.tensor_copy(w1e[:, c % 2, :, :], w1[:, ds(e, 1), :, :].rearrange("p e k f -> p (e k) f")).then_inc(w1_in.sem, 1)

                    def add_b2(j, c, r):
                        e = expert(dve, j)
                        wait(dve, ye_ps, j)
                        if not isinstance(j, int) or j >= 2:
                            dve.wait_ge(s_ye[c % 2], nth(c, r, 2) * 16)
                        dve.sem_inc(s_gate, 1)
                        dve.tensor_tensor(ye[:, c % 2, :], pY[c % 2][:, 0:D], b2[:, ds(e, 1), :].rearrange("p e n -> p (e n)"), ALU.add).then_inc(ye_sb.sem, 1)
                    pipeline(dve, TILES, [(0, copy_x), (0, take_w1), (2, add_b2)], U, S3)

                @block.gpsimd
                def _(pool):
                    def store(j, c, r):
                        wait(pool, ye_sb, j)
                        pool.sem_inc(s_gate, 1)
                        pool.dma_start(row(ys_rows, j), ye[:, c % 2, :]).then_inc(s_ye[c % 2], 16)
                    pipeline(pool, TILES, [(0, store)], U, S3)
                    for c in range(2):
                        pool.wait_ge(s_ye[c], 16 * (TILES // 2))
        experts_ctx.close()

        with ExitStack() as ctx:
            U = 4
            g = sb("g", [P, U, 2, D], ctx=ctx)
            xb = sb("xb", [P, 2, D], ctx=ctx)
            v = sb("v", [P, U, D], ctx=ctx)
            o = sb("o", [P, 2, D], ctx=ctx)
            sf = sb("sf", [P, U, 8], ctx=ctx)
            gb = sb("gb", [P, D], ctx=ctx)
            s_g = [sem(f"s_g{c}") for c in range(U)]
            consts.expect(1)
            s_xb, s_out = [sem(f"s_xb{c}") for c in range(2)], [sem(f"s_out{c}") for c in range(2)]
            v_in, v_mom, v_sd, v_inv = Count(sem("v_in"), 2), Count(sem("v_mom"), 2), Count(sem("v_sd")), Count(sem("v_inv"))
            o_in = Count(sem("o_fin"), 2)

            def nth(c, r):
                return r * (U // 2) + c // 2

            with nc.Block() as block:
                @block.gpsimd
                def _(pool):
                    for t in range(NT):
                        wait(pool, v_in, t - U)
                        for k in range(2):
                            pool.indirect_dma_start(g[:, t % U, k, :], None, ys_rows[:, :], at_row(slot[:, k, t:t + 1])).then_inc(s_g[t % U], 16)

                @block.scalar
                def _(act):
                    def std(t, c, r):
                        wait(act, v_mom, t)
                        act.activation(sf[:, c, 7:8], sf[:, c, 7:8], ACT.Sqrt, bias=eps[:, 0:1]).then_inc(v_sd.sem, 1)
                    pipeline(act, NT, [(0, std)], U, U)

                @block.vector
                def _(dve):
                    consts.wait(dve)

                    def add_expert(k):
                        def stage(t, c, r):
                            if k == 0:
                                dve.wait_ge(s_g[c], (r + 1) * 32)
                            else:
                                wait(dve, v_in, t, 1)
                            w = wts[:, k, t:t + 1] if isinstance(t, int) else wts[:, k, ds(t, 1)]
                            dve.scalar_tensor_tensor(out=v[:, c, :], in0=g[:, c, k, :], scalar=w, in1=v[:, c, :] if k else tile(y_all, t, 0, D), op0=ALU.mult, op1=ALU.add).then_inc(v_in.sem, 1)
                        return stage

                    def stats(t, c, r):
                        wait(dve, v_in, t)
                        dve.sem_inc(s_gate, 1)
                        dve.bn_stats(sf[:, c, 0:6], v[:, c, :]).then_inc(v_mom.sem, 1)

                    def moments(t, c, r):
                        wait(dve, v_mom, t, 1)
                        dve.sem_inc(s_gate, 1)
                        dve.bn_aggr(sf[:, c, 6:8], sf[:, c, 0:6]).then_inc(v_mom.sem, 1)

                    def inverse(t, c, r):
                        wait(dve, v_sd, t)
                        dve.reciprocal(sf[:, c, 7:8], sf[:, c, 7:8]).then_inc(v_inv.sem, 1)

                    def scaled(t, c, r):
                        if not isinstance(t, int) or t >= 2:
                            dve.wait_ge(s_out[c % 2], nth(c, r) * 16)
                        wait(dve, v_mom, t)
                        dve.scalar_tensor_tensor(out=o[:, c % 2, :], in0=v[:, c, :], scalar=sf[:, c, 6:7], in1=gb[:, :], op0=ALU.subtract, op1=ALU.mult).then_inc(o_in.sem, 1)

                    def finish(t, c, r):
                        wait(dve, o_in, t, 1)
                        wait(dve, v_inv, t)
                        dve.wait_ge(s_xb[c % 2], (nth(c, r) + 1) * 16)
                        dve.scalar_tensor_tensor(out=o[:, c % 2, :], in0=o[:, c % 2, :], scalar=sf[:, c, 7:8], in1=xb[:, c % 2, :], op0=ALU.mult, op1=ALU.add).then_inc(o_in.sem, 1)
                    pipeline(dve, NT, [(0, add_expert(0)), (1, inverse), (1, scaled), (0, add_expert(1)), (1, finish), (0, stats), (0, moments)], U, U)

                @block.sync
                def _(sp):
                    sp.dma_start(gb[:, :], a["ffn_gamma"].partition_broadcast(P)).then_inc(consts.sem, 16)

                    def load(t, c, r):
                        wait(sp, o_in, t - 2)
                        sp.dma_start(xb[:, c % 2, :], row(x2_rows, t)).then_inc(s_xb[c % 2], 16)

                    def store(t, c, r):
                        wait(sp, o_in, t)
                        sp.dma_start(row(out, t), o[:, c % 2, :]).then_inc(s_out[c % 2], 16)
                    pipeline(sp, NT, [(2, store), (0, load)], U, U)
                    for c in range(2):
                        sp.wait_ge(s_out[c], 16 * len(range(c, NT, 2)))


def constants():
    import numpy as np
    p = np.arange(P)
    same_step = (p[:, None] // DW == np.arange(G)[None, :]).repeat(H, axis=1)
    same_window = p[:, None] % (P // DW) == p[None, :] // DW
    window_in_tile = (np.arange(2)[None, :, None] * P + p[:, None, None]) // (P // DW) == np.arange(NT)[None, None, :]
    window_in_tile = window_in_tile.reshape(P, 2 * NT)
    parts = [np.eye(P), p[:, None] < p[None, :], np.ones((P, P)), same_window, np.tile(np.arange(16), (P, 1)),
             p[:, None] + P * np.arange(SJ)[None, :], window_in_tile, (p % DW)[:, None], same_step]
    return np.concatenate([np.asarray(x, np.float32) for x in parts], axis=1)


def lay_out(inputs):
    import numpy as np
    g = {k: np.asarray(v) for k, v in inputs.items()}
    x = np.zeros((NP, D), g["x"].dtype)
    x[:N] = g["x"]
    src = np.zeros((CHUNKS * P,), g["src"].dtype)
    dst = np.full((CHUNKS * P,), DST_PAD, g["dst"].dtype)
    src[:NE], dst[:NE] = g["src"], g["dst"]
    a = {"x": x, "src_dst": np.concatenate([src.reshape(CHUNKS, P), dst.reshape(CHUNKS, P)], axis=1), "cst": constants(),
         "chunk_end": dst[P - 1::P][:CHUNKS - 1].reshape(1, -1), "chunk_no": np.arange(CHUNKS - 1, dtype=np.float32).reshape(1, -1)}
    for k, v in g.items():
        if k.startswith("L0_"):
            a[k.split("_", 2)[2] if k.split("_")[1] == "gnn" else k[3:]] = v
    for k in ("mix_w_norm1", "ln_gamma", "ln_beta"):
        a[k] = a[k].reshape(KD, P).T
    a["ffn_b1"] = a["ffn_b1"].reshape(E, FK, P).transpose(2, 0, 1)
    a["tile_no"] = np.arange(TILES, dtype=np.float32).reshape(1, -1)
    a["WoT"] = a.pop("Wo").T
    return {k: np.ascontiguousarray(v) for k, v in a.items()}


def kernel(**inputs):
    import concourse.bacc as _bacc
    from concourse.bass_utils import run_bass_kernel_spmd as _run
    nc = _bacc.Bacc("TRN2", target_bir_lowering=False, num_devices=1)
    arrays = lay_out(inputs)
    args = {k: nc.dram_tensor("in_" + k, v.shape, mybir.dt.from_np(v.dtype), kind="ExternalInput").ap()
            for k, v in arrays.items()}
    out = nc.dram_tensor("out", (NP, D), F32, kind="ExternalOutput").ap()
    build(nc, args, out, DEBUG)
    r = _run(nc, [{"in_" + k: v for k, v in arrays.items()}], core_ids=[0])
    return r.results[0]["out"][:N]


DEBUG = False
```

```python
from contextlib import ExitStack

import concourse.bass as bass
from concourse import mybir

P = 128
N, D, H = 3125, 256, 8
KD = D // P
NT = -(-N // P)
NP = NT * P
LAST = N - (NT - 1) * P
NE = 50000
CHUNKS = -(-NE // P)
DW = P // H
WINDOWS = -(-N // DW)
STEPS = CHUNKS + WINDOWS - 1
G = 8
GROUPS = -(-STEPS // G)
SJ = -(-(GROUPS * G) // P)
SP_ = SJ * P
ONE, AS = D, D + 1
RW = 272
DST_PAD = 4080
BIG = 1e30
QH = 8
HD = D // QH
E, F, FK = 16, 512, 512 // P
TILES = 2 * NP // P + E
SLOTS = TILES * P
PART = NP + P
REC = 2 * E + 4
LN_EPS, RMS_EPS, ATT_EPS = 1e-5, 1e-6, 1e-6

F32 = mybir.dt.float32
I32, U32 = mybir.dt.int32, mybir.dt.uint32
ALU = mybir.AluOpType
ACT = mybir.ActivationFunctionType
AX = mybir.AxisListType
ds = bass.ds


class Count:

    def __init__(self, sem, n=1, base=0):
        self.sem, self.n, self.base = sem, n, base

    def at(self, t, k=None):
        return self.base + t * self.n + (self.n if k is None else k)

    def again(self, tiles):
        return Count(self.sem, self.n, self.at(tiles - 1))


def wait(eng, count, t, k=None):
    v = count.at(t, k)
    if not isinstance(v, int) or v > 0:
        eng.wait_ge(count.sem, v)


def pipeline(eng, n, stages, U=2, extra=2, between=None):
    L = max(lag for lag, _ in stages)
    start = L + extra
    turns = (n - start) // U
    for tau in range(start):
        for lag, stage in stages:
            if 0 <= tau - lag < n:
                t = tau - lag
                stage(t, t % U, t // U)
    if between:
        between()
    with eng.Fori(0, turns) as i:
        for u in range(U):
            for lag, stage in stages:
                t = start + u - lag
                stage(i * U + t, t % U, i + t // U)
    for tau in range(start + turns * U, n + L):
        for lag, stage in stages:
            if 0 <= tau - lag < n:
                t = tau - lag
                stage(t, t % U, t // U)


def tile(T, t, lo, hi):
    return T[:, t, lo:hi] if isinstance(t, int) else T[:, ds(t, 1), lo:hi].rearrange("p t f -> p (t f)")


def col(T, t, n=1):
    return T[:, t * n:t * n + n] if isinstance(t, int) else T[:, ds(t * n, n)]


def row(T, t):
    return T[t * P:(t + 1) * P, :] if isinstance(t, int) else T[ds(t * P, P), :]


def at_row(ap):
    return bass.IndirectOffsetOnAxis(ap=ap, axis=0)


class Line:

    def __init__(self, sem):
        self.sem, self.n = sem, 0

    def on(self, eng):
        self.eng = eng
        return self

    def do(self, ins):
        ins.then_inc(self.sem, 1)
        self.n += 1
        self.eng.wait_ge(self.sem, self.n)


class Loads:

    def __init__(self, sem):
        self.sem, self.n = sem, 0

    def expect(self, n):
        self.n += n

    def wait(self, eng, but=0):
        eng.wait_ge(self.sem, 16 * (self.n - but))


def build(nc, a, out):
    with ExitStack() as top:
        def dram(name, shape, dt=F32):
            return nc.dram_tensor(name, shape, dt, kind="Internal").ap()

        def sb(name, shape, dt=F32, ctx=top):
            return ctx.enter_context(nc.sbuf_tensor(name, shape, dt))

        def ps(ctx, name, shape=(P, 512)):
            return ctx.enter_context(nc.psum_tensor(name, list(shape), F32))

        def sem(name):
            return top.enter_context(nc.semaphore(name))

        node_rows = dram("node_rows", (NP, RW))
        ad_rows = dram("ad_rows", (NP, H))
        x2_rows = dram("x2_rows", (NP, D))
        xs_rows, ys_rows = dram("xs_rows", (E * PART, D)), dram("ys_rows", (SLOTS, D))
        agg_rows = dram("agg_rows", (GROUPS * G, P, D))
        cst = sb("cst", [P, 4 * P + 16 + SJ + 2 * NT + 1 + G * H + 2 * E])
        ident, tri, ones, same_win = (cst[:, i * P:(i + 1) * P] for i in range(4))
        o = 4 * P
        iota16, step_no = cst[:, o:o + 16], cst[:, o + 16:o + 16 + SJ]
        o += 16 + SJ
        tile_win, dst_no = cst[:, o:o + 2 * NT].rearrange("p (j t) -> p j t", t=NT), cst[:, o + 2 * NT:o + 2 * NT + 1]
        o += 2 * NT + 1
        same_step = cst[:, o:o + G * H].rearrange("p (s h) -> p s h", h=H)
        o += G * H
        from_end, part_row = cst[:, o:o + E], cst[:, o + E:o + 2 * E]
        eps = sb("eps", [P, 3])
        last_row = sb("last_row", [P, NT], U32)
        last_step = sb("last_step", [P, 2], U32)
        picks = sb("picks", [P, NT, REC])
        used = sb("used", [P, E])
        both_y = sb("qT_y", [P, NT * D])
        qT = both_y.rearrange("p (k n) -> p k n", k=KD)
        y_all = both_y.rearrange("p (t f) -> p t f", f=D)
        node_ctx = ExitStack()
        xna = sb("xna", [P, NT, RW], ctx=node_ctx)
        ad = sb("ad", [P, NT, H], ctx=node_ctx)
        W = sb("W", [P, KD, H, D], ctx=node_ctx)
        kvd = sb("kvd", [P, KD, P + 4], ctx=node_ctx)
        gw = sb("gw", [P, H], ctx=node_ctx)
        WoT = sb("WoT", [P, KD, D], ctx=node_ctx)
        gwb = sb("gwb", [P, D], ctx=node_ctx)
        bob = sb("bob", [P, D], ctx=node_ctx)
        v_chain = Line(sem("v_chain"))
        consts = Loads(sem("consts_loaded"))
        moves = Loads(sem("sp_moved"))
        s_gate = sem("s_gate")

        edge_ctx = ExitStack()
        srcT = sb("srcT", [P, SP_], U32, edge_ctx)
        dlocT = sb("dlocT", [P, SP_], ctx=edge_ctx)
        resetT = sb("resetT", [P, SP_], ctx=edge_ctx)
        rowc = sb("rowc", [P, 2, SJ], U32, edge_ctx)
        with ExitStack() as ctx:
            C1 = CHUNKS - 1
            end_i = sb("end_i", [1, C1], I32, ctx)
            ends = sb("ends", [1, 3, C1], ctx=ctx)
            junk = sb("junk", [P, C1], ctx=ctx)
            cs = sb("cs", [P, 6, SJ], ctx=ctx)
            cnt = sb("cnt", [P, 2], ctx=ctx)
            by_tile = sb("by_tile", [P, 2, NT], ctx=ctx)
            gsd = sb("gsd", [P, SJ, 2, P], I32, ctx)
            tab = sb("tab", [P, SJ, 3, P], ctx=ctx)
            end_ready, ends_ps, rows_ready, steps_in, steps_ps = sem("end_ready"), sem("ends_ps"), sem("rows_ready"), sem("steps_in"), sem("steps_ps")
            s_gsd, tabs, tabs_ps = sem("s_gsd"), sem("tabs"), sem("tabs_ps")
            A = sb("att", [P, 2, H, D], ctx=ctx)
            tmpW = sb("tmpW", [P, 3, H, D], ctx=ctx)
            V = sb("V", [P, KD, 2 * H], ctx=ctx)
            wq = sb("wq", [P, KD, 3 * D], ctx=ctx)
            wn1 = sb("wn1", [P, KD], ctx=ctx)
            gmx = sb("gmx", [P, 2], ctx=ctx)
            st6 = sb("st6", [P, NT, 6], ctx=ctx)
            mean = sb("mean", [P, NT], ctx=ctx)
            var = sb("var", [P, NT], ctx=ctx)
            rs = sb("rs", [P, NT], ctx=ctx)
            rr = sb("rr", [P, NT], ctx=ctx)
            xs = sb("xs", [P, 2, D], ctx=ctx)
            xT = sb("xT", [P, 2, KD, P], ctx=ctx)
            ez = sb("ez", [P, 2, 2 * D], ctx=ctx)
            mz = sb("mz", [P, 2, 2 * D], ctx=ctx)
            qk = sb("qk", [P, 2, 2 * D], ctx=ctx)
            vv = sb("vv", [P, 2, KD, P + 1], ctx=ctx)
            pT = [ps(ctx, f"pT{c}") for c in range(2)]
            pQ = [ps(ctx, f"pQ{c}") for c in range(2)]
            pV = [ps(ctx, f"pV{c}") for c in range(2)]
            pq = ps(ctx, "pq")
            pK = ps(ctx, "pK")[:, 0:KD * (P + 1)].rearrange("p (g n) -> p g n", g=KD)
            s_W, s_att, s_wq = sem("s_W"), sem("s_att"), sem("s_wq")
            consts.expect(3)
            v_prod, a_wq = sem("v_prod"), sem("a_wq")
            s_x = [sem(f"s_x{j}") for j in range(5)]
            pE, pW = pT[0], pT[1]
            pj = [pT[0], pT[1], pQ[0], pQ[1], pV[0]]
            ones_in, v_W, v_gw, v_stat = sem("ones_in"), sem("v_W"), sem("v_gw"), sem("v_stat")
            a_gw, a_rs = sem("a_gw"), sem("a_rs")
            normed, copied, xT_ps, xT_sb = (Count(sem(n)) for n in ("normed", "copied", "xT_ps", "xT_sb"))
            qkv_ps, elu_e, v_sb = Count(sem("qkv_ps")), Count(sem("elu_e")), Count(sem("v_sb"), 2)
            qk_sb, a_sb, kv_done = Count(sem("qk_sb"), 2), Count(sem("a_sb"), 2), Count(sem("kv_done"))
            qT_ps, qT_sb = Count(sem("qT_ps")), Count(sem("qT_sb"))
            with nc.Block() as block:
                @block.sync
                def _(sp):
                    sp.dma_start(cst[:, :], a["cst"][:, :]).then_inc(consts.sem, 16)
                    sp.dma_start(end_i[:, :], a["chunk_end"][:, :]).then_inc(consts.sem, 16)
                    sp.dma_start(ends[:, 2, :], a["chunk_no"][:, :]).then_inc(consts.sem, 16)
                    consts.wait(sp)
                    for k in range(KD):
                        sp.dma_start(W[:, k, :, :], a["W"][:, k * P:(k + 1) * P, :].rearrange("h p d -> p h d")).then_inc(s_W, 16)
                    for j in range(5):
                        sp.dma_start(xna[:, 5 * j:5 * j + 5, 0:D],
                                     a["x"][5 * j * P:(5 * j + 5) * P, :].rearrange("(t p) f -> p t f", p=P)).then_inc(s_x[j], 16)
                    sp.wait_ge(ones_in, 1)

                    def store(t, c, r):
                        wait(sp, a_sb, t)
                        sp.sem_inc(s_gate, 1)
                        wait(sp, copied, t)
                        sp.sem_inc(s_gate, 1)
                        sp.dma_start(row(node_rows, t), tile(xna, t, 0, RW)).then_inc(moves.sem, 16)
                    pipeline(sp, NT, [(0, store)])
                    sp.dma_start(ad_rows.rearrange("(t p) h -> p t h", p=P), ad[:, :, :]).then_inc(moves.sem, 16)
                    moves.expect(NT + 1)
                    moves.wait(sp)

                @block.gpsimd
                def _(pool):
                    pool.memset(xna[:, :, AS + H:RW], 0.0)
                    pool.memset(xna[:, :, ONE:ONE + 1], 1.0).then_inc(ones_in, 1)
                    pool.wait_ge(rows_ready, 1)
                    for j in range(SJ):
                        pool.indirect_dma_start(gsd[:, j, :, :].rearrange("p i n -> p (i n)"), None, a["src_dst"][:, :], at_row(rowc[:, 0, j:j + 1])).then_inc(s_gsd, 16)
                    pool.wait_ge(s_W, 32)
                    pool.wait_ge(s_att, 32)
                    for i in range(2):
                        pool.tensor_tensor(tmpW[:, 1 + i, :, :], W[:, 1, :, :], A[:, i, :, :], ALU.mult).then_inc(v_prod, 1)

                @block.scalar
                def _(act):
                    consts.wait(act)
                    act.dma_start(A[:, 0, :, :], a["att_src"].partition_broadcast(P)).then_inc(s_att, 16)
                    act.dma_start(A[:, 1, :, :], a["att_dst"].partition_broadcast(P)).then_inc(s_att, 16)
                    act.dma_start(wq[:, :, :], a["mix_w_qkv"].rearrange("(k p) n -> p k n", p=P)).then_inc(s_wq, 16)
                    act.dma_start(wn1[:, :], a["mix_w_norm1"][:, :]).then_inc(s_wq, 16)
                    act.dma_start(gw[:, :], a["gate_weights"].partition_broadcast(P)).then_inc(s_wq, 16)
                    act.wait_ge(s_wq, 48)
                    for k in range(KD):
                        act.activation(wq[:, k, :], wq[:, k, :], ACT.Copy, scale=wn1[:, k:k + 1]).then_inc(a_wq, 1)
                    act.wait_ge(v_stat, NT + 1)
                    act.activation(rs[:, :], var[:, :], ACT.Sqrt, bias=eps[:, 0:1]).then_inc(a_rs, 1)
                    act.wait_ge(v_stat, NT + 2)
                    act.activation(rr[:, :], rr[:, :], ACT.Sqrt, bias=eps[:, 1:2]).then_inc(a_rs, 1)

                    def copies(t, c, r):
                        wait(act, normed, t)
                        act.sem_inc(s_gate, 1)
                        act.activation(tile(xna, t, 0, D), xs[:, c, :], ACT.Copy).then_inc(copied.sem, 1)
                        wait(act, xT_ps, t)
                        wait(act, qkv_ps, t - 2)
                        act.activation(xT[:, c, :, :], pT[c][:, 0:D].rearrange("p (k f) -> p k f", k=KD), ACT.Copy).then_inc(xT_sb.sem, 1)

                    def exps(t, c, r):
                        wait(act, qkv_ps, t)
                        wait(act, qk_sb, t - 2)
                        act.sem_inc(s_gate, 1)
                        act.activation(ez[:, c, :], pQ[c][:, :], ACT.Exp, scale=col(rr, t)).then_inc(elu_e.sem, 1)

                    def vs(t, c, r):
                        wait(act, kv_done, t - 2)
                        act.sem_inc(s_gate, 1)
                        for g in range(KD):
                            act.activation(vv[:, c, g, 0:P], pV[c][:, g * P:(g + 1) * P], ACT.Copy, scale=col(rr, t)).then_inc(v_sb.sem, 1)

                    act.wait_ge(v_gw, 1)
                    act.activation(gw[:, :], gw[:, :], ACT.Exp, bias=gmx[:, 0:1], accum_out=gmx[:, 1:2]).then_inc(a_gw, 1)
                    act.wait_ge(v_stat, NT + 3)
                    pipeline(act, NT, [(0, copies), (1, exps), (1, vs)])

                @block.tensor
                def _(pe):
                    consts.wait(pe)
                    pe.wait_ge(end_ready, 1)
                    pe.matmul(pE[:, 0:C1], ones[0:1, :], ends[:, 1, :], start=True, stop=True).then_inc(ends_ps, 1)
                    pe.matmul(pW[:, 0:C1], ones[0:1, :], ends[:, 0, :], start=True, stop=True).then_inc(ends_ps, 1)
                    pe.wait_ge(steps_in, 1)
                    for j in range(2):
                        mm = pe.matmul(pE[:, 448:448 + NT], same_win, by_tile[:, j, :], start=(j == 0), stop=(j == 1))
                    mm.then_inc(steps_ps, 1)
                    pe.wait_ge(v_W, 2)
                    pe.wait_ge(a_wq, KD)

                    def xTs(t, c, r):
                        wait(pe, normed, t)
                        wait(pe, xT_sb, t - 2)
                        for k in range(KD):
                            mm = pe.transpose(pT[c][:, k * P:(k + 1) * P], xs[:, c, k * P:(k + 1) * P], ident)
                        mm.then_inc(xT_ps.sem, 1)

                    def qkv(t, c, r):
                        wait(pe, xT_sb, t)
                        wait(pe, elu_e, t - 2)
                        wait(pe, v_sb, t - 2)
                        wait(pe, qk_sb, t - 2)
                        wait(pe, a_sb, t - 2)
                        for k in range(KD):
                            pe.matmul(pQ[c][:, :], xT[:, c, k, :], wq[:, k, 0:2 * D], start=(k == 0), stop=(k == KD - 1))
                        for k in range(KD):
                            pe.matmul(pV[c][:, 0:D], xT[:, c, k, :], wq[:, k, 2 * D:3 * D], start=(k == 0), stop=(k == KD - 1))
                        for k in range(KD):
                            mm = pe.matmul(pV[c][:, D:D + 2 * H], xT[:, c, k, :], V[:, k, :], start=(k == 0), stop=(k == KD - 1))
                        mm.then_inc(qkv_ps.sem, 1)

                    def kv(t, c, r):
                        wait(pe, qk_sb, t)
                        wait(pe, v_sb, t)
                        first, last = isinstance(t, int) and t == 0, isinstance(t, int) and t == NT - 1
                        m = LAST if last else P
                        for g in range(KD):
                            mm = pe.matmul(pK[:, g, :], qk[0:m, c, D + g * P:D + (g + 1) * P], vv[0:m, c, g, :],
                                           start=first and g == 0, stop=last, skip_group_check=True)
                        mm.then_inc(kv_done.sem, 1)
                        wait(pe, qT_sb, t - 1)
                        for k in range(KD):
                            mm = pe.transpose(pq[:, k * P:(k + 1) * P], qk[:, c, k * P:(k + 1) * P], ident)
                        mm.then_inc(qT_ps.sem, 1)

                    pipeline(pe, NT, [(3, kv), (0, xTs), (1, qkv)])
                    for j in range(SJ):
                        pe.wait_ge(tabs, j + 1)
                        for i in range(3):
                            mm = pe.transpose(pj[j][:, i * P:(i + 1) * P], tab[:, j, i, :], ident)
                        mm.then_inc(tabs_ps, 1)

                @block.vector
                def _(dve):
                    line = v_chain.on(dve)
                    dve.memset(eps[:, 0:1], LN_EPS)
                    dve.memset(eps[:, 1:2], RMS_EPS)
                    dve.memset(eps[:, 2:3], 0.0)
                    line.do(dve.memset(vv[:, :, :, P:P + 1], 1.0))
                    consts.wait(dve)
                    line.do(dve.tensor_scalar(end_i[:, :], end_i[:, :], 4, None, ALU.arith_shift_right))
                    line.do(dve.tensor_copy(ends[:, 0, :], end_i[:, :]))
                    dve.tensor_tensor(ends[:, 1, :], ends[:, 0, :], ends[:, 2, :], ALU.add).then_inc(end_ready, 1)
                    line.do(dve.tensor_scalar(cs[:, 5, :], step_no, -1.0, None, ALU.add))
                    dve.wait_ge(ends_ps, 2)
                    for j in range(SJ):
                        line.do(dve.tensor_scalar(junk[:, :], pE[:, 0:C1], step_no[:, j:j + 1], None, ALU.is_lt, ALU.add, accum_out=cs[:, 0, j:j + 1]))
                        line.do(dve.tensor_scalar(junk[:, :], pE[:, 0:C1], cs[:, 5, j:j + 1], None, ALU.is_lt, ALU.add, accum_out=cs[:, 1, j:j + 1]))
                    line.do(dve.tensor_copy(rowc[:, 0, :], cs[:, 0, :]))
                    line.do(dve.tensor_tensor(cs[:, 2, :], step_no, cs[:, 0, :], ALU.subtract))
                    line.do(dve.tensor_scalar(cs[:, 3, :], cs[:, 2, :], float(DW), None, ALU.mult))
                    line.do(dve.tensor_scalar(rowc[:, 1, :], cs[:, 2, :], float(WINDOWS - 1), None, ALU.min))
                    dve.sem_inc(rows_ready, 1)
                    line.do(dve.tensor_tensor(cs[:, 4, :], cs[:, 0, :], cs[:, 1, :], ALU.subtract))
                    line.do(dve.tensor_scalar(cs[:, 4, :], cs[:, 4, :], -1.0, BIG, ALU.add, ALU.mult))
                    for j in range(2):
                        line.do(dve.tensor_scalar(junk[:, :], pW[:, 0:C1], step_no[:, j:j + 1], None, ALU.is_le, ALU.add, accum_out=cnt[:, j:j + 1]))
                    line.do(dve.tensor_tensor(cnt[:, :], cnt[:, :], step_no[:, 0:2], ALU.add))
                    line.do(dve.tensor_scalar(cnt[:, :], cnt[:, :], float(STEPS - 1), None, ALU.min))
                    line.do(dve.tensor_copy(last_step[:, :], cnt[:, :]))
                    for j in range(2):
                        line.do(dve.tensor_scalar(by_tile[:, j, :], tile_win[:, j, :], cnt[:, j:j + 1], None, ALU.mult))
                    dve.sem_inc(steps_in, 1)
                    dve.wait_ge(steps_ps, 1)
                    line.do(dve.tensor_scalar(last_row[:, :], pE[:, 448:448 + NT], float(DW), dst_no, ALU.mult, ALU.add))
                    dve.wait_ge(s_W, 32)
                    dve.wait_ge(s_att, 32)
                    for i in range(2):
                        line.do(dve.tensor_tensor(tmpW[:, 0, :, :], W[:, 0, :, :], A[:, i, :, :], ALU.mult))
                        line.do(dve.tensor_reduce(V[:, 0, i * H:(i + 1) * H], tmpW[:, 0, :, :], AX.X, ALU.add))
                    for j in range(5):
                        dve.wait_ge(s_x[j], 16)
                        for t in range(5 * j, 5 * j + 5):
                            dve.bn_stats(tile(st6, t, 0, 6), tile(xna, t, 0, D)).then_inc(v_stat, 1)
                    dve.wait_ge(v_stat, NT)
                    line.do(dve.tensor_tensor(mean[:, :], st6[:, :, 1], st6[:, :, 4], ALU.subtract))
                    line.do(dve.tensor_scalar(mean[:, :], mean[:, :], 0.5, None, ALU.mult))
                    line.do(dve.tensor_tensor(mean[:, :], mean[:, :], mean[:, :], ALU.mult))
                    line.do(dve.tensor_tensor(var[:, :], st6[:, :, 2], st6[:, :, 5], ALU.add))
                    line.do(dve.scalar_tensor_tensor(out=var[:, :], in0=var[:, :], scalar=1.0 / D, in1=mean[:, :], op0=ALU.mult, op1=ALU.add))
                    line.do(dve.tensor_tensor(mean[:, :], st6[:, :, 1], st6[:, :, 4], ALU.add))
                    line.do(dve.tensor_scalar(mean[:, :], mean[:, :], 0.5, None, ALU.mult))
                    dve.sem_inc(v_stat, 1)
                    dve.wait_ge(a_rs, 1)
                    line.do(dve.reciprocal(rs[:, :], rs[:, :]))
                    line.do(dve.tensor_tensor(rr[:, :], rs[:, :], rs[:, :], ALU.mult))
                    dve.tensor_tensor(rr[:, :], rr[:, :], var[:, :], ALU.mult).then_inc(v_stat, 1)
                    dve.wait_ge(a_rs, 2)
                    dve.reciprocal(rr[:, :], rr[:, :]).then_inc(v_stat, 1)
                    dve.wait_ge(v_stat, NT + 3)
                    dve.wait_ge(s_wq, 48)
                    line.do(dve.tensor_reduce(gmx[:, 0:1], gw[:, :], AX.X, ALU.max))
                    dve.tensor_scalar(gmx[:, 0:1], gmx[:, 0:1], -1.0, None, ALU.mult).then_inc(v_gw, 1)
                    for i in range(2):
                        dve.wait_ge(v_prod, i + 1)
                        dve.tensor_reduce(V[:, 1, i * H:(i + 1) * H], tmpW[:, 1 + i, :, :], AX.X, ALU.add).then_inc(v_W, 1)

                    def norm(t, c, r):
                        wait(dve, xT_ps, t - 2)
                        wait(dve, copied, t - 2)
                        dve.tensor_scalar(xs[:, c, :], tile(xna, t, 0, D), col(mean, t), col(rs, t), ALU.subtract, ALU.mult).then_inc(normed.sem, 1)

                    def elu(t, c, r):
                        wait(dve, elu_e, t)
                        dve.tensor_scalar(mz[:, c, :], pQ[c][:, :], col(rr, t), 0.0, ALU.mult, ALU.max).then_inc(qk_sb.sem, 1)
                        wait(dve, qk_sb, t, 1)
                        wait(dve, kv_done, t - 2)
                        wait(dve, qT_ps, t - 2)
                        dve.scalar_tensor_tensor(out=qk[:, c, :], in0=ez[:, c, :], scalar=1.0, in1=mz[:, c, :], op0=ALU.min, op1=ALU.add).then_inc(qk_sb.sem, 1)
                        wait(dve, v_sb, t)
                        dve.tensor_scalar(tile(xna, t, AS, AS + H), pV[c][:, D:D + H], 0.0, None, ALU.add).then_inc(a_sb.sem, 1)
                        dve.tensor_scalar(tile(ad, t, 0, H), pV[c][:, D + H:D + 2 * H], 0.0, None, ALU.add).then_inc(a_sb.sem, 1)

                    def qTs(t, c, r):
                        wait(dve, qT_ps, t)
                        for k in range(KD):
                            ins = dve.tensor_scalar(qT[:, k, t * P:(t + 1) * P] if isinstance(t, int) else qT[:, k, ds(t * P, P)],
                                                    pq[:, k * P:(k + 1) * P], 0.0, None, ALU.add)
                        ins.then_inc(qT_sb.sem, 1)

                    pipeline(dve, NT, [(0, norm), (2, elu), (3, qTs)])
                    dve.wait_ge(a_gw, 1)
                    line.do(dve.reciprocal(gmx[:, 1:2], gmx[:, 1:2]))
                    line.do(dve.tensor_scalar(gw[:, :], gw[:, :], gmx[:, 1:2], None, ALU.mult))
                    dve.wait_ge(s_gsd, 16 * SJ)
                    for j in range(SJ):
                        dve.tensor_copy(tab[:, j, 0, :], gsd[:, j, 0, :])
                        dve.tensor_scalar(tab[:, j, 1, :], gsd[:, j, 1, :], cs[:, 3, j:j + 1], None, ALU.subtract)
                        dve.tensor_scalar(tab[:, j, 2, :], ones, cs[:, 4, j:j + 1], None, ALU.mult).then_inc(tabs, 1)
                    wait(dve, kv_done, NT - 1)
                    line.do(dve.memset(kvd[:, :, :], 0.0))
                    for g in range(KD):
                        for b in range(P // HD):
                            s = slice(b * HD, (b + 1) * HD)
                            dve.tensor_copy(kvd[s, g, b * HD:(b + 1) * HD], pK[s, g, b * HD:(b + 1) * HD])
                            dve.tensor_copy(kvd[s, g, P + b:P + b + 1], pK[s, g, P:P + 1])
                    for j in range(SJ):
                        dve.wait_ge(tabs_ps, j + 1)
                        s = slice(j * P, (j + 1) * P)
                        dve.tensor_copy(srcT[:, s], pj[j][:, 0:P])
                        dve.tensor_copy(dlocT[:, s], pj[j][:, P:2 * P])
                        dve.tensor_copy(resetT[:, s], pj[j][:, 2 * P:3 * P])


        md_rows = dram("md_rows", (SP_ * DW, 2 * H))
        ad_step = dram("ad_step", (SP_, P))
        with ExitStack() as ctx:
            gad = sb("gad", [P, SJ, P], ctx=ctx)
            adsd = sb("adsd", [P, SP_ // G, H], ctx=ctx)
            s_gad = sem("s_gad")
            moves.expect(2)
            U, V2 = 6, 2
            idx = sb("idx", [P, U, G], U32, ctx)
            rows = sb("rows", [P, U, G, RW], ctx=ctx)
            eq = sb("eq", [P, V2, G, DW], ctx=ctx)
            pen = sb("pen", [P, V2, G, DW], ctx=ctx)
            adb = sb("adb", [P, V2, G, H], ctx=ctx)
            eqT = sb("eqT", [P, V2, P], ctx=ctx)
            zs = sb("zs", [P, V2, 2, G, H], ctx=ctx)
            zm = sb("zm", [P, V2, G, DW, H], ctx=ctx)
            mst = sb("mst", [P, V2, 3, G], ctx=ctx)
            rsc = sb("rsc", [P, V2, G], ctx=ctx)
            pexp = sb("pexp", [P, V2, G, P], ctx=ctx)
            pw = sb("pw", [P, V2, G, P], ctx=ctx)
            acc = sb("acc", [P, V2, G, D + 2], ctx=ctx)
            mall = sb("mall", [P, SP_ + 8], ctx=ctx)
            dall = sb("dall", [P, SP_], ctx=ctx)
            mdT = sb("mdT", [P, SJ, DW, 2, H], ctx=ctx)
            pA = ps(ctx, "pA", (P, 1024))
            pP = ps(ctx, "pP", (P, 1024))
            pO = [ps(ctx, f"pO{i}") for i in range(3)]
            pM = ps(ctx, "pM")
            bg = sb("bg", [P, H, D], ctx=ctx)
            gam = sb("gam", [P, 2, KD], ctx=ctx)
            betaR = sb("betaR", [P, KD, P], ctx=ctx)
            v_cw, cw_ps = sem("v_cw"), sem("cw_ps")
            consts.expect(5)
            s_rows = [sem(f"s_rows{c}") for c in range(U)]
            s_agg = [sem(f"s_agg{c}") for c in range(V2)]
            idx_in, masks, eqT_ps, eqT_sb = Count(sem("idx_in")), Count(sem("masks"), 3), Count(sem("eqT_ps")), Count(sem("eqT_sb"))
            adE_ps, scored, zT_ps, maxed = Count(sem("adE_ps")), Count(sem("scored"), 3), Count(sem("zT_ps")), Count(sem("maxed"), 5)
            exped, pT_ps, pw_in, prod, acced = Count(sem("exped"), 2), Count(sem("pT_ps")), Count(sem("pw_in")), Count(sem("prod"), G), Count(sem("acced"), G + 1)
            md_ps, md_sb = Count(sem("md_ps")), Count(sem("md_sb"))

            def md_bank(i):
                return (pA, pP)[i][:, 0:SJ * P]

            def half(g, c, r):
                return r * (U // V2) + c // V2

            with nc.Block() as block:
                @block.gpsimd
                def _(pool):
                    for j in range(SJ):
                        pool.indirect_dma_start(gad[:, j, :], None, ad_rows.rearrange("(w d) h -> w (d h)", d=DW), at_row(rowc[:, 1, j:j + 1])).then_inc(s_gad, 16)

                    def gather(g, c, r):
                        wait(pool, prod, g - U)
                        wait(pool, idx_in, g)
                        pool.sem_inc(s_gate, 1)
                        for s in range(G):
                            pool.indirect_dma_start(rows[:, c, s, :], None, node_rows[:, :], at_row(idx[:, c, s:s + 1])).then_inc(s_rows[c], 16)
                    pipeline(pool, GROUPS, [(0, gather)], U, U)

                @block.vector
                def _(dve):
                    dve.memset(acc[:, V2 - 1, G - 1, :], 0.0)
                    dve.memset(dall[:, :], 0.0)
                    v_chain.on(dve).do(dve.memset(mall[:, :], 0.0))

                    def small_weights():
                        line = v_chain.on(dve)
                        consts.wait(dve)
                        for k in range(KD):
                            ins = dve.tensor_scalar(betaR[:, k, :], ones, gam[:, 1, k:k + 1], None, ALU.mult)
                        ins.then_inc(v_cw, 1)
                        line.do(dve.tensor_scalar(gwb[:, :], bg[:, 0, :], gw[:, 0:1], None, ALU.mult))
                        for h in range(1, H):
                            line.do(dve.scalar_tensor_tensor(out=gwb[:, :], in0=bg[:, h, :], scalar=gw[:, h:h + 1], in1=gwb[:, :], op0=ALU.mult, op1=ALU.add))
                        dve.wait_ge(cw_ps, 1)
                        dve.tensor_tensor(bob[:, :], bob[:, :], pM[:, D:2 * D], ALU.add).then_inc(v_cw, 1)
                        for k in range(KD):
                            dve.tensor_scalar(WoT[:, k, :], WoT[:, k, :], gam[:, 0, k:k + 1], None, ALU.mult)

                    m_at = lambda g, one: mall[:, one + g * G:one + g * G + G] if isinstance(g, int) else mall[:, ds(g * G + one, G)]

                    def sources(g, c, r):
                        dve.tensor_scalar(idx[:, c, :], col(srcT, g, G), 0.0, None, ALU.add).then_inc(idx_in.sem, 1)

                    def mask_eq(g, c, r):
                        wait(dve, eqT_ps, g - V2)
                        wait(dve, masks, g - V2)
                        dve.tensor_tensor(eq[:, c % V2, :, :], col(dlocT, g, G).unsqueeze(2).to_broadcast([P, G, DW]),
                                          iota16.unsqueeze(1).to_broadcast([P, G, DW]), ALU.is_equal).then_inc(masks.sem, 1)

                    def mask_ad(g, c, r):
                        if isinstance(g, int) and g == 0:
                            moves.wait(dve)
                        wait(dve, adE_ps, g - V2)
                        dve.tensor_tensor(adb[:, c % V2, :, :], same_step, tile(adsd, g, 0, H).unsqueeze(1).to_broadcast([P, G, H]),
                                          ALU.mult).then_inc(masks.sem, 1)

                    def mask_pen(g, c, r):
                        wait(dve, masks, g, 1)
                        wait(dve, scored, g - V2)
                        dve.tensor_scalar(pen[:, c % V2, :, :], eq[:, c % V2, :, :], -1.0, BIG, ALU.add, ALU.mult).then_inc(masks.sem, 1)

                    def score_sum(g, c, r):
                        dve.wait_ge(s_rows[c], (r + 1) * (16 * G))
                        wait(dve, adE_ps, g)
                        dve.tensor_tensor(zs[:, c % V2, 0, :, :], rows[:, c, :, AS:AS + H], pM[:, P:P + G * H].rearrange("p (s h) -> p s h", h=H),
                                          ALU.add).then_inc(scored.sem, 1)

                    def score_relu(g, c, r):
                        wait(dve, scored, g, 1)
                        dve.scalar_tensor_tensor(out=zs[:, c % V2, 1, :, :], in0=zs[:, c % V2, 0, :, :], scalar=0.2, in1=zs[:, c % V2, 0, :, :],
                                                 op0=ALU.mult, op1=ALU.max).then_inc(scored.sem, 1)

                    def score_mask(g, c, r):
                        wait(dve, scored, g, 2)
                        wait(dve, masks, g)
                        wait(dve, zT_ps, g - V2)
                        dve.tensor_tensor(zm[:, c % V2, :, :, :], zs[:, c % V2, 1, :, :].unsqueeze(2).to_broadcast([P, G, DW, H]),
                                          pen[:, c % V2, :, :].unsqueeze(3).to_broadcast([P, G, DW, H]), ALU.add).then_inc(scored.sem, 1)

                    def max_step(g, c, r):
                        wait(dve, zT_ps, g)
                        wait(dve, maxed, g - 1)
                        wait(dve, exped, g - V2)
                        dve.tensor_reduce(mst[:, c % V2, 0, :], pA[:, :].rearrange("p (s e) -> p s e", s=G), AX.X, ALU.max).then_inc(maxed.sem, 1)

                    def max_scan(g, c, r):
                        wait(dve, maxed, g, 1)
                        dve.tensor_tensor_scan(m_at(g, 1), col(resetT, g, G), mst[:, c % V2, 0, :], mall[:, g * G:g * G + 1] if isinstance(g, int) else mall[:, ds(g * G, 1)],
                                               ALU.add, ALU.max).then_inc(maxed.sem, 1)

                    def max_neg(g, c, r):
                        wait(dve, maxed, g, 2)
                        dve.tensor_scalar(mst[:, c % V2, 1, :], m_at(g, 1), -1.0, None, ALU.mult).then_inc(maxed.sem, 1)

                    def max_old(g, c, r):
                        dve.tensor_tensor(mst[:, c % V2, 2, :], col(mall, g, G), col(resetT, g, G), ALU.add).then_inc(maxed.sem, 1)

                    def max_change(g, c, r):
                        wait(dve, maxed, g, 4)
                        dve.tensor_tensor(mst[:, c % V2, 2, :], mst[:, c % V2, 2, :], mst[:, c % V2, 1, :], ALU.add).then_inc(maxed.sem, 1)

                    def accumulate(s):
                        def stage(g, c, r):
                            if s == 0:
                                wait(dve, exped, g)
                                if not isinstance(g, int) or g >= V2:
                                    dve.wait_ge(s_agg[c % V2], half(g, c, r) * 16)
                            wait(dve, prod, g, s + 1)
                            before = acc[:, c % V2, s - 1, 0:D + 1] if s else acc[:, (c - 1) % V2, G - 1, 0:D + 1]
                            if s or not (isinstance(g, int) and g == 0):
                                wait(dve, acced, g if s else g - 1, s if s else None)
                            dve.scalar_tensor_tensor(out=acc[:, c % V2, s, 0:D + 1], in0=before, scalar=rsc[:, c % V2, s:s + 1],
                                                     in1=pO[(c * G + s) % 3][:, 0:D + 1], op0=ALU.mult, op1=ALU.add).then_inc(acced.sem, 1)
                        return stage

                    def keep_den(g, c, r):
                        wait(dve, acced, g, G)
                        dve.tensor_scalar(col(dall, g, G), acc[:, c % V2, :, D], 0.0, None, ALU.add).then_inc(acced.sem, 1)

                    add = [(4, accumulate(s)) for s in range(G)]
                    pipeline(dve, GROUPS, [(0, sources), (2, score_sum), (1, mask_eq), (2, score_relu), (1, mask_ad), (2, score_mask), (3, max_step),
                                           add[0], (3, max_scan), add[1], (3, max_neg), add[2], (3, max_old), add[3], (3, max_change),
                                           add[4], (1, mask_pen), add[5], add[6], add[7], (4, keep_den)], U, U, small_weights)
                    for i in range(2):
                        wait(dve, md_ps, i)
                        dve.tensor_copy(mdT[:, :, :, i, :], md_bank(i).rearrange("p (j d h) -> p j d h", d=DW, h=H)).then_inc(md_sb.sem, 1)

                @block.scalar
                def _(act):
                    def copy_eq(g, c, r):
                        wait(act, eqT_ps, g)
                        wait(act, adE_ps, g - V2)
                        act.activation(eqT[:, c % V2, :], pM[:, 0:P], ACT.Copy).then_inc(eqT_sb.sem, 1)

                    def exps(g, c, r):
                        wait(act, maxed, g)
                        wait(act, pT_ps, g - V2)
                        wait(act, acced, g - V2)
                        for s in range(G):
                            ins = act.activation(pexp[:, c % V2, s, :], pA[:, s * P:(s + 1) * P], ACT.Exp, bias=mst[:, c % V2, 1, s:s + 1])
                        ins.then_inc(exped.sem, 1)
                        act.activation(rsc[:, c % V2, :], mst[:, c % V2, 2, :], ACT.Exp).then_inc(exped.sem, 1)

                    def copy_p(g, c, r):
                        wait(act, pT_ps, g)
                        wait(act, prod, g - V2)
                        act.activation(pw[:, c % V2, :, :], pP[:, :].rearrange("p (s e) -> p s e", s=G), ACT.Copy).then_inc(pw_in.sem, 1)

                    pipeline(act, GROUPS, [(4, copy_p), (1, copy_eq), (3, exps)], U, U)

                @block.tensor
                def _(pe):
                    def beta_out():
                        pe.wait_ge(v_cw, 1)
                        for k in range(KD):
                            mm = pe.matmul(pM[:, D:2 * D], betaR[:, k, :], WoT[:, k, :], start=(k == 0), stop=(k == KD - 1))
                        mm.then_inc(cw_ps, 1)
                        pe.wait_ge(v_cw, 2)

                    def eq_turn(g, c, r):
                        wait(pe, masks, g, 1)
                        wait(pe, scored, g - 1, 1)
                        pe.transpose(pM[:, 0:P], eq[:, c % V2, :, :].rearrange("p s d -> p (s d)"), ident).then_inc(eqT_ps.sem, 1)

                    def ad_edges(g, c, r):
                        wait(pe, eqT_sb, g)
                        wait(pe, masks, g, 2)
                        pe.matmul(pM[:, P:P + G * H], eqT[:, c % V2, :], adb[:, c % V2, :, :].rearrange("p s h -> p (s h)"), start=True, stop=True).then_inc(adE_ps.sem, 1)

                    def z_turn(g, c, r):
                        wait(pe, scored, g)
                        wait(pe, exped, g - 1, 1)
                        for s in range(G):
                            mm = pe.transpose(pA[:, s * P:(s + 1) * P], zm[:, c % V2, s, :, :].rearrange("p d h -> p (d h)"), ident)
                        mm.then_inc(zT_ps.sem, 1)

                    def p_turn(g, c, r):
                        wait(pe, exped, g, 1)
                        wait(pe, pw_in, g - 1)
                        for s in range(G):
                            mm = pe.transpose(pP[:, s * P:(s + 1) * P], pexp[:, c % V2, s, :], ident)
                        mm.then_inc(pT_ps.sem, 1)

                    def product(lo, hi):
                        def stage(g, c, r):
                            if lo == 0:
                                wait(pe, pw_in, g)
                            for s in range(lo, hi):
                                if s >= 3:
                                    wait(pe, acced, g, s - 2)
                                elif not isinstance(g, int) or g > 0:
                                    wait(pe, acced, g - 1, G - 2 + s)
                                pe.matmul(pO[(c * G + s) % 3][:, 0:D + 1], pw[:, c % V2, s, :], rows[:, c, s, 0:D + 1], start=True, stop=True).then_inc(prod.sem, 1)
                        return stage

                    pipeline(pe, GROUPS, [(4, p_turn), (3, z_turn), (1, eq_turn), (4, product(0, 4)), (1, ad_edges), (4, product(4, G))], U, U, beta_out)
                    wait(pe, acced, GROUPS - 1)
                    for i in range(2):
                        for j in range(SJ):
                            mm = pe.transpose(md_bank(i)[:, j * P:(j + 1) * P], (mall[:, 1 + j * P:1 + (j + 1) * P], dall[:, j * P:(j + 1) * P])[i], ident)
                        mm.then_inc(md_ps.sem, 1)

                @block.sync
                def _(sp):
                    sp.wait_ge(s_gad, 16 * SJ)
                    sp.dma_start(ad_step.rearrange("(j p) n -> p j n", p=P), gad[:, :, :]).then_inc(moves.sem, 16)
                    moves.wait(sp, 1)
                    sp.dma_start(adsd[:, :, :], ad_step.rearrange("(g s) (d h) -> (s d) g h", s=G, h=H)).then_inc(moves.sem, 16)

                    def store(g, c, r):
                        wait(sp, acced, g)
                        o8 = agg_rows[g * G:(g + 1) * G, :, :] if isinstance(g, int) else agg_rows[ds(g * G, G), :, :]
                        sp.dma_start(o8.rearrange("s p f -> p s f"), acc[:, c % V2, :, 0:D]).then_inc(s_agg[c % V2], 16)
                    sp.dma_start(WoT[:, :, :], a["WoT"].rearrange("(k p) n -> p k n", p=P)).then_inc(consts.sem, 16)
                    sp.dma_start(gam[:, 0, :], a["ln_gamma"][:, :]).then_inc(consts.sem, 16)
                    sp.dma_start(gam[:, 1, :], a["ln_beta"][:, :]).then_inc(consts.sem, 16)
                    sp.dma_start(bob[:, :], a["bo"].partition_broadcast(P)).then_inc(consts.sem, 16)
                    sp.dma_start(bg[:, :, :], a["bias_gat"].partition_broadcast(P)).then_inc(consts.sem, 16)
                    pipeline(sp, GROUPS, [(0, store)], U, U)
                    for c in range(V2):
                        sp.wait_ge(s_agg[c], 16 * len(range(c, GROUPS, V2)))
                    wait(sp, md_sb, 1)
                    moves.expect(1)
                    sp.dma_start(md_rows.rearrange("(j p d) m -> p j (d m)", p=P, d=DW), mdT[:, :, :, :, :].rearrange("p j d i h -> p j (d i h)")).then_inc(moves.sem, 16)
                    moves.wait(sp)
        edge_ctx.close()

        x2 = sb("x2", [P, NT, D], ctx=node_ctx)
        al = sb("al", [P, 2, NT, H], ctx=node_ctx)
        with ExitStack() as ctx:
            U = 4
            qs = sb("qs", [P, U, KD, P], ctx=ctx)
            xt = sb("xt", [P, U, D], ctx=ctx)
            wo = sb("wo", [P, KD, D], ctx=ctx)
            bo_, wn2 = sb("mix_bo", [P, D], ctx=ctx), sb("wn2", [P, D], ctx=ctx)
            rz = sb("rz", [P, 2, 2 * QH], ctx=ctx)
            on = sb("on", [P, 2, D], ctx=ctx)
            onT = sb("onT", [P, 2, KD, P], ctx=ctx)
            nb = sb("nb", [P, 2, D], ctx=ctx)
            hh = sb("hh", [P, 2, D], ctx=ctx)
            sq = sb("sq", [P, D], ctx=ctx)
            hw = sb("hw", [P, 2, D], ctx=ctx)
            ms = sb("ms", [P, 2, 2], ctx=ctx)
            mdw = sb("mdw", [P, 2, DW * 2 * H], ctx=ctx)
            mdg = sb("mdg", [P, NT, 2, H], ctx=ctx)
            es = sb("es", [P, 4, NT, H], ctx=ctx)
            md_win = dram("md_win", (2 * P * DW, 2 * H))
            pN = [ps(ctx, f"pN{c}") for c in range(2)]
            pT = [ps(ctx, f"pnT{c}") for c in range(2)]
            pH = [ps(ctx, f"pH{c}") for c in range(2)]
            consts.expect(3)
            s_q, s_xt = [sem(f"s_q{c}") for c in range(U)], [sem(f"s_xt{c}") for c in range(U)]
            num_ps, on_sb, onT_ps, onT_sb, h_ps = Count(sem("num_ps")), Count(sem("on_sb"), 3), Count(sem("onT_ps")), Count(sem("onT_sb")), Count(sem("h_ps"))
            h_sb, rms, hw_in, mixed = Count(sem("h_sb")), Count(sem("rms"), 2), Count(sem("hw_in")), Count(sem("mixed"), 3)
            nb_in, xt_in = Count(sem("nb_in")), Count(sem("xt_in"))
            s_mdw, al_in, al_ex = sem("s_mdw"), sem("al_in"), sem("al_ex")
            with nc.Block() as block:
                @block.sync
                def _(sp):
                    sp.dma_start(wo[:, :, :], a["mix_w_out"].rearrange("(k p) n -> p k n", p=P)).then_inc(consts.sem, 16)
                    sp.dma_start(bo_[:, :], a["mix_b_out"].partition_broadcast(P)).then_inc(consts.sem, 16)
                    sp.dma_start(wn2[:, :], a["mix_w_norm2"].partition_broadcast(P)).then_inc(consts.sem, 16)

                    def load_q(t, c, r):
                        wait(sp, num_ps, t - U)
                        sp.dma_start(qs[:, c, :, :], qT[:, :, t * P:(t + 1) * P] if isinstance(t, int) else qT[:, :, ds(t * P, P)]).then_inc(s_q[c], 16)

                    def load_x(t, c, r):
                        wait(sp, mixed, t - U)
                        sp.dma_start(xt[:, c, :], row(a["x"], t)).then_inc(s_xt[c], 16)

                    def by_node():
                        sp.wait_ge(s_mdw, 32)
                        sp.dma_start(md_win.rearrange("(j p d) m -> p j (d m)", p=P, d=DW), mdw[:, :, :]).then_inc(moves.sem, 16)
                        moves.expect(1)
                        moves.wait(sp)
                        sp.dma_start(mdg[:, :, :, :], md_win[0:NP, :].rearrange("(t p) (i h) -> p t i h", p=P, h=H)).then_inc(moves.sem, 16)
                        moves.expect(1)
                    pipeline(sp, NT, [(0, load_q), (2, load_x)], U, U, by_node)

                @block.gpsimd
                def _(pool):
                    for j in range(2):
                        pool.indirect_dma_start(mdw[:, j, :], None, md_rows.rearrange("(s d) m -> s (d m)", d=DW), at_row(last_step[:, j:j + 1])).then_inc(s_mdw, 16)
                    consts.wait(pool)

                    def biased(t, c, r):
                        wait(pool, h_sb, t - 2)
                        pool.tensor_tensor(nb[:, c % 2, :], tile(xna, t, 0, D), bo_[:, :], ALU.add).then_inc(nb_in.sem, 1)

                    def with_bias(t, c, r):
                        pool.wait_ge(s_xt[c], (r + 1) * 16)
                        pool.tensor_tensor(xt[:, c, :], xt[:, c, :], bob[:, :], ALU.add).then_inc(xt_in.sem, 1)

                    def scaled(t, c, r):
                        wait(pool, h_sb, t)
                        wait(pool, mixed, t - 2)
                        pool.tensor_tensor(hw[:, c % 2, :], hh[:, c % 2, :], wn2[:, :], ALU.mult).then_inc(hw_in.sem, 1)
                    pipeline(pool, NT, [(1, biased), (2, scaled), (2, with_bias)], U, U)

                @block.tensor
                def _(pe):
                    consts.wait(pe)

                    def num(t, c, r):
                        pe.wait_ge(s_q[c], (r + 1) * 16)
                        wait(pe, on_sb, t - 2)
                        for g in range(KD):
                            mm = pe.matmul(pN[c % 2][:, g * (P + 4):(g + 1) * (P + 4)], qs[:, c, g, :], kvd[:, g, :], start=True, stop=True)
                        mm.then_inc(num_ps.sem, 1)

                    def turn(t, c, r):
                        wait(pe, on_sb, t)
                        wait(pe, onT_sb, t - 2)
                        for k in range(KD):
                            mm = pe.transpose(pT[c % 2][:, k * P:(k + 1) * P], on[:, c % 2, k * P:(k + 1) * P], ident)
                        mm.then_inc(onT_ps.sem, 1)

                    def out_proj(t, c, r):
                        wait(pe, onT_sb, t)
                        wait(pe, h_sb, t - 2)
                        for k in range(KD):
                            mm = pe.matmul(pH[c % 2][:, 0:D], onT[:, c % 2, k, :], wo[:, k, :], start=(k == 0), stop=(k == KD - 1))
                        mm.then_inc(h_ps.sem, 1)
                    pipeline(pe, NT, [(0, num), (2, out_proj), (1, turn)], U, U)

                @block.scalar
                def _(act):
                    def copy_t(t, c, r):
                        wait(act, onT_ps, t)
                        wait(act, h_ps, t - 2)
                        act.activation(onT[:, c % 2, :, :], pT[c % 2][:, 0:D].rearrange("p (k f) -> p k f", k=KD), ACT.Copy).then_inc(onT_sb.sem, 1)

                    def rms_of(t, c, r):
                        wait(act, h_sb, t)
                        wait(act, mixed, t - 2)
                        wait(act, rms, t - 1)
                        act.activation(sq[:, :], hh[:, c % 2, :], ACT.Square, accum_out=ms[:, c % 2, 0:1]).then_inc(rms.sem, 1)
                        wait(act, rms, t, 1)
                        act.activation(ms[:, c % 2, 1:2], ms[:, c % 2, 0:1], ACT.Sqrt, scale=1.0 / D, bias=eps[:, 1:2]).then_inc(rms.sem, 1)

                    def weigh_loops():
                        act.wait_ge(al_in, 1)
                        act.activation(es[:, 2:4, :, :], es[:, 2:4, :, :], ACT.Exp).then_inc(al_ex, 1)
                    pipeline(act, NT, [(2, rms_of), (1, copy_t)], U, U + 1, weigh_loops)

                @block.vector
                def _(dve):
                    z_of = lambda c: pN[c % 2][:, 0:KD * (P + 4)].rearrange("p (g n) -> p g n", g=KD)

                    def z_sum(t, c, r):
                        wait(dve, num_ps, t)
                        wait(dve, onT_ps, t - 2)
                        dve.tensor_scalar(rz[:, c % 2, 0:QH].rearrange("p (g b) -> p g b", g=KD), z_of(c)[:, :, P:P + 4], ATT_EPS, None, ALU.add).then_inc(on_sb.sem, 1)

                    def z_inverse(t, c, r):
                        wait(dve, on_sb, t, 1)
                        dve.reciprocal(rz[:, c % 2, QH:2 * QH], rz[:, c % 2, 0:QH]).then_inc(on_sb.sem, 1)

                    def divide(t, c, r):
                        wait(dve, on_sb, t, 2)
                        for g in range(KD):
                            ins = dve.tensor_tensor(on[:, c % 2, g * P:(g + 1) * P].rearrange("p (b m) -> p b m", m=HD), z_of(c)[:, g, 0:P].rearrange("p (b m) -> p b m", m=HD),
                                                    rz[:, c % 2, QH + g * 4:QH + g * 4 + 4].unsqueeze(2).to_broadcast([P, 4, HD]), ALU.mult)
                        ins.then_inc(on_sb.sem, 1)

                    def residual(t, c, r):
                        wait(dve, h_ps, t)
                        wait(dve, nb_in, t)
                        wait(dve, hw_in, t - 2)
                        wait(dve, rms, t - 2)
                        dve.tensor_tensor(hh[:, c % 2, :], pH[c % 2][:, 0:D], nb[:, c % 2, :], ALU.add).then_inc(h_sb.sem, 1)

                    def rms_inverse(t, c, r):
                        wait(dve, rms, t)
                        dve.reciprocal(ms[:, c % 2, 1:2], ms[:, c % 2, 1:2]).then_inc(mixed.sem, 1)

                    def normed_sum(t, c, r):
                        wait(dve, mixed, t, 1)
                        wait(dve, hw_in, t)
                        dve.scalar_tensor_tensor(out=hw[:, c % 2, :], in0=hw[:, c % 2, :], scalar=ms[:, c % 2, 1:2], in1=hh[:, c % 2, :], op0=ALU.mult, op1=ALU.add).then_inc(mixed.sem, 1)

                    def with_x(t, c, r):
                        wait(dve, mixed, t, 2)
                        wait(dve, xt_in, t)
                        dve.tensor_tensor(tile(x2, t, 0, D), hw[:, c % 2, :], xt[:, c, :], ALU.add).then_inc(mixed.sem, 1)

                    def loops():
                        line = v_chain.on(dve)
                        moves.wait(dve)
                        line.do(dve.tensor_tensor(es[:, 0, :, :], xna[:, :, AS:AS + H], ad[:, :, :], ALU.add))
                        line.do(dve.scalar_tensor_tensor(out=es[:, 0, :, :], in0=es[:, 0, :, :], scalar=0.2, in1=es[:, 0, :, :], op0=ALU.mult, op1=ALU.max))
                        line.do(dve.tensor_tensor(es[:, 1, :, :], es[:, 0, :, :], mdg[:, :, 0, :], ALU.max))
                        dve.tensor_tensor(es[:, 2, :, :], mdg[:, :, 0, :], es[:, 1, :, :], ALU.subtract)
                        dve.tensor_tensor(es[:, 3, :, :], es[:, 0, :, :], es[:, 1, :, :], ALU.subtract).then_inc(al_in, 1)
                        dve.wait_ge(al_ex, 1)
                        line.do(dve.tensor_tensor(es[:, 0, :, :], es[:, 2, :, :], mdg[:, :, 1, :], ALU.mult))
                        line.do(dve.tensor_tensor(es[:, 0, :, :], es[:, 0, :, :], es[:, 3, :, :], ALU.add))
                        line.do(dve.reciprocal(es[:, 1, :, :], es[:, 0, :, :]))
                        line.do(dve.tensor_tensor(es[:, 1, :, :], es[:, 1, :, :], gw[:, :].unsqueeze(1).to_broadcast([P, NT, H]), ALU.mult))
                        for i in range(2):
                            line.do(dve.tensor_tensor(al[:, i, :, :], es[:, 1, :, :], es[:, 2 + i, :, :], ALU.mult))
                    pipeline(dve, NT, [(0, z_sum), (4, rms_inverse), (0, z_inverse), (4, normed_sum), (0, divide), (4, with_x), (2, residual)], U, U, loops)

        with ExitStack() as ctx:
            lr = sb("lr", [P, 2], U32, ctx)
            AG = sb("AG", [P, 2, H, D], ctx=ctx)
            own = sb("own", [P, 2, H, D], ctx=ctx)
            aT = sb("aT", [P, 2, H * KD, P], ctx=ctx)
            betb = sb("betb", [P, D], ctx=ctx)
            gtw = sb("gtw", [P, KD, E], ctx=ctx)
            gtb = sb("gtb", [P, E], ctx=ctx)
            xg = sb("xg", [P, 2, D], ctx=ctx)
            xo = sb("xo", [P, 2, D], ctx=ctx)
            lgt = sb("lgt", [P, 2, 2, E], ctx=ctx)
            tk = sb("tk", [P, 2, 2, E], ctx=ctx)
            last = sb("last_equal", [P, 2, 2], ctx=ctx)
            both = sb("both", [P, 2, E], ctx=ctx)
            pick = sb("pick", [P, 2, REC], ctx=ctx)
            prod2 = sb("prod2", [P, 2, 2, E], ctx=ctx)
            slot_x = sb("slot_x", [P, 2, 2], U32, ctx)
            ysc = sb("ysc", [P, 2, D], ctx=ctx)
            res = sb("res", [P, 2, D], ctx=ctx)
            st = sb("st", [P, 2, 2, 8], ctx=ctx)
            nT = sb("nT", [P, 2, KD, P], ctx=ctx)
            yt = sb("yt", [P, 2, D], ctx=ctx)
            yT = sb("yT", [P, 2, KD, P], ctx=ctx)
            pA = [ps(ctx, f"pa{i}") for i in range(4)]
            pW, pG, pX, pY = ps(ctx, "pW_"), ps(ctx, "pG_"), ps(ctx, "pX_"), ps(ctx, "pY_")
            consts.expect(3)
            s_AG, s_xo = [sem(f"s_AG{c}") for c in range(2)], [sem(f"s_xo{c}") for c in range(2)]
            lr_in, own_in, agg_in, aT_ps = Count(sem("lr_in")), Count(sem("own_in")), Count(sem("agg_in")), Count(sem("aT_ps"), 4)
            aT_a, aT_v, w_ps = Count(sem("aT_a"), 2), Count(sem("aT_v"), 2), Count(sem("w_ps"))
            nT_ps, nT_sb, g_ps, yT_ps, yT_sb = (Count(sem(n)) for n in ("nT_ps", "nT_sb", "g_ps", "yT_ps", "yT_sb"))
            s_scat = [sem(f"s_scat{c}") for c in range(2)]
            picked, rank_ps, placed, pick_kept, y_moved = Count(sem("picked"), 10), Count(sem("rank_ps")), Count(sem("placed"), 5), Count(sem("pick_kept")), Count(sem("y_moved"))
            lg_ps, lg_in, xg_in, xo_in, y_kept = (Count(sem(n)) for n in ("lg_ps", "lg_in", "xg_in", "xo_in", "y_kept"))

            def norm_counts(name):
                return [Count(sem(name + "_sum")), Count(sem(name + "_mom"), 2), Count(sem(name + "_std")), Count(sem(name + "_inv")), Count(sem(name + "_out"))]
            r_sum, r_mom, r_std, r_inv, r_out = r_norm = norm_counts("res")
            y_sum, y_mom, y_std, y_inv, y_out = y_norm = norm_counts("y")
            with nc.Block() as block:
                @block.sync
                def _(sp):
                    sp.dma_start(betb[:, :], a["ffn_beta"].partition_broadcast(P)).then_inc(consts.sem, 16)
                    sp.dma_start(gtw[:, :, :], a["ffn_gate_w"].rearrange("(k p) n -> p k n", p=P)).then_inc(consts.sem, 16)
                    sp.dma_start(gtb[:, :], a["ffn_gate_b"].partition_broadcast(P)).then_inc(consts.sem, 16)

                    def store(t, c, r):
                        wait(sp, xo_in, t)
                        sp.dma_start(row(x2_rows, t), xo[:, c, :]).then_inc(s_xo[c], 16)
                    pipeline(sp, NT, [(0, store)])
                    for c in range(2):
                        sp.wait_ge(s_xo[c], 16 * len(range(c, NT, 2)))

                @block.gpsimd
                def _(pool):
                    def gather(t, c, r):
                        wait(pool, agg_in, t - 2)
                        pool.sem_inc(s_gate, 1)
                        pool.tensor_copy(lr[:, c:c + 1], col(last_row, t)).then_inc(lr_in.sem, 1)
                        wait(pool, lr_in, t)
                        pool.sem_inc(s_gate, 1)
                        pool.indirect_dma_start(AG[:, c, :, :].rearrange("p h f -> p (h f)"), None,
                                                agg_rows.rearrange("s (d h) f -> (s d) (h f)", h=H), at_row(lr[:, c:c + 1])).then_inc(s_AG[c], 16)

                    def with_bias(t, c, r):
                        wait(pool, r_sum, t - 2)
                        pool.tensor_tensor(xg[:, c, :], tile(xna, t, 0, D), gwb[:, :], ALU.add).then_inc(xg_in.sem, 1)

                    def with_beta(t, c, r):
                        if isinstance(t, int) and t == 0:
                            consts.wait(pool)
                        wait(pool, y_sum, t)
                        if not isinstance(r, int) or r > 0:
                            pool.wait_ge(s_xo[c], r * 16)
                        pool.tensor_tensor(xo[:, c, :], tile(x2, t, 0, D), betb[:, :], ALU.add).then_inc(xo_in.sem, 1)
                    def move_y(t, c, r):
                        wait(pool, y_kept, t)
                        if not isinstance(r, int) or r > 0:
                            pool.wait_ge(s_scat[c], r * 32)
                        pool.sem_inc(s_gate, 1)
                        pool.tensor_copy(ysc[:, c, :], tile(y_all, t, 0, D)).then_inc(y_moved.sem, 1)

                    def scatter(t, c, r):
                        wait(pool, placed, t)
                        wait(pool, y_moved, t)
                        pool.sem_inc(s_gate, 1)
                        for k in range(2):
                            pool.indirect_dma_start(xs_rows[:, :], at_row(slot_x[:, c, k:k + 1]), ysc[:, c, :], None).then_inc(s_scat[c], 16)
                    pipeline(pool, NT, [(0, gather), (3, with_bias), (6, with_beta), (7, move_y), (8, scatter)])
                    for c in range(2):
                        pool.wait_ge(s_scat[c], 32 * len(range(c, NT, 2)))

                @block.scalar
                def _(act):
                    def own_rows(t, c, r):
                        wait(act, agg_in, t - 2)
                        wait(act, aT_ps, t - 2)
                        act.sem_inc(s_gate, 1)
                        for h in range(H):
                            ins = act.activation(own[:, c, h, :], tile(xna, t, 0, D), ACT.Copy, scale=al[:, 1, t, h:h + 1] if isinstance(t, int) else al[:, 1, ds(t, 1), h:h + 1].rearrange("p t h -> p (t h)"))
                        ins.then_inc(own_in.sem, 1)

                    def copy_a(t, c, r):
                        for i in range(2):
                            wait(act, aT_ps, t, 2 * i + 1)
                            wait(act, w_ps, t - 2)
                            act.activation(aT[:, c, 8 * i:8 * i + 4, :], pA[2 * i][:, :].rearrange("p (k f) -> p k f", k=4), ACT.Copy).then_inc(aT_a.sem, 1)

                    def root(i, counts):
                        def stage(t, c, r):
                            wait(act, counts[1], t)
                            act.activation(st[:, c, i, 7:8], st[:, c, i, 7:8], ACT.Sqrt, bias=eps[:, 0:1]).then_inc(counts[2].sem, 1)
                        return stage

                    def copy_n(t, c, r):
                        wait(act, nT_ps, t)
                        wait(act, g_ps, t - 2)
                        act.activation(nT[:, c, :, :], pX[:, 0:D].rearrange("p (k f) -> p k f", k=KD), ACT.Copy).then_inc(nT_sb.sem, 1)

                    def copy_y(t, c, r):
                        wait(act, yT_ps, t)
                        wait(act, lg_ps, t - 2)
                        act.activation(yT[:, c, :, :], pY[:, 0:D].rearrange("p (k f) -> p k f", k=KD), ACT.Copy).then_inc(yT_sb.sem, 1)

                    def keep_y(t, c, r):
                        wait(act, y_out, t)
                        act.sem_inc(s_gate, 1)
                        act.activation(tile(y_all, t, 0, D), yt[:, c, :], ACT.Copy).then_inc(y_kept.sem, 1)
                    def keep_pick(t, c, r):
                        wait(act, placed, t)
                        act.sem_inc(s_gate, 1)
                        act.activation(tile(picks, t, 0, REC), pick[:, c, :], ACT.Copy).then_inc(pick_kept.sem, 1)
                    pipeline(act, NT, [(9, keep_pick), (4, root(0, r_norm)), (5, root(1, y_norm)), (2, copy_a), (4, copy_n), (5, keep_y), (5, copy_y), (0, own_rows)])

                @block.tensor
                def _(pe):
                    consts.wait(pe)

                    def turn_a(t, c, r):
                        wait(pe, agg_in, t)
                        for i in range(4):
                            wait(pe, (aT_a, aT_v)[i % 2], t - 1, i // 2 + 1)
                            for k in range(4):
                                n = 4 * i + k
                                mm = pe.transpose(pA[i][:, k * P:(k + 1) * P], own[:, c, n // KD, (n % KD) * P:(n % KD + 1) * P], ident)
                            mm.then_inc(aT_ps.sem, 1)

                    def weigh(lo, hi):
                        def stage(t, c, r):
                            if lo == 0:
                                wait(pe, r_sum, t - 1)
                            for i in range(lo, hi):
                                wait(pe, (aT_a, aT_v)[i % 2], t, i // 2 + 1)
                                for k in range(4):
                                    n = 4 * i + k
                                    mm = pe.matmul(pW[:, 0:D], aT[:, c, n, :], W[:, n % KD, n // KD, :], start=(n == 0), stop=(n == H * KD - 1))
                            if hi == 4:
                                mm.then_inc(w_ps.sem, 1)
                        return stage

                    def turn_n(t, c, r):
                        wait(pe, r_out, t)
                        wait(pe, nT_sb, t - 1)
                        for k in range(KD):
                            mm = pe.transpose(pX[:, k * P:(k + 1) * P], res[:, c, k * P:(k + 1) * P], ident)
                        mm.then_inc(nT_ps.sem, 1)

                    def project(t, c, r):
                        wait(pe, nT_sb, t)
                        wait(pe, y_sum, t - 1)
                        for k in range(KD):
                            mm = pe.matmul(pG[:, 0:D], nT[:, c, k, :], WoT[:, k, :], start=(k == 0), stop=(k == KD - 1))
                        mm.then_inc(g_ps.sem, 1)

                    def turn_y(t, c, r):
                        wait(pe, y_out, t)
                        wait(pe, lg_in, t - 1)
                        wait(pe, placed, t - 3, 2)
                        for k in range(KD):
                            mm = pe.transpose(pY[:, k * P:(k + 1) * P], yt[:, c, k * P:(k + 1) * P], ident)
                        mm.then_inc(yT_ps.sem, 1)

                    def rank(t, c, r):
                        wait(pe, picked, t)
                        wait(pe, lg_in, t + 1 if isinstance(t, int) and t == NT - 2 else t)
                        wait(pe, placed, t - 1, 2)
                        pe.matmul(pY[:, D + E:D + 2 * E], tri, both[:, c, :], start=True, stop=True)
                        pe.matmul(pY[:, D + 2 * E:D + 3 * E], ones, both[:, c, :], start=True, stop=True).then_inc(rank_ps.sem, 1)

                    def gate(t, c, r):
                        wait(pe, yT_sb, t)
                        for k in range(KD):
                            mm = pe.matmul(pY[:, D:D + E], yT[:, c, k, :], gtw[:, k, :], start=(k == 0), stop=(k == KD - 1))
                        mm.then_inc(lg_ps.sem, 1)
                    pipeline(pe, NT, [(6, gate), (8, rank), (2, turn_a), (3, weigh(0, 2)), (4, turn_n), (5, turn_y), (3, weigh(2, 4)), (4, project)])

                @block.vector
                def _(dve):
                    def neighbours(lo, hi):
                        def stage(t, c, r):
                            if lo == 0:
                                dve.wait_ge(s_AG[c], (r + 1) * 16)
                                wait(dve, own_in, t)
                            for h in range(lo, hi):
                                ins = dve.scalar_tensor_tensor(out=own[:, c, h, :], in0=AG[:, c, h, :], scalar=al[:, 0, t, h:h + 1] if isinstance(t, int) else al[:, 0, ds(t, 1), h:h + 1].rearrange("p t h -> p (t h)"),
                                                               in1=own[:, c, h, :], op0=ALU.mult, op1=ALU.add)
                            if hi == H:
                                ins.then_inc(agg_in.sem, 1)
                        return stage

                    def copy_a(t, c, r):
                        for i in range(2):
                            wait(dve, aT_ps, t, 2 * i + 2)
                            wait(dve, w_ps, t - 2)
                            dve.tensor_copy(aT[:, c, 8 * i + 4:8 * i + 8, :], pA[2 * i + 1][:, :].rearrange("p (k f) -> p k f", k=4)).then_inc(aT_v.sem, 1)

                    def residual(t, c, r):
                        wait(dve, w_ps, t)
                        wait(dve, xg_in, t)
                        wait(dve, nT_ps, t - 2)
                        dve.tensor_tensor(res[:, c, :], pW[:, 0:D], xg[:, c, :], ALU.add).then_inc(r_sum.sem, 1)

                    def node_out(t, c, r):
                        wait(dve, g_ps, t)
                        dve.tensor_tensor(tile(x2, t, 0, D), pG[:, 0:D], tile(x2, t, 0, D), ALU.add).then_inc(y_sum.sem, 1)

                    source = lambda i, t, c: tile(x2, t, 0, D) if i else res[:, c, :]

                    def stats(i, counts):
                        def stage(t, c, r):
                            wait(dve, counts[0], t)
                            dve.sem_inc(s_gate, 1)
                            dve.bn_stats(st[:, c, i, 0:6], source(i, t, c)).then_inc(counts[1].sem, 1)
                        return stage

                    def moments(i, counts):
                        def stage(t, c, r):
                            wait(dve, counts[1], t, 1)
                            dve.sem_inc(s_gate, 1)
                            dve.bn_aggr(st[:, c, i, 6:8], st[:, c, i, 0:6]).then_inc(counts[1].sem, 1)
                        return stage

                    def inverse(i, counts):
                        def stage(t, c, r):
                            wait(dve, counts[2], t)
                            dve.reciprocal(st[:, c, i, 7:8], st[:, c, i, 7:8]).then_inc(counts[3].sem, 1)
                        return stage

                    def normalise(i, counts):
                        def stage(t, c, r):
                            wait(dve, counts[3], t)
                            if i:
                                wait(dve, yT_ps, t - 2)
                                wait(dve, y_kept, t - 2)
                            dve.tensor_scalar(yt[:, c, :] if i else res[:, c, :], source(i, t, c), st[:, c, i, 6:7], st[:, c, i, 7:8],
                                              ALU.subtract, ALU.mult).then_inc(counts[4].sem, 1)
                        return stage

                    def logits(t, c, r):
                        wait(dve, lg_ps, t)
                        wait(dve, rank_ps, t - 2)
                        dve.tensor_tensor(lgt[:, c, 0, :], pY[:, D:D + E], gtb[:, :], ALU.add).then_inc(lg_in.sem, 1)

                    def top(i):
                        def stage(t, c, r):
                            one_hot = lambda k: pick[:, c, k * E:(k + 1) * E]
                            value = lambda k: pick[:, c, 2 * E + 2 + k:2 * E + 3 + k]
                            k, step = divmod(i, 5)
                            if i == 0:
                                wait(dve, lg_in, t)
                                wait(dve, pick_kept, t - 2)
                            wait(dve, picked, t, i)
                            if step == 0:
                                ins = dve.tensor_reduce(value(k), lgt[:, c, k, :], AX.X, ALU.max)
                            elif step == 1:
                                ins = dve.scalar_tensor_tensor(out=tk[:, c, 0, :], in0=lgt[:, c, k, :], scalar=value(k), in1=from_end, op0=ALU.is_equal, op1=ALU.mult)
                            elif step == 2:
                                ins = dve.tensor_reduce(last[:, c, k:k + 1], tk[:, c, 0, :], AX.X, ALU.max)
                            elif step == 3:
                                ins = dve.tensor_scalar(one_hot(k), from_end, last[:, c, k:k + 1], None, ALU.is_equal)
                            elif k == 0:
                                ins = dve.scalar_tensor_tensor(out=lgt[:, c, 1, :], in0=one_hot(0), scalar=-3e38, in1=lgt[:, c, 0, :], op0=ALU.mult, op1=ALU.add)
                            else:
                                wait(dve, rank_ps, t - 1)
                                ins = dve.tensor_tensor(both[:, c, :], one_hot(0), one_hot(1), ALU.add)
                            ins.then_inc(picked.sem, 1)
                        return stage

                    def place(i):
                        def stage(t, c, r):
                            wait(dve, placed, t, i)
                            if i == 0:
                                wait(dve, rank_ps, t)
                                wait(dve, placed, t - 1)
                                ins = dve.tensor_tensor(tk[:, c, 1, :], pY[:, D + E:D + 2 * E], used[:, :], ALU.add)
                            elif i == 1:
                                ins = dve.tensor_tensor(used[:, :], pY[:, D + 2 * E:D + 3 * E], used[:, :], ALU.add)
                            elif i == 2:
                                ins = dve.tensor_tensor(prod2[:, c, :, :], tk[:, c, 1, :].unsqueeze(1).to_broadcast([P, 2, E]),
                                                        pick[:, c, 0:2 * E].rearrange("p (k e) -> p k e", k=2), ALU.mult)
                            elif i == 3:
                                ins = dve.tensor_reduce(pick[:, c, 2 * E:2 * E + 2], prod2[:, c, :, :], AX.X, ALU.add)
                            else:
                                if not isinstance(r, int) or r > 0:
                                    dve.wait_ge(s_scat[c], r * 32)
                                ins = dve.tensor_scalar(slot_x[:, c, :], pick[:, c, 2 * E:2 * E + 2], 0.0, None, ALU.add)
                            ins.then_inc(placed.sem, 1)
                        return stage
                    v_chain.on(dve).do(dve.tensor_copy(used[:, :], part_row))
                    T, L = [(7, top(i)) for i in range(10)], [(8, place(i)) for i in range(5)]
                    pipeline(dve, NT, [(4, residual), (5, node_out), (4, stats(0, r_norm)), (6, logits), L[0], (5, stats(1, y_norm)), L[1], T[0],
                                       (4, moments(0, r_norm)), L[2], (5, moments(1, y_norm)), T[1], (1, neighbours(0, 1)), T[2], (1, neighbours(1, 2)), L[3],
                                       (4, inverse(0, r_norm)), T[3], (5, inverse(1, y_norm)), (1, neighbours(2, 3)), (4, normalise(0, r_norm)), T[4],
                                       (5, normalise(1, y_norm)), L[4], (2, copy_a), T[5], (1, neighbours(3, 4)), T[6], (1, neighbours(4, 5)), T[7],
                                       (1, neighbours(5, 6)), T[8], (1, neighbours(6, 7)), T[9], (1, neighbours(7, H))])

        node_ctx.close()
        slot = sb("slot", [P, 2, NT], U32)
        wts = sb("wts", [P, 2, NT])
        expert_of = sb("expert_of", [1, TILES], I32)
        row_of = sb("row_of", [1, TILES], I32)
        experts_ctx = ExitStack()
        w1 = sb("w1", [P, E, KD, F], ctx=experts_ctx)
        w2 = sb("w2", [P, E, FK, D], ctx=experts_ctx)
        b1 = sb("b1", [P, E, FK], ctx=experts_ctx)
        b2 = sb("b2", [P, E, D], ctx=experts_ctx)
        m = sb("m", [P, 2, NT], ctx=experts_ctx)
        T = sb("T", [P, NT, 2, E], ctx=experts_ctx)
        sy = sb("sy", [P, NT, 2], ctx=experts_ctx)
        te = sb("te", [P, 3, E], ctx=experts_ctx)
        WS = 2
        s_w = [sem(f"s_w{i}") for i in range(WS)]

        def load_weights(eng, e):
            eng.dma_start(w1[:, e, :, :], a["ffn_w1"][e, :, :].rearrange("(k p) f -> p k f", p=P)).then_inc(s_w[e % WS], 16)
            eng.dma_start(w2[:, e, :, :], a["ffn_w2"][e, :, :].rearrange("(k p) f -> p k f", p=P)).then_inc(s_w[e % WS], 16)
        with ExitStack() as ctx:
            ti = sb("ti", [P, E], I32, ctx)
            tj = sb("tj", [1, 2, TILES, E], ctx=ctx)
            tv = sb("tv", [1, 4, TILES], ctx=ctx)
            jn = sb("jn", [1, TILES], ctx=ctx)
            free_row = sb("free_row", [1, E], I32, ctx)
            zero = sb("zero", [P, D], ctx=ctx)
            a_rt, m_in, free_in, zero_in = sem("a_rt"), sem("m_in"), sem("free_in"), sem("zero_in")
            consts.expect(2)
            b2_in = sem("b2_in")
            moves.expect(E)

            def clear(eng, half):
                eng.wait_ge(zero_in, 1)
                eng.wait_ge(free_in, 1)
                for e in range(half, E, 2):
                    first = eng.value_load(free_row[0:1, e:e + 1], min_val=0, max_val=E * PART - P)
                    eng.dma_start(xs_rows[ds(first, P), :], zero[:, :]).then_inc(moves.sem, 16)

            with nc.Block() as block:
                @block.sync
                def _(sp):
                    sp.dma_start(jn[:, :], a["tile_no"][:, :]).then_inc(consts.sem, 16)
                    sp.dma_start(b1[:, :, :], a["ffn_b1"][:, :, :]).then_inc(consts.sem, 16)
                    load_weights(sp, 0)
                    clear(sp, 0)
                    sp.dma_start(b2[:, :, :], a["ffn_b2"].partition_broadcast(P)).then_inc(b2_in, 16)
                    moves.wait(sp)

                @block.scalar
                def _(act):
                    clear(act, 1)

                @block.vector
                def _(dve):
                    line = v_chain.on(dve)
                    line.do(dve.tensor_copy(free_row[:, :], used[0:1, :]))
                    dve.sem_inc(free_in, 1)
                    line.do(dve.tensor_tensor(te[:, 0, :], used[:, :], part_row, ALU.subtract))
                    line.do(dve.tensor_scalar(ti[:, :], te[:, 0, :], float(P - 1), None, ALU.add))
                    line.do(dve.tensor_scalar(ti[:, :], ti[:, :], 7, None, ALU.arith_shift_right))
                    line.do(dve.tensor_copy(te[:, 0, :], ti[:, :]))
                    line.do(dve.tensor_tensor_scan(te[:, 1, :], ones[:, 0:E], te[:, 0, :], 0.0, ALU.mult, ALU.add))
                    line.do(dve.tensor_tensor(te[:, 2, :], te[:, 1, :], te[:, 0, :], ALU.subtract))
                    line.do(dve.tensor_scalar(te[:, 2, :], te[:, 2, :], float(P), None, ALU.mult))
                    line.do(dve.tensor_tensor(te[:, 2, :], te[:, 2, :], part_row, ALU.subtract))
                    consts.wait(dve)
                    line.do(dve.tensor_tensor(tj[:, 0, :, :], te[0:1, 1, :].unsqueeze(1).to_broadcast([1, TILES, E]), jn[:, :].unsqueeze(2).to_broadcast([1, TILES, E]), ALU.is_le))
                    line.do(dve.tensor_tensor(tj[:, 1, :, :], tj[:, 0, :, :], te[0:1, 0, :].unsqueeze(1).to_broadcast([1, TILES, E]), ALU.mult))
                    line.do(dve.tensor_reduce(tv[:, 0:2, :], tj[:, :, :, :], AX.X, ALU.add))
                    line.do(dve.tensor_scalar(expert_of[:, :], tv[:, 0, :], float(E - 1), None, ALU.min))
                    line.do(dve.tensor_tensor(tv[:, 1, :], jn[:, :], tv[:, 1, :], ALU.subtract))
                    line.do(dve.tensor_scalar(tv[:, 2, :], tv[:, 0, :], float(E), float(P), ALU.is_lt, ALU.mult))
                    line.do(dve.tensor_tensor(tv[:, 1, :], tv[:, 1, :], tv[:, 2, :], ALU.mult))
                    line.do(dve.tensor_scalar(tv[:, 3, :], tv[:, 0, :], float(E - 1), float(PART), ALU.min, ALU.mult))
                    line.do(dve.tensor_tensor(row_of[:, :], tv[:, 1, :], tv[:, 3, :], ALU.add))

                @block.gpsimd
                def _(pool):
                    pool.memset(zero[:, :], 0.0).then_inc(zero_in, 1)

        with ExitStack() as ctx:
            U = 6
            S3 = 3
            xe = sb("xe", [P, S3, D], ctx=ctx)
            xeT = sb("xeT", [P, 2, KD, P], ctx=ctx)
            w1e = sb("w1e", [P, S3, KD, F], ctx=ctx)
            hT = sb("hT", [P, 2, FK, P], ctx=ctx)
            ye = sb("ye", [P, 2, D], ctx=ctx)
            pX = [ps(ctx, f"pXe{c}") for c in range(2)]
            pH = [ps(ctx, f"pHe{c}") for c in range(2)]
            pY = [ps(ctx, f"pYe{c}") for c in range(2)]
            s_xe = [sem(f"s_xe{c}") for c in range(S3)]
            s_ye = [sem(f"s_ye{c}") for c in range(2)]
            w_ready = sem("w_ready")
            xeT_ps, xeT_sb = xT_ps.again(NT), xT_sb.again(NT)
            w1_in, he_ps = Count(sem("w1_in")), Count(sem("he_ps"))
            he_sb, ye_ps, ye_sb = (Count(sem(n)) for n in ("he_sb", "ye_ps", "ye_sb"))

            def nth(c, r, slots):
                return r * (U // slots) + c // slots

            def expert(eng, j):
                return eng.value_load(expert_of[0:1, j:j + 1] if isinstance(j, int) else expert_of[0:1, ds(j, 1)], min_val=0, max_val=E - 1)

            def of_expert(T, e, k):
                return T[:, ds(e, 1), k, :].rearrange("p e n -> p (e n)")

            with nc.Block() as block:
                @block.sync
                def _(sp):
                    for c in range(S3):
                        sp.wait_ge(s_xe[c], 16)
                    for e in range(E):
                        if e + 1 < E:
                            load_weights(sp, e + 1)
                        sp.wait_ge(s_w[e % WS], 32 * (e // WS + 1))
                        sp.sem_inc(w_ready, 1)

                @block.scalar
                def _(act):
                    act.wait_ge(m_in, 1)
                    act.activation(m[:, 0, :], m[:, 0, :], ACT.Exp).then_inc(a_rt, 1)

                    def load(j, c, r):
                        wait(act, xeT_ps, j - S3)
                        first = act.value_load(row_of[0:1, j:j + 1] if isinstance(j, int) else row_of[0:1, ds(j, 1)], min_val=0, max_val=E * PART - P)
                        act.dma_start(xe[:, c % S3, :], xs_rows[ds(first, P), :]).then_inc(s_xe[c % S3], 16)

                    def relu(j, c, r):
                        e = expert(act, j)
                        wait(act, he_ps, j)
                        wait(act, ye_ps, j - 2)
                        act.sem_inc(s_gate, 1)
                        for f in range(FK):
                            ins = act.activation(hT[:, c % 2, f, :], pH[c % 2][:, f * P:(f + 1) * P], ACT.Relu,
                                                 bias=b1[:, ds(e, 1), f:f + 1].rearrange("p e f -> p (e f)"))
                        ins.then_inc(he_sb.sem, 1)
                    pipeline(act, TILES, [(0, load), (2, relu)], U, S3)

                @block.tensor
                def _(pe):
                    def turn(j, c, r):
                        pe.wait_ge(s_xe[c % S3], (nth(c, r, S3) + 1) * 16)
                        wait(pe, xeT_sb, j - 2)
                        for k in range(KD):
                            mm = pe.transpose(pX[c % 2][:, k * P:(k + 1) * P], xe[:, c % S3, k * P:(k + 1) * P], ident)
                        mm.then_inc(xeT_ps.sem, 1)

                    def hidden(j, c, r):
                        wait(pe, w1_in, j)
                        wait(pe, xeT_sb, j)
                        wait(pe, he_sb, j - 2)
                        for f in range(FK):
                            for k in range(KD):
                                mm = pe.matmul(pH[c % 2][:, f * P:(f + 1) * P], w1e[:, c % S3, k, f * P:(f + 1) * P], xeT[:, c % 2, k, :], start=(k == 0), stop=(k == KD - 1))
                        mm.then_inc(he_ps.sem, 1)

                    def output(j, c, r):
                        e = expert(pe, j)
                        wait(pe, he_sb, j)
                        wait(pe, ye_sb, j - 2)
                        pe.sem_inc(s_gate, 1)
                        for f in range(FK):
                            mm = pe.matmul(pY[c % 2][:, 0:D], hT[:, c % 2, f, :], of_expert(w2, e, f), start=(f == 0), stop=(f == FK - 1))
                        mm.then_inc(ye_ps.sem, 1)
                    pipeline(pe, TILES, [(1, hidden), (0, turn), (2, output)], U, S3)

                @block.vector
                def _(dve):
                    def copy_x(j, c, r):
                        wait(dve, xeT_ps, j)
                        wait(dve, he_ps, j - 2)
                        dve.tensor_copy(xeT[:, c % 2, :, :], pX[c % 2][:, 0:D].rearrange("p (k f) -> p k f", k=KD)).then_inc(xeT_sb.sem, 1)

                    line = v_chain.on(dve)
                    line.do(dve.tensor_tensor(T[:, :, :, :], picks[:, :, 0:2 * E].rearrange("p t (k e) -> p t k e", k=2),
                                              te[:, 2, :].unsqueeze(1).unsqueeze(1).to_broadcast([P, NT, 2, E]), ALU.mult))
                    line.do(dve.tensor_reduce(sy[:, :, :], T[:, :, :, :], AX.X, ALU.add))
                    line.do(dve.tensor_tensor(slot[:, :, :].rearrange("p k t -> p t k"), sy[:, :, :], picks[:, :, 2 * E:2 * E + 2], ALU.add))
                    dve.tensor_tensor(m[:, 0, :], picks[:, :, 2 * E + 3], picks[:, :, 2 * E + 2], ALU.subtract).then_inc(m_in, 1)
                    dve.wait_ge(a_rt, 1)
                    line.do(dve.tensor_scalar(m[:, 1, :], m[:, 0, :], 1.0, None, ALU.add))
                    line.do(dve.reciprocal(wts[:, 0, :], m[:, 1, :]))
                    line.do(dve.tensor_tensor(wts[:, 1, :], wts[:, 0, :], m[:, 0, :], ALU.mult))

                    def take_w1(j, c, r):
                        e = expert(dve, j)
                        dve.wait_ge(w_ready, e + 1)
                        wait(dve, he_ps, j - S3)
                        dve.sem_inc(s_gate, 1)
                        dve.tensor_copy(w1e[:, c % S3, :, :], w1[:, ds(e, 1), :, :].rearrange("p e k f -> p (e k) f")).then_inc(w1_in.sem, 1)

                    def add_b2(j, c, r):
                        if isinstance(j, int) and j == 0:
                            dve.wait_ge(b2_in, 16)
                        e = expert(dve, j)
                        wait(dve, ye_ps, j)
                        if not isinstance(j, int) or j >= 2:
                            dve.wait_ge(s_ye[c % 2], nth(c, r, 2) * 16)
                        dve.sem_inc(s_gate, 1)
                        dve.tensor_tensor(ye[:, c % 2, :], pY[c % 2][:, 0:D], b2[:, ds(e, 1), :].rearrange("p e n -> p (e n)"), ALU.add).then_inc(ye_sb.sem, 1)
                    pipeline(dve, TILES, [(1, copy_x), (0, take_w1), (3, add_b2)], U, S3)

                @block.gpsimd
                def _(pool):
                    def store(j, c, r):
                        wait(pool, ye_sb, j)
                        pool.sem_inc(s_gate, 1)
                        pool.dma_start(row(ys_rows, j), ye[:, c % 2, :]).then_inc(s_ye[c % 2], 16)
                    pipeline(pool, TILES, [(0, store)], U, S3)
                    for c in range(2):
                        pool.wait_ge(s_ye[c], 16 * (TILES // 2))
        experts_ctx.close()

        with ExitStack() as ctx:
            U = 4
            g = sb("g", [P, U, 2, D], ctx=ctx)
            xb = sb("xb", [P, 2, D], ctx=ctx)
            v = sb("v", [P, U, D], ctx=ctx)
            o = sb("o", [P, 2, D], ctx=ctx)
            sf = sb("sf", [P, U, 8], ctx=ctx)
            gb = sb("gb", [P, D], ctx=ctx)
            s_g = [sem(f"s_g{c}") for c in range(U)]
            consts.expect(1)
            s_xb, s_out = [sem(f"s_xb{c}") for c in range(2)], [sem(f"s_out{c}") for c in range(2)]
            v_in, v_mom, v_sd, v_inv = Count(sem("v_in"), 2), y_mom.again(NT), y_std.again(NT), y_inv.again(NT)
            o_in = Count(sem("o_fin"), 2)

            def nth(c, r):
                return r * (U // 2) + c // 2

            with nc.Block() as block:
                @block.gpsimd
                def _(pool):
                    for t in range(NT):
                        wait(pool, v_in, t - U)
                        for k in range(2):
                            pool.indirect_dma_start(g[:, t % U, k, :], None, ys_rows[:, :], at_row(slot[:, k, t:t + 1])).then_inc(s_g[t % U], 16)

                @block.scalar
                def _(act):
                    def std(t, c, r):
                        wait(act, v_mom, t)
                        act.activation(sf[:, c, 7:8], sf[:, c, 7:8], ACT.Sqrt, bias=eps[:, 0:1]).then_inc(v_sd.sem, 1)
                    pipeline(act, NT, [(0, std)], U, U)

                @block.vector
                def _(dve):
                    consts.wait(dve)

                    def add_expert(k):
                        def stage(t, c, r):
                            if k == 0:
                                dve.wait_ge(s_g[c], (r + 1) * 32)
                            else:
                                wait(dve, v_in, t, 1)
                            w = wts[:, k, t:t + 1] if isinstance(t, int) else wts[:, k, ds(t, 1)]
                            dve.scalar_tensor_tensor(out=v[:, c, :], in0=g[:, c, k, :], scalar=w, in1=v[:, c, :] if k else tile(y_all, t, 0, D), op0=ALU.mult, op1=ALU.add).then_inc(v_in.sem, 1)
                        return stage

                    def stats(t, c, r):
                        wait(dve, v_in, t)
                        dve.sem_inc(s_gate, 1)
                        dve.bn_stats(sf[:, c, 0:6], v[:, c, :]).then_inc(v_mom.sem, 1)

                    def moments(t, c, r):
                        wait(dve, v_mom, t, 1)
                        dve.sem_inc(s_gate, 1)
                        dve.bn_aggr(sf[:, c, 6:8], sf[:, c, 0:6]).then_inc(v_mom.sem, 1)

                    def inverse(t, c, r):
                        wait(dve, v_sd, t)
                        dve.reciprocal(sf[:, c, 7:8], sf[:, c, 7:8]).then_inc(v_inv.sem, 1)

                    def scaled(t, c, r):
                        if not isinstance(t, int) or t >= 2:
                            dve.wait_ge(s_out[c % 2], nth(c, r) * 16)
                        wait(dve, v_mom, t)
                        dve.scalar_tensor_tensor(out=o[:, c % 2, :], in0=v[:, c, :], scalar=sf[:, c, 6:7], in1=gb[:, :], op0=ALU.subtract, op1=ALU.mult).then_inc(o_in.sem, 1)

                    def finish(t, c, r):
                        wait(dve, o_in, t, 1)
                        wait(dve, v_inv, t)
                        dve.wait_ge(s_xb[c % 2], (nth(c, r) + 1) * 16)
                        dve.scalar_tensor_tensor(out=o[:, c % 2, :], in0=o[:, c % 2, :], scalar=sf[:, c, 7:8], in1=xb[:, c % 2, :], op0=ALU.mult, op1=ALU.add).then_inc(o_in.sem, 1)
                    pipeline(dve, NT, [(0, add_expert(0)), (1, inverse), (1, scaled), (0, add_expert(1)), (1, finish), (0, stats), (0, moments)], U, U)

                @block.sync
                def _(sp):
                    sp.dma_start(gb[:, :], a["ffn_gamma"].partition_broadcast(P)).then_inc(consts.sem, 16)

                    def load(t, c, r):
                        wait(sp, o_in, t - 2)
                        sp.dma_start(xb[:, c % 2, :], row(x2_rows, t)).then_inc(s_xb[c % 2], 16)

                    def store(t, c, r):
                        wait(sp, o_in, t)
                        sp.dma_start(row(out, t), o[:, c % 2, :]).then_inc(s_out[c % 2], 16)
                    pipeline(sp, NT, [(2, store), (0, load)], U, U)
                    for c in range(2):
                        sp.wait_ge(s_out[c], 16 * len(range(c, NT, 2)))


def constants():
    import numpy as np
    p = np.arange(P)
    same_step = (p[:, None] // DW == np.arange(G)[None, :]).repeat(H, axis=1)
    same_window = p[:, None] % (P // DW) == p[None, :] // DW
    window_in_tile = (np.arange(2)[None, :, None] * P + p[:, None, None]) // (P // DW) == np.arange(NT)[None, None, :]
    window_in_tile = window_in_tile.reshape(P, 2 * NT)
    parts = [np.eye(P), p[:, None] < p[None, :], np.ones((P, P)), same_window, np.tile(np.arange(16), (P, 1)),
             p[:, None] + P * np.arange(SJ)[None, :], window_in_tile, (p % DW)[:, None], same_step,
             np.tile(E - np.arange(E), (P, 1)), np.tile(PART * np.arange(E), (P, 1))]
    return np.concatenate([np.asarray(x, np.float32) for x in parts], axis=1)


def lay_out(inputs):
    import numpy as np
    g = {k: np.asarray(v) for k, v in inputs.items()}
    x = np.zeros((NP, D), g["x"].dtype)
    x[:N] = g["x"]
    src = np.zeros((CHUNKS * P,), g["src"].dtype)
    dst = np.full((CHUNKS * P,), DST_PAD, g["dst"].dtype)
    src[:NE], dst[:NE] = g["src"], g["dst"]
    a = {"x": x, "src_dst": np.concatenate([src.reshape(CHUNKS, P), dst.reshape(CHUNKS, P)], axis=1), "cst": constants(),
         "chunk_end": dst[P - 1::P][:CHUNKS - 1].reshape(1, -1), "chunk_no": np.arange(CHUNKS - 1, dtype=np.float32).reshape(1, -1)}
    for k, v in g.items():
        if k.startswith("L0_"):
            a[k.split("_", 2)[2] if k.split("_")[1] == "gnn" else k[3:]] = v
    for k in ("mix_w_norm1", "ln_gamma", "ln_beta"):
        a[k] = a[k].reshape(KD, P).T
    a["ffn_b1"] = a["ffn_b1"].reshape(E, FK, P).transpose(2, 0, 1)
    a["tile_no"] = np.arange(TILES, dtype=np.float32).reshape(1, -1)
    a["WoT"] = a.pop("Wo").T
    return {k: np.ascontiguousarray(v) for k, v in a.items()}


def kernel(**inputs):
    import concourse.bacc as _bacc
    from concourse.bass_utils import run_bass_kernel_spmd as _run
    nc = _bacc.Bacc("TRN2", target_bir_lowering=False, num_devices=1)
    arrays = lay_out(inputs)
    args = {k: nc.dram_tensor("in_" + k, v.shape, mybir.dt.from_np(v.dtype), kind="ExternalInput").ap()
            for k, v in arrays.items()}
    out = nc.dram_tensor("out", (NP, D), F32, kind="ExternalOutput").ap()
    build(nc, args, out)
    r = _run(nc, [{"in_" + k: v for k, v in arrays.items()}], core_ids=[0])
    return r.results[0]["out"][:N]
```
